# Optimizing a Trainium2 kernel written in Bass

```python
import numpy as np
import jax
import jax.numpy as jnp

def _softmax(x, axis=-1):
    return jax.nn.softmax(x, axis=axis)

def _gelu(x):
    return jax.nn.gelu(x, approximate=True)

def _silu(x):
    return jax.nn.silu(x)

def _sigmoid(x):
    return jax.nn.sigmoid(x)

def _layernorm(x, axis=-1, eps=1e-05):
    m = jnp.mean(x, axis=axis, keepdims=True)
    v = jnp.var(x, axis=axis, keepdims=True)
    return (x - m) / jnp.sqrt(v + eps)

def _scatter_add(tgt, idx, src, axis=0):
    return tgt.at[idx].add(src)

def _segment_sum(src, seg, n):
    return jax.ops.segment_sum(src, seg, n)
kernel_name = 'mk_early_fusion_d1_tok_img256_r4_eae486'

def setup_inputs(seed: int=0):
    np.random.seed(seed)
    _w = jnp.asarray

    def _rec_inputs():
        import jax
        import jax.numpy as jnp
        _rk = jax.random.key(seed)
        x = -0.0003702 + 0.999946 * jax.random.normal(jax.random.fold_in(_rk, 1), (32, 1, 64, 64), jnp.float32)
        txt = 0.281643 + 0.58738 * jax.random.normal(jax.random.fold_in(_rk, 2), (32, 128, 64), jnp.float32)
        return (x, txt)
    x, txt = _rec_inputs()

    def _L0_tok_setup():
        import jax, jax.numpy as jnp
        import numpy as np
        PH, PW = (64, 25)
        SH, SW = (64, 12)

        def _unfold(x, ph, pw, sh, sw):
            B, C, H, W = x.shape
            nh = (H - ph) // sh + 1
            nw = (W - pw) // sw + 1
            rows = jnp.arange(nh)[:, None] * sh + jnp.arange(ph)[None, :]
            cols = jnp.arange(nw)[:, None] * sw + jnp.arange(pw)[None, :]
            p = x[:, :, rows, :]
            p = p[:, :, :, :, cols]
            p = jnp.transpose(p, (0, 2, 4, 1, 3, 5))
            return p.reshape(B, nh * nw, C * ph * pw)
        key = jax.random.key(seed)
        kx, kw = jax.random.split(key, 2)
        x = jax.random.normal(kx, (64, 1, 64, 1000), dtype=jnp.float32)
        in_dim = 1 * PH * PW
        weight = jax.random.normal(kw, (in_dim, 64), dtype=jnp.float32) / np.sqrt(in_dim).astype(np.float32)
        bias = jnp.zeros((64,), dtype=jnp.float32)
        return {'x': x, 'weight': weight, 'bias': bias}
    _L0_tok_all = _L0_tok_setup()
    _L0_tok_in = {k: v for k, v in _L0_tok_all.items() if k in ('weight', 'bias')}
    del _L0_tok_all

    def _L0_attn_setup():
        import jax, jax.numpy as jnp
        import numpy as np
        B, N, D = (8, 512, 64)
        key = jax.random.key(seed)
        k1, k2, k3, k4 = jax.random.split(key, 4)
        s = D ** (-0.5)
        return {'x': jax.random.normal(k1, (B, N, D), dtype=jnp.float32), 'Wq': jax.random.normal(k2, (D, D), dtype=jnp.float32) * s, 'Wk': jax.random.normal(k3, (D, D), dtype=jnp.float32) * s, 'Wv': jax.random.normal(k4, (D, D), dtype=jnp.float32) * s}
    _L0_attn_all = _L0_attn_setup()
    _L0_attn_in = {k: v for k, v in _L0_attn_all.items() if k in ('Wq', 'Wk', 'Wv')}
    del _L0_attn_all

    def _L0_ffn_setup():
        import jax, jax.numpy as jnp
        import numpy as np
        B, S, H, NH, NE = (4, 256, 64, 4, 4)
        D = H // NH
        EPS = 1e-08

        def layernorm(x, g, b):
            m = jnp.mean(x, axis=-1, keepdims=True)
            v = jnp.mean((x - m) ** 2, axis=-1, keepdims=True)
            return (x - m) / jnp.sqrt(v + EPS) * g + b
        key = jax.random.key(seed)
        ks = jax.random.split(key, 18)
        sc = 0.05
        return {'x': jax.random.normal(ks[0], (B, S, H), jnp.float32), 'hl_w': jax.random.normal(ks[1], (NH, D, H), jnp.float32) * sc, 'hl_b': jax.random.normal(ks[2], (NH, D), jnp.float32) * sc, 'wq': jax.random.normal(ks[3], (NH, NE, D, D), jnp.float32) * sc, 'wk': jax.random.normal(ks[4], (NH, D, D), jnp.float32) * sc, 'wv': jax.random.normal(ks[5], (NH, D, D), jnp.float32) * sc, 'gate_w': jax.random.normal(ks[6], (NH, NE, NE * D), jnp.float32) * sc, 'gate_b': jax.random.normal(ks[7], (NH, NE), jnp.float32) * sc, 'ln_g': jnp.ones((D,), jnp.float32), 'ln_b': jnp.zeros((D,), jnp.float32), 'fc1_w': jax.random.normal(ks[8], (D, D), jnp.float32) * sc, 'fc1_b': jax.random.normal(ks[9], (D,), jnp.float32) * sc, 'fc2_w': jax.random.normal(ks[10], (D, D), jnp.float32) * sc, 'fc2_b': jax.random.normal(ks[11], (D,), jnp.float32) * sc, 'fnorm_g': jnp.ones((D,), jnp.float32), 'fnorm_b': jnp.zeros((D,), jnp.float32), 'fgate_w': jax.random.normal(ks[12], (NH, H), jnp.float32) * sc}
    _L0_ffn_all = _L0_ffn_setup()
    _L0_ffn_in = {k: v for k, v in _L0_ffn_all.items() if k in ('hl_w', 'hl_b', 'wq', 'wk', 'wv', 'gate_w', 'gate_b', 'ln_g', 'ln_b', 'fc1_w', 'fc1_b', 'fc2_w', 'fc2_b', 'fnorm_g', 'fnorm_b', 'fgate_w')}
    del _L0_ffn_all
    return {'x': x, 'txt': txt, 'L0_tok_weight': _L0_tok_in['weight'], 'L0_tok_bias': _L0_tok_in['bias'], 'L0_attn_Wq': _L0_attn_in['Wq'], 'L0_attn_Wk': _L0_attn_in['Wk'], 'L0_attn_Wv': _L0_attn_in['Wv'], 'L0_ffn_hl_w': _L0_ffn_in['hl_w'], 'L0_ffn_hl_b': _L0_ffn_in['hl_b'], 'L0_ffn_wq': _L0_ffn_in['wq'], 'L0_ffn_wk': _L0_ffn_in['wk'], 'L0_ffn_wv': _L0_ffn_in['wv'], 'L0_ffn_gate_w': _L0_ffn_in['gate_w'], 'L0_ffn_gate_b': _L0_ffn_in['gate_b'], 'L0_ffn_ln_g': _L0_ffn_in['ln_g'], 'L0_ffn_ln_b': _L0_ffn_in['ln_b'], 'L0_ffn_fc1_w': _L0_ffn_in['fc1_w'], 'L0_ffn_fc1_b': _L0_ffn_in['fc1_b'], 'L0_ffn_fc2_w': _L0_ffn_in['fc2_w'], 'L0_ffn_fc2_b': _L0_ffn_in['fc2_b'], 'L0_ffn_fnorm_g': _L0_ffn_in['fnorm_g'], 'L0_ffn_fnorm_b': _L0_ffn_in['fnorm_b'], 'L0_ffn_fgate_w': _L0_ffn_in['fgate_w']}

def reference(x, txt, L0_tok_weight, L0_tok_bias, L0_attn_Wq, L0_attn_Wk, L0_attn_Wv, L0_ffn_hl_w, L0_ffn_hl_b, L0_ffn_wq, L0_ffn_wk, L0_ffn_wv, L0_ffn_gate_w, L0_ffn_gate_b, L0_ffn_ln_g, L0_ffn_ln_b, L0_ffn_fc1_w, L0_ffn_fc1_b, L0_ffn_fc2_w, L0_ffn_fc2_b, L0_ffn_fnorm_g, L0_ffn_fnorm_b, L0_ffn_fgate_w):
    import jax
    import jax.numpy as jnp

    def _L0_tok_ref(x, weight, bias):
        import jax, jax.numpy as jnp
        import numpy as np
        PH, PW = (64, 25)
        SH, SW = (64, 12)

        def _unfold(x, ph, pw, sh, sw):
            B, C, H, W = x.shape
            nh = (H - ph) // sh + 1
            nw = (W - pw) // sw + 1
            rows = jnp.arange(nh)[:, None] * sh + jnp.arange(ph)[None, :]
            cols = jnp.arange(nw)[:, None] * sw + jnp.arange(pw)[None, :]
            p = x[:, :, rows, :]
            p = p[:, :, :, :, cols]
            p = jnp.transpose(p, (0, 2, 4, 1, 3, 5))
            return p.reshape(B, nh * nw, C * ph * pw)
        p = _unfold(x, PH, PW, SH, SW)
        return jax.nn.gelu(jnp.einsum('bnk,kd->bnd', p, weight) + bias, approximate=False)

    def _L0_attn_ref(x, Wq, Wk, Wv):
        import jax, jax.numpy as jnp
        import numpy as np
        B, N, D = (8, 512, 64)
        q = jnp.einsum('bnd,ed->bne', x, Wq)
        k = jnp.einsum('bnd,ed->bne', x, Wk)
        v = jnp.einsum('bnd,ed->bne', x, Wv)
        energy = jnp.einsum('bqd,bkd->bqk', q, k)
        scaling = jnp.asarray(x.shape[-1] ** (-0.5), x.dtype)
        att = jax.nn.softmax(energy, axis=-1) * scaling
        out = jnp.einsum('bqk,bkv->bqv', att, v)
        return out

    def _L0_ffn_ref(x, hl_w, hl_b, wq, wk, wv, gate_w, gate_b, ln_g, ln_b, fc1_w, fc1_b, fc2_w, fc2_b, fnorm_g, fnorm_b, fgate_w):
        import jax, jax.numpy as jnp
        import numpy as np
        B, S, H, NH, NE = (4, 256, 64, 4, 4)
        D = H // NH
        EPS = 1e-08

        def layernorm(x, g, b):
            m = jnp.mean(x, axis=-1, keepdims=True)
            v = jnp.mean((x - m) ** 2, axis=-1, keepdims=True)
            return (x - m) / jnp.sqrt(v + EPS) * g + b
        b, s, h = x.shape
        nh, d, _ = wk.shape
        ne = wq.shape[1]
        sx = jnp.einsum('bsh,ndh->bnsd', x, hl_w) + hl_b[None, :, None, :]
        pad = sx == 0
        q = jnp.einsum('bnsd,neod->bneso', sx, wq)
        k = jnp.einsum('bnsd,nod->bnso', sx, wk)
        v = jnp.einsum('bnsd,nod->bnso', sx, wv)
        causal = jnp.where(jnp.tril(jnp.ones((s, s), bool)), 0.0, -jnp.inf).astype(x.dtype)
        scores = jnp.einsum('bnesd,bntd->bnest', q, k) * d ** 0.5 + causal
        att = jax.nn.softmax(scores, axis=-1)
        qkv = jnp.einsum('bnest,bntd->bnesd', att, v)
        qkv = jnp.where(pad[:, :, None], 0.0, qkv)
        out = jnp.transpose(qkv, (0, 1, 3, 2, 4)).reshape(b, nh, s, ne * d)
        gs = jax.nn.softmax(jnp.einsum('bnsf,nef->bnse', out, gate_w) + gate_b[None, :, None, :], axis=-1)
        mixed = jnp.einsum('bnsed,bnse->bnsd', out.reshape(b, nh, s, ne, d), gs)
        resid = sx[jnp.arange(nh), jnp.arange(nh)]
        hn = layernorm(mixed + resid, ln_g, ln_b)
        f_n = jnp.transpose(hn, (0, 2, 1, 3)).reshape(b, s, h)
        fx = f_n.reshape(b, s, nh, d)
        pm = fx == 0
        hx = jnp.where(pm, 0.0, fx @ fc1_w.T + fc1_b)
        hx = jax.nn.relu(hx)
        hx = jnp.where(pm, 0.0, hx @ fc2_w.T + fc2_b)
        hx = layernorm(hx + fx, fnorm_g, fnorm_b)
        fout = hx.reshape(b, s, h)
        fg = jax.nn.softmax(fout @ fgate_w.T, axis=-1)
        return (fout.reshape(b, s, nh, d) * fg[..., None]).reshape(b, s, h)
    h = _L0_tok_ref(x, L0_tok_weight, L0_tok_bias)
    h = jnp.concatenate([h, txt], axis=1)
    h = h + _L0_attn_ref(_layernorm(h, axis=-1), L0_attn_Wq, L0_attn_Wk, L0_attn_Wv)
    h = h + _L0_ffn_ref(_layernorm(h, axis=-1), L0_ffn_hl_w, L0_ffn_hl_b, L0_ffn_wq, L0_ffn_wk, L0_ffn_wv, L0_ffn_gate_w, L0_ffn_gate_b, L0_ffn_ln_g, L0_ffn_ln_b, L0_ffn_fc1_w, L0_ffn_fc1_b, L0_ffn_fc2_w, L0_ffn_fc2_b, L0_ffn_fnorm_g, L0_ffn_fnorm_b, L0_ffn_fgate_w)
    return h

_drawn_inputs = setup_inputs


def setup_inputs(seed=0):
    import zlib

    import numpy as np

    out = dict(_drawn_inputs(seed))
    spreads = {'L0_tok_bias': (0.0, 0.385),
     'L0_ffn_ln_g': (1.0, 0.2),
     'L0_ffn_ln_b': (0.0, 0.1),
     'L0_ffn_fnorm_g': (1.0, 0.2),
     'L0_ffn_fnorm_b': (0.0, 0.1)}
    factors = {'L0_ffn_wq': 8.0,
     'L0_ffn_wk': 8.0,
     'L0_ffn_wv': 2.761,
     'L0_ffn_gate_w': 8.0,
     'L0_ffn_gate_b': 8.0,
     'L0_ffn_fc1_w': 5.522,
     'L0_ffn_fc1_b': 8.0,
     'L0_ffn_fc2_w': 3.89}
    for name, (base, spread) in spreads.items():
        noise = np.random.default_rng([zlib.crc32(name.encode()), seed]).standard_normal(out[name].shape)
        drawn = base * np.exp(spread * noise) if base else spread * noise
        out[name] = jnp.asarray(drawn.astype(out[name].dtype))
    for name, factor in factors.items():
        out[name] = (out[name] * factor).astype(out[name].dtype)
    return out
```

```python
import numpy as np
from contextlib import ExitStack

import concourse.bass as bass
from concourse import mybir

F32 = mybir.dt.float32
BF16 = mybir.dt.bfloat16
ALU = mybir.AluOpType
ACT = mybir.ActivationFunctionType
AX = mybir.AxisListType.X

B = 32
NTOK = 4
NTXT = 128
S = NTOK + NTXT
HS = S // 2
D = 64
NH, NE, HD = 4, 4, 16
HP = 32
PH, PW, STEP = 64, 25, 12
P = 128
MAIN = 128
TAIL = S - MAIN
TILES = B + 1
ARENA = 14080
BUFS = 3
BIG = -3e38

C128 = {}
C64 = {}


def _columns(table, *parts):
    at = 0
    for name, n in parts:
        table[name] = (at, at + n)
        at += n
    return at


N128 = _columns(C128, ("ident", P), ("kz", NH * S), ("tmask", S), ("hl_b", 1), ("wq", NE * P), ("wk", P),
                ("wvs", 2 * D), ("sel", NH * D), ("gw", 2 * NH * NE), ("gate_b", NH * NE), ("ln_g", D),
                ("ln_b", D), ("fn_g", D), ("fn_b", D))
N64 = _columns(C64, ("wv", D), ("aq", D), ("ak", D), ("hl", P), ("fc1", D), ("fg", NH), ("fc1_b", 1), ("tok_b", 1))

GB = 4
GROUPS = B // GB
GH = 2 * GB
GT = 11
CGROUPS = TILES // GT

DVE_A = 4
DVE_A_END = 3


class Chain:

    def __init__(self, eng, sem, base=0):
        self.eng, self.sem, self.base, self.n = eng, sem, base, 0

    def mark(self, ins):
        ins.then_inc(self.sem, 1)
        self.n += 1
        return self.n

    def need(self, n):
        self.eng.wait_ge(self.sem, self.base + n)


def fusion_kernel(nc, x, txt, tokw, c128, c64, fc2, masks, out, dbg=None):
    ctx = ExitStack()
    with ctx:
        def sb(name, shape, dt=F32):
            return ctx.enter_context(nc.sbuf_tensor(name, shape, dt))

        def sem(name):
            return ctx.enter_context(nc.semaphore(name))

        arena = sb("arena", [P, ARENA])

        class Carve:

            def __init__(self):
                self.at = 0

            def take(self, rows, *shape):
                n = int(np.prod(shape))
                a = arena[0:rows, self.at:self.at + n]
                self.at += n
                assert self.at <= ARENA
                names = "abc"[:len(shape)]
                if len(shape) == 1:
                    return a
                return a.rearrange("p (%s) -> p %s" % (" ".join(names), " ".join(names)), **dict(zip(names[1:], shape[1:])))

        k128 = sb("k128", [P, N128])
        k64 = sb("k64", [D, N64])
        fc2_sb = sb("fc2_sb", [D + 1, D])
        masks_sb = sb("masks_sb", [P, P + 2 * NE * P], BF16)

        def c(name, rows=P):
            a, b = C128[name]
            return k128[0:rows, a:b]

        def w(name):
            a, b = C64[name]
            return k64[:, a:b]

        ident = c("ident")
        ident_bf = masks_sb[:, 0:P]
        mask_rows = masks_sb[:, P:P + NE * P]
        mask_cols = masks_sb[:, P + NE * P:P + 2 * NE * P]
        gmat = sb("gmat", [D, P])
        half_neg = sb("half_neg", [P, GT * NH])
        eps_ln = sb("eps_ln", [HS, GH])
        eps_hd = sb("eps_hd", [P, GT * NH])

        early = Carve()
        xs = early.take(PH, B, D)
        tokw_sb = early.take(PH, PW, D)
        tokT = sb("tokT", [D, P])
        tok = sb("tok", [P, D])
        h0 = early.take(HS, B, 2, D)

        masks_f = early.take(P, P + 2 * NE * P)

        nsum = sb("nsum", [HS, 2, GH])
        xc = early.take(HS, 2, GH, D)
        sq = early.take(HS, 2, GH, D)
        var = sb("var", [HS, 2, GH])
        vare = sb("vare", [HS, 2, GH])
        rstd = sb("rstd", [HS, 2, GH])
        xn = early.take(HS, 2, GH, D)
        xnT = [early.take(D, GB * S) for i in range(2)]
        zT = [early.take(D, GB * S) for i in range(2)]
        vs = [sb(f"vs{i}", [HS, GH, D]) for i in range(2)]
        nmax = sb("nmax", [HS, GH])
        rsum = sb("rsum", [HS, GH])
        rinv = sb("rinv", [HS, GH])
        probs = [sb(f"probs{i}", [HS, 2, S]) for i in range(2)]
        probsT = [sb(f"probsT{i}", [HS, 2, S]) for i in range(2)]
        attn = sb("attn", [HS, GH, D])
        h1 = [sb(f"h1_{i}", [HS, GH, D]) for i in range(2)]
        xn2T = sb("xn2T", [D, GB * S])[:]
        sxT = sb("sxT", [P, B * S])
        h1_dram = nc.dram_tensor("h1_dram", (B, S, D), F32, kind="Internal").ap()

        sxb = [sb(f"sxb{i}", [P, S]) for i in range(BUFS)]
        qs = [sb(f"qs{i}", [P, NE, MAIN]) for i in range(BUFS)]
        qt = [sb(f"qt{i}", [P, NE * TAIL]) for i in range(BUFS)]
        kz = [sb(f"kz{i}", [P, NH, S]) for i in range(BUFS)]
        va = [sb(f"va{i}", [P, NH, HP]) for i in range(BUFS)]
        va_t = [sb(f"va_t{i}", [TAIL, NH, HP]) for i in range(BUFS)]
        mx = sb("mx", [P, NH * NE])
        mxT = sb("mxT", [NH * NE, P])
        st_m = sb("st_m", [P, S])
        nmt = sb("nmt", [P, 1])
        pt_row = sb("pt_row", [P, S])
        ptT = sb("ptT", [P, P])
        ptT4 = sb("ptT4", [TAIL, P])
        pT = sb("pT", [P, NH, NE * P])
        u_sb = sb("u_sb", [P, NE, P])
        u_tail = sb("u_tail", [P, NE, B, TAIL])
        rden = sb("rden", [P, NE * NH])
        sx_rep = sb("sx_rep", [P, NH + 1, B, TAIL])
        o_all = sb("o_all", [P, TILES, NE * D])
        sx_tok = sb("sx_tok", [P, TILES, D])
        resid = sb("resid", [P, TILES, D])

        late = Carve()
        h1c = sb("h1c", [P, TILES, D])
        nz = late.take(P, GT, D)
        om = late.take(P, GT, NE * D)
        omT = late.take(P, GT, 2, P)
        lg = sb("lg", [P, GT, NE * NH])
        lgm = sb("lgm", [P, GT, NH])
        y = late.take(P, GT, D)
        ysq = late.take(P, GT, D)
        fx = late.take(P, GT, D)
        nzf = late.take(P, GT, D)
        st1 = sb("st1", [P, GT * NH])
        st2 = sb("st2", [P, GT * NH])
        st3 = sb("st3", [P, GT * NH])
        fxT = late.take(D, GT * P)
        nzT = late.take(D, GT * P)
        hT = late.take(D + 1, GT * P)
        hg = sb("hg", [P, GT, NH])
        res = late.take(P, GT, D)

        banks = [ctx.enter_context(nc.psum_tensor(f"bank{i}", [P, 512], F32)) for i in range(8)]

        s_cst = sem("s_cst")
        s_x_in = sem("s_x_in")
        s_w_in = sem("s_w_in")
        s_h0_in = sem("s_h0_in")
        s_init = sem("s_init")
        s_gm = sem("s_gm")
        s_gmc = sem("s_gmc")
        s_tokp = sem("s_tokp")
        s_tokg = sem("s_tokg")
        s_tok_out = sem("s_tok_out")
        s_a_nm = sem("s_a_nm")
        s_a_sq = sem("s_a_sq")
        s_a_var = sem("s_a_var")
        s_a_rs = sem("s_a_rs")
        s_a_xn = sem("s_a_xn")
        s_a_tp = sem("s_a_tp")
        s_a_tc = sem("s_a_tc")
        s_a_zv = sem("s_a_zv")
        s_a_zc = sem("s_a_zc")
        s_a_vc = sem("s_a_vc")
        s_a_s = sem("s_a_s")
        s_a_mx = sem("s_a_mx")
        s_a_e = sem("s_a_e")
        s_a_pt = sem("s_a_pt")
        s_a_ptc = sem("s_a_ptc")
        s_a_av = sem("s_a_av")
        s_a_h1 = sem("s_a_h1")
        s_b_nm = sem("s_b_nm")
        s_b_sq = sem("s_b_sq")
        s_b_var = sem("s_b_var")
        s_b_rs = sem("s_b_rs")
        s_b_xn = sem("s_b_xn")
        s_b_tp = sem("s_b_tp")
        s_b_tc = sem("s_b_tc")
        s_b_sx = sem("s_b_sx")
        s_b_sxc = sem("s_b_sxc")
        s_dve_a_end = sem("s_dve_a_end")
        s_dve_a = sem("s_dve_a")
        s_pool_a = sem("s_pool_a")
        s_p1 = sem("s_p1")
        s_p1_free = sem("s_p1_free")
        s_p2 = sem("s_p2")
        s_ex = sem("s_ex")
        s_proj = sem("s_proj")
        s_pevA = sem("s_pevA")
        s_pevD = sem("s_pevD")
        s_mT = sem("s_mT")
        s_mTc = sem("s_mTc")
        s_st = sem("s_st")
        s_stD = sem("s_stD")
        s_nmtd = sem("s_nmtd")
        s_ptd = sem("s_ptd")
        s_tt = sem("s_tt")
        s_ttc = sem("s_ttc")
        s_ut = sem("s_ut")
        s_utc = sem("s_utc")
        s_av = sem("s_av")
        s_uc = sem("s_uc")
        s_tT = sem("s_tT")
        s_rd = sem("s_rd")
        s_oc = sem("s_oc")
        s_sxr = sem("s_sxr")
        s_rs_mm = sem("s_rs_mm")
        s_resd = sem("s_resd")
        s_h1_in = sem("s_h1_in")
        s_dve_c = sem("s_dve_c")
        s_act_c = sem("s_act_c")
        s_pe_c = sem("s_pe_c")
        s_pool_cc = sem("s_pool_cc")
        s_c_out = sem("s_c_out")
        m_in = [sem(f"s_m_in{i}") for i in range(BUFS)]
        sx_in = [sem(f"s_sx_in{i}") for i in range(BUFS)]
        a_out = [sem(f"s_a_out{i}") for i in range(2)]

        block = ctx.enter_context(nc.Block())
        N_CST = 4
        NB_TXT = 4
        PB = B // NB_TXT

        def steps_a(eng, step, last_too=True):
            step(0, 0, first=True)
            with eng.Fori(0, (GROUPS - 2) // 2) as it:
                for u in range(2):
                    step(it * 2 + (u + 1), (u + 1) % 2, it=it, u=u)
            step(GROUPS - 1, (GROUPS - 1) % 2, last=True)

        def steps_b(eng, step):
            with eng.Fori(0, (B - 2) // BUFS) as it:
                for u in range(BUFS):
                    step(it * BUFS + (u + 1), u + 1, it)
            step(B - 1, (B - 1) % BUFS + BUFS, (B - 2) // BUFS)

        @block.sync
        def _(sp):
            sp.dma_start(xs[:], x.rearrange("b c r w -> r (b c) w")).then_inc(s_x_in, 16)
            sp.dma_start(k64[:], c64).then_inc(s_cst, 16)
            sp.dma_start(k128[:], c128).then_inc(s_cst, 16)
            for q in range(NB_TXT):
                rows = slice(q * PB, (q + 1) * PB)
                sp.dma_start(h0[NTOK:HS, rows, 0, :], txt[rows, 0:HS - NTOK, :].rearrange("b t d -> t b d")).then_inc(s_h0_in, 16)
                sp.dma_start(h0[:, rows, 1, :], txt[rows, HS - NTOK:NTXT, :].rearrange("b t d -> t b d")).then_inc(s_h0_in, 16)
            sp.wait_ge(s_tokg, 2)
            for n in range(NTOK):
                sp.dma_start(h0[n:n + 1, :, 0, :], tok[n:P:NTOK, :]).then_inc(s_tok_out, 16)

            def step(g, p, first=False, last=False, it=None, u=0):
                sp.wait_ge(s_a_h1, g + 1)
                dst = h1_dram[bass.ds(g * GB, GB), :, :].rearrange("b (h t) d -> t b h d", t=HS)
                src = h1[p][:].rearrange("t (b h) d -> t b h d", h=2)
                sp.dma_start(dst, src).then_inc(a_out[p], 16)
            steps_a(sp, step)

            def load_sx(b, p, first=False):
                if not first:
                    sp.wait_ge(s_mT, b - 1)
                sp.dma_start(sxb[p][:], sxT[:, bass.ds(b * S, S)]).then_inc(sx_in[p], 16)

            def send_m(b, p):
                sp.wait_ge(s_mTc, b + 1)
                for n in range(NH):
                    sp.dma_start(qs[p][HP * n + HD:HP * n + HD + 1, :, :],
                                 mxT[NE * n:NE * n + NE, :]).then_inc(m_in[p], 16)
            sp.wait_ge(s_b_sxc, 2 * GROUPS)
            load_sx(0, 0, True)
            load_sx(1, 1, True)
            send_m(0, 0)

            def step_b(b, u, it):
                if b is not B - 1:
                    load_sx(b + 1, (u + 1) % BUFS)
                send_m(b, u % BUFS)
            steps_b(sp, step_b)

            for q in range(2):
                sp.wait_ge(a_out[q], 16 * (GROUPS // 2 + 1))
            sp.dma_start(h1c[:, 0:B, :], h1_dram[:, 0:MAIN, :].rearrange("b t d -> t b d")).then_inc(s_h1_in, 16)
            sp.dma_start(h1c[:, B, :], h1_dram[:, MAIN:S, :]).then_inc(s_h1_in, 16)
            for g in range(CGROUPS):
                sp.wait_ge(s_dve_c, (g + 1) * C_DVE)
                n = min(GT, B - g * GT)
                sp.dma_start(out[g * GT:g * GT + n, 0:MAIN, :].rearrange("b t d -> t b d"), res[:, 0:n, :]).then_inc(s_c_out, 16)
            sp.dma_start(out[:, MAIN:S, :], res[:, GT - 1, :]).then_inc(s_c_out, 16)
            sp.wait_ge(s_c_out, 16 * (CGROUPS + 1))

        @block.gpsimd
        def _(pool):
            pool.dma_start(tokw_sb[:], tokw).then_inc(s_w_in, 16)
            pool.memset(eps_ln[:], 1e-5)
            pool.memset(eps_hd[:], 1e-8)
            pool.memset(half_neg[:], -0.5).then_inc(s_init, 1)
            pool.wait_ge(s_init, 1)

            def rs(which, n_sem, base):
                pool.tensor_tensor(vare[:, which, :], var[:, which, :], eps_ln[:], ALU.add).then_inc(s_pool_a, 1)
                pool.wait_ge(s_pool_a, base)
                pool.tensor_tensor(rstd[:, which, :], vare[:, which, :], half_neg[0:HS, 0:GH], ALU.pow).then_inc(n_sem, 1)

            def step(g, p, first=False, last=False, it=None, u=0):
                if not first:
                    pool.wait_ge(s_b_var, g)
                    rs(1, s_b_rs, 2 * g + 1)
                if not last:
                    pool.wait_ge(s_a_var, g + 2)
                    rs(0, s_a_rs, 2 * g + 2)
            pool.wait_ge(s_a_var, 1)
            rs(0, s_a_rs, 1)
            steps_a(pool, step)
            pool.wait_ge(s_b_var, GROUPS)
            rs(1, s_b_rs, 2 * GROUPS)

            for g in range(CGROUPS):
                for j, at in enumerate((C_VAR1, C_VAR2)):
                    pool.wait_ge(s_dve_c, g * C_DVE + at)
                    pool.tensor_tensor(st2[:], st2[:], eps_hd[:], ALU.add).then_inc(s_pool_cc, 1)
                    pool.wait_ge(s_pool_cc, 4 * g + 2 * j + 1)
                    pool.tensor_tensor(st3[:], st2[:], half_neg[:], ALU.pow).then_inc(s_pool_cc, 1)

        @block.scalar
        def _(act):
            act.dma_start(fc2_sb[:], fc2).then_inc(s_cst, 16)
            act.dma_start(masks_f, masks).then_inc(s_cst, 16)
            act.wait_ge(s_cst, 16 * N_CST)
            act.wait_ge(s_tokp, 1)
            act.activation(tokT[:], banks[6][0:D, 0:P], ACT.Gelu, bias=w("tok_b")).then_inc(s_tokg, 1)
            act.wait_ge(s_tokp, 2)
            act.activation(tok[:], banks[6][:, P:P + D], ACT.Copy).then_inc(s_tokg, 1)

            def square(which, need, count, done):
                act.wait_ge(need, count)
                act.activation(sq[:, which], xc[:, which], ACT.Square, scale=float(D) ** -0.5).then_inc(done, 1)

            def evac2(dst, need, count, done):
                act.wait_ge(need, count)
                for h in range(2):
                    act.activation(dst[:, h * 2 * S:(h + 1) * 2 * S], banks[h][0:D, 0:2 * S], ACT.Copy).then_inc(done, 1)

            def evac_turned(dst, need, count, done):
                act.wait_ge(need, count)
                for h in range(2):
                    act.activation(dst.rearrange("d (b h t) -> d b h t", h=2, t=HS)[:, :, h, :],
                                   banks[0][h * D:(h + 1) * D, 0:GB * HS].rearrange("d (b t) -> d b t", t=HS),
                                   ACT.Copy).then_inc(done, 1)

            def entry_a(g, p, first):
                square(0, s_a_nm, g + 1, s_a_sq)
                evac_turned(xnT[p], s_a_tp, g + 1, s_a_tc)
                evac2(zT[p], s_a_zv, g + 1, s_a_zc)
                act.activation(vs[p][:], banks[2][0:HS, 0:GH * D].rearrange("t (j d) -> t j d", d=D), ACT.Copy).then_inc(s_a_vc, 1)

            def exps(g, b):
                act.wait_ge(s_a_mx, g * GB + b + 1)
                if b >= 2:
                    act.wait_ge(s_a_pt, g * GB + b - 1)
                for h in range(2):
                    act.activation(probs[b % 2][:, h, :], banks[4 + b % 2][0:HS, h * S:(h + 1) * S], ACT.Exp,
                                   bias=nmax[:, 2 * b + h:2 * b + h + 1],
                                   accum_out=rsum[:, 2 * b + h:2 * b + h + 1]).then_inc(s_a_e, 1)

            def exit_a(g):
                square(1, s_b_nm, g + 1, s_b_sq)
                evac_turned(xn2T, s_b_tp, g + 1, s_b_tc)
                act.wait_ge(s_b_sx, g + 1)
                for h in range(2):
                    act.activation(sxT[:, bass.ds(g * (GB * S) + h * 2 * S, 2 * S)], banks[h][:, 0:2 * S], ACT.Identity,
                                   bias=c("hl_b")).then_inc(s_b_sxc, 1)

            def step(g, p, first=False, last=False, it=None, u=0):
                if not first:
                    act.wait_ge(s_a_h1, g)
                for b in range(GB):
                    exps(g, b)
                    if b == 1 and not first:
                        exit_a(g - 1)
                if not last:
                    entry_a(g + 1, 1 - p, False)
            entry_a(0, 0, True)
            steps_a(act, step)
            exit_a(GROUPS - 1)

            def evac_proj(b, p):
                act.wait_ge(s_proj, b + 1)
                q = banks[5][:, 0:3 * S].rearrange("p (e t) -> p e t", e=3)
                act.activation(qs[p][:, 0:3, :], q[:, :, 0:MAIN], ACT.Copy)
                act.activation(qt[p][:, 0:3 * TAIL].rearrange("p (e t) -> p e t", e=3), q[:, :, MAIN:S], ACT.Copy).then_inc(s_pevA, 1)

            def exp_tail(b):
                act.wait_ge(s_nmtd, b + 1)
                act.activation(pt_row[:], st_m[:], ACT.Exp, bias=nmt[:]).then_inc(s_ptd, 1)

            def copy_m(b):
                act.wait_ge(s_mT, b + 1)
                act.activation(mxT[:], banks[7][0:NH * NE, 0:P], ACT.Copy).then_inc(s_mTc, 1)

            def exp_main(b, n):
                act.wait_ge(s_p2, b * NH + n + 1)
                act.activation(pT[:, n, :], banks[2 + n % 2][:, :], ACT.Exp).then_inc(s_ex, 1)

            def evac_tail_probs(b):
                act.wait_ge(s_tt, b + 1)
                act.activation(ptT[:], banks[7][:, S:S + P], ACT.Copy)
                act.activation(ptT4[:], banks[7][0:TAIL, S + P:S + 2 * P], ACT.Copy).then_inc(s_ttc, 1)

            def evac_tail_out(b):
                act.wait_ge(s_ut, b + 1)
                act.activation(u_tail[:, :, bass.ds(b, 1), :],
                               banks[7][:, S + 2 * P:S + 2 * P + NE * TAIL].rearrange("p (e o t) -> p e o t", e=NE, o=1),
                               ACT.Copy).then_inc(s_utc, 1)

            def evac_out(b):
                act.wait_ge(s_av, (b + 1) * NH)
                act.activation(u_sb[:], banks[4][:, :].rearrange("p (e t) -> p e t", e=NE), ACT.Copy).then_inc(s_uc, 1)

            def step_b(b, u, it):
                exp_main(b - 1, 0)
                exp_main(b - 1, 1)
                evac_tail_probs(b - 1)
                exp_main(b - 1, 2)
                evac_tail_out(b - 1)
                exp_main(b - 1, 3)
                copy_m(b)
                evac_out(b - 1)
                if b is not B - 1:
                    evac_proj(b + 1, (u + 1) % BUFS)
                exp_tail(b)

            evac_proj(0, 0)
            evac_proj(1, 1)
            copy_m(0)
            exp_tail(0)
            steps_b(act, step_b)
            exp_main(B - 1, 0)
            exp_main(B - 1, 1)
            evac_tail_probs(B - 1)
            exp_main(B - 1, 2)
            evac_tail_out(B - 1)
            exp_main(B - 1, 3)
            evac_out(B - 1)

            for g in range(CGROUPS):
                for q in range((GT + 1) // 2):
                    n = min(2, GT - 2 * q)
                    act.wait_ge(s_pe_c, g * C_PE + q + 1)
                    act.activation(omT[:, 2 * q:2 * q + n, :, :],
                                   banks[q % 3][:, 0:n * 2 * P].rearrange("p (t h s) -> p t h s", t=n, h=2),
                                   ACT.Copy).then_inc(s_act_c, 1)
                act.wait_ge(s_dve_c, g * C_DVE + C_LGS)
                act.activation(lg[:], lg[:], ACT.Exp).then_inc(s_act_c, 1)
                act.wait_ge(s_dve_c, g * C_DVE + C_YC1)
                act.activation(ysq[:], y[:], ACT.Square, scale=float(HD) ** -0.5).then_inc(s_act_c, 1)
                for q in range(3):
                    n = min(4, GT - 4 * q)
                    act.wait_ge(s_pe_c, g * C_PE + C_PFX + q)
                    act.activation(fxT[:, q * 4 * P:(q * 4 + n) * P], banks[4 + q][0:D, 0:n * P], ACT.Copy).then_inc(s_act_c, 1)
                for q in range(3):
                    n = min(4, GT - 4 * q)
                    act.wait_ge(s_pe_c, g * C_PE + C_PFC1 + q)
                    act.activation(hT[0:D, q * 4 * P:(q * 4 + n) * P], banks[4 + q][0:D, 0:n * P], ACT.Relu,
                                   bias=w("fc1_b")).then_inc(s_act_c, 1)
                act.wait_ge(s_dve_c, g * C_DVE + C_YC2)
                act.activation(ysq[:], y[:], ACT.Square, scale=float(HD) ** -0.5).then_inc(s_act_c, 1)
                for q in range(3):
                    n = min(4, GT - 4 * q)
                    act.wait_ge(s_pe_c, g * C_PE + C_PFO + q)
                    act.activation(fxT[:, q * 4 * P:(q * 4 + n) * P], banks[4 + q][0:D, 0:n * P], ACT.Copy).then_inc(s_act_c, 1)
                act.wait_ge(s_dve_c, g * C_DVE + C_HGS)
                act.activation(hg[:], hg[:], ACT.Exp).then_inc(s_act_c, 1)

        @block.vector
        def _(dve):
            dve.memset(h1[0][:], 0.0).then_inc(a_out[0], 16)
            dve.memset(h1[1][:], 0.0).then_inc(a_out[1], 16)
            dve.memset(mx[:], 0.0).then_inc(s_p1_free, 2)
            dve.memset(st_m[:], 0.0).then_inc(s_ex, 2)
            dve.memset(ptT4[:], 0.0).then_inc(s_utc, 1)
            dve.memset(rden[:], 0.0).then_inc(s_oc, 1)
            for p in range(BUFS):
                dve.memset(va[p][:], 1.0)
                dve.memset(va_t[p][:], 1.0)
            dve.memset(banks[7][:], 0.0).then_inc(s_init, 1)
            dve.wait_ge(s_init, 2)
            dve.wait_ge(s_cst, 16 * N_CST)
            for p in range(BUFS):
                dve.tensor_copy(kz[p][:], c("kz").rearrange("p (n t) -> p n t", n=NH)).then_inc(s_init, 1)
            dve.tensor_copy(masks_sb[:], masks_f).then_inc(s_init, 1)
            dve.tensor_scalar(c("wq"), c("wq"), float(HD) ** 0.5, None, ALU.mult).then_inc(s_init, 1)
            dve.memset(gmat[:, D:P], 0.0)
            dve.wait_ge(s_gm, 1)
            dve.tensor_copy(gmat[:, 0:D], banks[7][0:D, 0:D]).then_inc(s_gmc, 1)

            def center(which, src, ch, done):
                a = ch.mark(dve.tensor_reduce(nsum[:, which, :], src, axis=AX, op=ALU.add, negate=True))
                ch.need(a)
                dve.scalar_tensor_tensor(xc[:, which], nsum[:, which, :].unsqueeze(2).broadcast_to([HS, GH, D]),
                                         1.0 / D, src, ALU.mult, ALU.add).then_inc(done, 1)

            def variance(which, need, count, done):
                dve.wait_ge(need, count)
                dve.tensor_reduce(var[:, which, :], sq[:, which], axis=AX, op=ALU.add).then_inc(done, 1)

            def scale(which, need, count, done):
                dve.wait_ge(need, count)
                dve.tensor_tensor(xn[:, which], xc[:, which], rstd[:, which, :].unsqueeze(2).broadcast_to([HS, GH, D]),
                                  ALU.mult).then_inc(done, 1)

            def h0_of(g):
                return h0[:, bass.ds(g * GB, GB), :, :].rearrange("t b h d -> t (b h) d")

            def maxima(g, b):
                dve.wait_ge(s_a_s, g * GB + b + 1)
                dve.tensor_reduce(nmax[:, 2 * b:2 * b + 2], banks[4 + b % 2][0:HS, 0:2 * S].rearrange("t (h u) -> t h u", h=2),
                                  axis=AX, op=ALU.max, negate=True).then_inc(s_a_mx, 1)

            def evac_pt(g, b, first):
                dve.wait_ge(s_a_pt, g * GB + b + 1)
                if not (first and b < 2):
                    dve.wait_ge(s_a_av, g * GB + b - 1)
                dve.tensor_copy(probsT[b % 2][:], banks[6 + b % 2][0:HS, 0:2 * S].rearrange("t (h u) -> t h u", h=2)).then_inc(s_a_ptc, 1)

            def step(g, p, first=False, last=False, it=None, u=0):
                if first:
                    ch = Chain(dve, s_dve_a_end, 1)
                elif last:
                    ch = Chain(dve, s_dve_a_end, 1 + DVE_A_END)
                else:
                    ch = Chain(dve, s_dve_a, (it * 2 + u) * DVE_A)
                if not first:
                    dve.wait_ge(s_a_h1, g)
                    center(1, h1[1 - p][:], ch, s_b_nm)
                maxima(g, 0)
                maxima(g, 1)
                if not first:
                    variance(1, s_b_sq, g, s_b_var)
                if not last:
                    center(0, h0_of(g + 1), ch, s_a_nm)
                evac_pt(g, 0, first)
                maxima(g, 2)
                if not first:
                    scale(1, s_b_rs, g, s_b_xn)
                evac_pt(g, 1, first)
                maxima(g, 3)
                evac_pt(g, 2, first)
                evac_pt(g, 3, first)
                if not last:
                    variance(0, s_a_sq, g + 2, s_a_var)
                dve.wait_ge(s_a_e, (g + 1) * GH)
                inverted = ch.mark(dve.reciprocal(rinv[:], rsum[:]))
                if not last:
                    scale(0, s_a_rs, g + 2, s_a_xn)
                ch.need(inverted)
                dve.wait_ge(s_a_av, (g + 1) * GB)
                scaled = ch.mark(dve.scalar_tensor_tensor(
                    attn[:], banks[3][0:HS, 0:GH * D].rearrange("t (j d) -> t j d", d=D), float(D) ** -0.5,
                    rinv[:].unsqueeze(2).broadcast_to([HS, GH, D]), ALU.mult, ALU.mult))
                ch.need(scaled)
                if last:
                    dve.wait_ge(a_out[p], 16 * ((GROUPS - 1) // 2 + 1))
                elif not first:
                    dve.wait_ge(a_out[p], (it + (u + 1)) * 16)
                dve.tensor_tensor(h1[p][:], attn[:], h0_of(g), ALU.add).then_inc(s_a_h1, 1)
                assert ch.n == (DVE_A_END if first or last else DVE_A)

            dve.wait_ge(s_h0_in, 16 * 2 * NB_TXT)
            dve.wait_ge(s_tok_out, 16 * NTOK)
            center(0, h0_of(0), Chain(dve, s_dve_a_end), s_a_nm)
            variance(0, s_a_sq, 1, s_a_var)
            scale(0, s_a_rs, 1, s_a_xn)
            steps_a(dve, step)
            dve.wait_ge(s_a_h1, GROUPS)
            center(1, h1[(GROUPS - 1) % 2][:], Chain(dve, s_dve_a_end, 1 + 2 * DVE_A_END), s_b_nm)
            variance(1, s_b_sq, GROUPS, s_b_var)
            scale(1, s_b_rs, GROUPS, s_b_xn)


            def evac_proj(b, p):
                dve.wait_ge(s_proj, b + 1)
                dve.tensor_copy(qs[p][:, 3, :], banks[6][:, 0:MAIN])
                dve.tensor_copy(qt[p][:, 3 * TAIL:], banks[6][:, MAIN:S])
                for n in range(NH):
                    rows = slice(HP * n, HP * n + HD)
                    dve.tensor_copy(kz[p][rows, n, :], banks[6][rows, S:2 * S])
                dve.tensor_copy(va[p][:, :, 0:HD], banks[6][:, 2 * S:2 * S + D].rearrange("t (n d) -> t n d", n=NH))
                dve.tensor_copy(va_t[p][:, :, 0:HD], banks[6][0:TAIL, 2 * S + 2 * D:2 * S + 3 * D].rearrange("t (n d) -> t n d", n=NH))
                dve.tensor_copy(sx_tok[:, bass.ds(b, 1), :], banks[6][:, 2 * S + D:2 * S + 2 * D].unsqueeze(1)).then_inc(s_pevD, 1)

            def row_max(b, n):
                dve.wait_ge(s_p1, b * NH + n + 1)
                dve.tensor_reduce(mx[:, n * NE:(n + 1) * NE], banks[n % 2][:, :].rearrange("p (e t) -> p e t", e=NE),
                                  axis=AX, op=ALU.max).then_inc(s_p1_free, 1)

            def tail_max(b):
                dve.wait_ge(s_st, b + 1)
                dve.wait_ge(s_ptd, b)
                dve.tensor_tensor(st_m[:], banks[7][:, 0:S], c("tmask"), ALU.add).then_inc(s_stD, 1)
                dve.wait_ge(s_stD, b + 1)
                dve.tensor_reduce(nmt[:], st_m[:], axis=AX, op=ALU.max, negate=True).then_inc(s_nmtd, 1)

            def norm(b):
                t = banks[4][:, :].rearrange("p (a h) -> p a h", h=HP)
                dve.wait_ge(s_tT, b + 1)
                dve.reciprocal(rden[:].unsqueeze(2), t[:, :, HD:HD + 1]).then_inc(s_rd, 1)
                dve.wait_ge(s_rd, b + 1)
                dve.tensor_tensor(o_all[:, bass.ds(b, 1), :].rearrange("p o (a d) -> p (o a) d", d=HD), t[:, :, 0:HD],
                                  rden[:].unsqueeze(2).broadcast_to([P, NE * NH, HD]), ALU.mult).then_inc(s_oc, 1)

            def step_b(b, u, it):
                row_max(b, 0)
                row_max(b, 1)
                tail_max(b)
                row_max(b, 2)
                row_max(b, 3)
                if b is not B - 1:
                    evac_proj(b + 1, (u + 1) % BUFS)
                norm(b - 1)

            evac_proj(0, 0)
            for n in range(NH):
                row_max(0, n)
            tail_max(0)
            evac_proj(1, 1)
            steps_b(dve, step_b)
            norm(B - 1)
            tails = sxT[:].rearrange("p (b t) -> p b t", b=B)[:, :, MAIN:S]
            dve.tensor_copy(sx_rep[:, 0:NH], tails[:, 0:NH, :].unsqueeze(2).broadcast_to([P, NH, B, TAIL]))
            dve.tensor_copy(sx_rep[:, NH], tails).then_inc(s_sxr, 1)
            norm(B)
            dve.wait_ge(s_rs_mm, 1)
            dve.tensor_copy(sx_tok[:, B, :], banks[6][:, 0:D]).then_inc(s_resd, 1)
            dve.tensor_copy(resid[:, B, :], banks[6][:, D:2 * D]).then_inc(s_resd, 1)
            for n in range(NH):
                dve.tensor_copy(resid[:, 0:B, n * HD:(n + 1) * HD],
                                sx_tok[:, n:n + 1, n * HD:(n + 1) * HD].broadcast_to([P, B, HD])).then_inc(s_resd, 1)
            dve.wait_ge(s_resd, 2 + NH)

            dve.memset(hT[D:D + 1, :], 1.0).then_inc(s_init, 1)
            dve.wait_ge(s_oc, TILES + 1)
            for g in range(CGROUPS):
                ch = Chain(dve, s_dve_c, g * C_DVE)
                tiles = slice(g * GT, (g + 1) * GT)
                heads = "p t (n d) -> p (t n) d"

                def wide(a):
                    return a.unsqueeze(2).broadcast_to([P, GT * NH, HD])

                def normalise(dst, gain, shift, a_sq, at_yc, at_var, pool_at):
                    yh = y[:].rearrange(heads, n=NH)
                    a = ch.mark(dve.tensor_reduce(st1[:], yh, axis=AX, op=ALU.add, negate=True))
                    ch.need(a)
                    a = ch.mark(dve.scalar_tensor_tensor(yh, wide(st1[:]), 1.0 / HD, yh, ALU.mult, ALU.add))
                    assert a == at_yc, a
                    dve.wait_ge(s_act_c, g * C_ACT + a_sq)
                    a = ch.mark(dve.tensor_reduce(st2[:], ysq[:].rearrange(heads, n=NH), axis=AX, op=ALU.add))
                    assert a == at_var, a
                    dve.wait_ge(s_pool_cc, 4 * g + pool_at)
                    a = ch.mark(dve.tensor_tensor(dst[:].rearrange(heads, n=NH), yh, wide(st3[:]), ALU.mult))
                    ch.need(a)
                    a = ch.mark(dve.tensor_tensor(dst[:], dst[:], c(gain).unsqueeze(1).broadcast_to([P, GT, D]), ALU.mult))
                    ch.need(a)
                    return ch.mark(dve.tensor_tensor(dst[:], dst[:], c(shift).unsqueeze(1).broadcast_to([P, GT, D]), ALU.add))

                def softmax(buf, view, tiny, inv, at_sub, act_at, spread):
                    a = ch.mark(dve.tensor_reduce(tiny, view, axis=AX, op=ALU.max))
                    ch.need(a)
                    a = ch.mark(dve.tensor_tensor(buf, buf, spread(tiny), ALU.subtract))
                    assert a == at_sub, a
                    dve.wait_ge(s_act_c, g * C_ACT + act_at)
                    a = ch.mark(dve.tensor_reduce(tiny, view, axis=AX, op=ALU.add))
                    ch.need(a)
                    a = ch.mark(dve.reciprocal(inv, tiny))
                    ch.need(a)
                    a = ch.mark(dve.tensor_tensor(buf, buf, spread(inv), ALU.mult))
                    ch.need(a)

                a = ch.mark(dve.tensor_scalar(nz[:], sx_tok[:, tiles, :], 0.0, None, ALU.not_equal))
                ch.need(a)
                a = ch.mark(dve.tensor_tensor(om[:].rearrange("p t (e d) -> p t e d", e=NE),
                                              o_all[:, tiles, :].rearrange("p t (e d) -> p t e d", e=NE),
                                              nz[:].unsqueeze(2).broadcast_to([P, GT, NE, D]), ALU.mult))
                assert a == C_OM
                dve.wait_ge(s_pe_c, g * C_PE + C_PLG)
                a = ch.mark(dve.tensor_tensor(lg[:], banks[3][:, 0:GT * NE * NH].rearrange("p (t a) -> p t a", t=GT),
                                              c("gate_b").unsqueeze(1).broadcast_to([P, GT, NE * NH]), ALU.add))
                ch.need(a)
                softmax(lg[:].rearrange("p t (e n) -> p t e n", e=NE), lg[:].rearrange("p t (e n) -> p t n e", e=NE),
                        lgm[:], st1[:].rearrange("p (t n) -> p t n", n=NH), C_LGS, C_AEXP,
                        lambda v: v.unsqueeze(2).broadcast_to([P, GT, NE, NH]))
                a = ch.mark(dve.tensor_tensor(om[:].rearrange("p t (a d) -> p (t a) d", d=HD),
                                              om[:].rearrange("p t (a d) -> p (t a) d", d=HD),
                                              lg[:].rearrange("p t a -> p (t a)").unsqueeze(2).broadcast_to([P, GT * NE * NH, HD]),
                                              ALU.mult))
                ch.need(a)
                a = ch.mark(dve.tensor_reduce(y[:], om[:].rearrange("p t (e d) -> p t d e", e=NE), axis=AX, op=ALU.add))
                ch.need(a)
                a = ch.mark(dve.tensor_tensor(y[:], y[:], resid[:, tiles, :], ALU.add))
                ch.need(a)
                a = normalise(fx, "ln_g", "ln_b", C_ASQ1, C_YC1, C_VAR1, 2)
                assert a == C_FX, a
                ch.need(a)
                ch.mark(dve.tensor_scalar(nzf[:], fx[:], 0.0, None, ALU.not_equal))
                dve.wait_ge(s_act_c, g * C_ACT + C_AFX)
                a = ch.mark(dve.tensor_scalar(nzT[:], fxT[:], 0.0, None, ALU.not_equal))
                ch.need(a)
                dve.wait_ge(s_act_c, g * C_ACT + C_AH)
                a = ch.mark(dve.tensor_tensor(hT[0:D, :], hT[0:D, :], nzT[:], ALU.mult))
                assert a == C_HT, a
                dve.wait_ge(s_pe_c, g * C_PE + C_PFC2)
                a = ch.mark(dve.tensor_tensor(y[:, 0:8, :], banks[0][:, :].rearrange("p (t d) -> p t d", d=D), nzf[:, 0:8, :], ALU.mult))
                a = ch.mark(dve.tensor_tensor(y[:, 8:GT, :], banks[1][:, 0:(GT - 8) * D].rearrange("p (t d) -> p t d", d=D), nzf[:, 8:GT, :], ALU.mult))
                ch.need(a)
                a = ch.mark(dve.tensor_tensor(y[:], y[:], fx[:], ALU.add))
                ch.need(a)
                a = normalise(fx, "fn_g", "fn_b", C_ASQ2, C_YC2, C_VAR2, 4)
                assert a == C_FO, a
                dve.wait_ge(s_pe_c, g * C_PE + C_PHG)
                a = ch.mark(dve.tensor_copy(hg[:], banks[7][:, 0:GT * NH].rearrange("p (t n) -> p t n", n=NH)))
                ch.need(a)
                softmax(hg[:], hg[:], st1[:, 0:GT], st2[:, 0:GT], C_HGS, C_AHG,
                        lambda v: v.unsqueeze(2).broadcast_to([P, GT, NH]))
                if g:
                    dve.wait_ge(s_c_out, 16 * g)
                else:
                    dve.wait_ge(s_h1_in, 32)
                a = ch.mark(dve.tensor_tensor(res[:].rearrange(heads, n=NH), fx[:].rearrange(heads, n=NH),
                                              wide(hg[:].rearrange("p t n -> p (t n)")), ALU.mult))
                ch.need(a)
                a = ch.mark(dve.tensor_tensor(res[:], res[:], h1c[:, tiles, :], ALU.add))
                assert a == C_DVE, a
                ch.need(a)

        @block.tensor
        def _(pe):
            pe.wait_ge(s_cst, 16 * N_CST)
            pe.wait_ge(s_init, 2 + BUFS + 2)
            pe.matmul(banks[7][0:D, 0:D], w("aq"), w("ak"), start=True, stop=True).then_inc(s_gm, 1)
            pe.wait_ge(s_x_in, 16)
            pe.wait_ge(s_w_in, 16)
            for i in range(PW):
                mm = pe.matmul(banks[6][0:D, 0:P], tokw_sb[:, i, :], xs[:, :, i:i + STEP * (NTOK - 1) + 1:STEP],
                               start=(i == 0), stop=(i == PW - 1))
            mm.then_inc(s_tokp, 1)
            pe.wait_ge(s_tokg, 1)
            pe.transpose(banks[6][:, P:P + D], tokT[:], c("ident", D)[:, 0:D]).then_inc(s_tokp, 1)

            def turn_tokens(which, need, count, done):
                pe.wait_ge(need, count)
                for b in range(GB):
                    mm = pe.transpose(banks[0][:, b * HS:(b + 1) * HS],
                                      xn[:, which, 2 * b:2 * b + 2, :].rearrange("t h d -> t (h d)"),
                                      c("ident", HS)[:, 0:HS])
                mm.then_inc(done, 1)

            def entry_a(g, p, first):
                if not first:
                    turn_tokens(0, s_a_xn, g + 1, s_a_tp)
                else:
                    turn_tokens(0, s_a_xn, 1, s_a_tp)
                pe.wait_ge(s_a_tc, 2 * (g + 1))
                pe.wait_ge(s_gmc, 1)
                for h in range(2):
                    pe.matmul(banks[h][:, 0:2 * S], gmat[:], xnT[p][:, h * 2 * S:(h + 1) * 2 * S], start=True, stop=True)
                for j in range(GH):
                    mm = pe.matmul(banks[2][0:HS, j * D:(j + 1) * D], xnT[p][:, j * HS:(j + 1) * HS], w("wv"),
                                   start=True, stop=True)
                mm.then_inc(s_a_zv, 1)

            def exit_a(g):
                turn_tokens(1, s_b_xn, g + 1, s_b_tp)
                pe.wait_ge(s_b_tc, 2 * (g + 1))
                for h in range(2):
                    mm = pe.matmul(banks[h][:, 0:2 * S], w("hl"), xn2T[:, h * 2 * S:(h + 1) * 2 * S], start=True, stop=True)
                mm.then_inc(s_b_sx, 1)

            def scores(g, p, b, first):
                if b == 0:
                    pe.wait_ge(s_a_zc, 2 * (g + 1))
                    pe.wait_ge(s_a_vc, g + 1)
                if not (first and b < 2):
                    pe.wait_ge(s_a_e, 2 * (g * GB + b - 1))
                for h in range(2):
                    mm = pe.matmul(banks[4 + b % 2][0:HS, h * S:(h + 1) * S], zT[p][:, b * S + h * HS:b * S + (h + 1) * HS],
                                   xnT[p][:, b * S:(b + 1) * S], start=True, stop=True)
                mm.then_inc(s_a_s, 1)

            def turn(g, p, b, first):
                pe.wait_ge(s_a_e, 2 * (g * GB + b + 1))
                if not (first and b < 2):
                    pe.wait_ge(s_a_ptc, g * GB + b - 1)
                for h in range(2):
                    for u in range(2):
                        mm = pe.transpose(banks[6 + b % 2][0:HS, u * S + h * HS:u * S + (h + 1) * HS],
                                          probs[b % 2][:, h, u * HS:(u + 1) * HS], c("ident", HS)[:, 0:HS])
                mm.then_inc(s_a_pt, 1)

            def weigh(g, p, b, first):
                pe.wait_ge(s_a_ptc, g * GB + b + 1)
                if b == 0 and not first:
                    pe.wait_ge(s_a_h1, g)
                for h in range(2):
                    for u in range(2):
                        mm = pe.matmul(banks[3][0:HS, (2 * b + h) * D:(2 * b + h + 1) * D],
                                       probsT[b % 2][:, u, h * HS:(h + 1) * HS], vs[p][:, 2 * b + u, :],
                                       start=(u == 0), stop=(u == 1))
                mm.then_inc(s_a_av, 1)

            def step(g, p, first=False, last=False, it=None, u=0):
                scores(g, p, 0, first)
                scores(g, p, 1, first)
                turn(g, p, 0, first)
                scores(g, p, 2, first)
                turn(g, p, 1, first)
                weigh(g, p, 0, first)
                if not first:
                    exit_a(g - 1)
                scores(g, p, 3, first)
                turn(g, p, 2, first)
                weigh(g, p, 1, first)
                turn(g, p, 3, first)
                weigh(g, p, 2, first)
                weigh(g, p, 3, first)
                if not last:
                    if not first:
                        pe.wait_ge(s_b_sxc, 2 * g)
                    entry_a(g + 1, 1 - p, False)
            entry_a(0, 0, True)
            steps_a(pe, step)
            pe.wait_ge(s_b_sxc, 2 * (GROUPS - 1))
            exit_a(GROUPS - 1)

            def project(b, p, count):
                pe.wait_ge(sx_in[p], 16 * count)
                for e in range(NE):
                    dst = banks[5][:, e * S:(e + 1) * S] if e < 3 else banks[6][:, 0:S]
                    pe.matmul(dst, c("wq")[:, e * P:(e + 1) * P], sxb[p][:], start=True, stop=True)
                pe.matmul(banks[6][:, S:2 * S], c("wk"), sxb[p][:], start=True, stop=True)
                pe.matmul(banks[6][:, 2 * S:2 * S + 2 * D], sxb[p][:, 0:MAIN], c("wvs"), start=True, stop=True)
                pe.matmul(banks[6][0:TAIL, 2 * S + 2 * D:2 * S + 3 * D], sxb[p][:, MAIN:S], c("wvs")[:, 0:D],
                          start=True, stop=True).then_inc(s_proj, 1)

            def pass1(b, p, n):
                if n == 0:
                    pe.wait_ge(s_pevA, b + 1)
                    pe.wait_ge(s_pevD, b + 1)
                pe.wait_ge(s_p1_free, b * NH + n + 1)
                bank = banks[n % 2]
                pe.matmul(bank[:, :], ident_bf, mask_rows, start=True, stop=False)
                for e in range(NE):
                    mm = pe.matmul(bank[:, e * P:(e + 1) * P], qs[p][:, e, :], kz[p][:, n, 0:MAIN],
                                   start=False, stop=(e == NE - 1))
                mm.then_inc(s_p1, 1)

            def pass2(b, p, n, count):
                if n == 0:
                    pe.wait_ge(m_in[p], 16 * NH * count)
                pe.wait_ge(s_ex, b * NH + n + 1)
                bank = banks[2 + n % 2]
                pe.matmul(bank[:, :], ident_bf, mask_cols, start=True, stop=False)
                pe.matmul(bank[:, :], kz[p][:, n, 0:MAIN], qs[p][:, :, :], start=False, stop=True).then_inc(s_p2, 1)

            def weigh_b(b, p, n):
                pe.wait_ge(s_ex, b * NH + n + 3)
                if n == 0:
                    pe.wait_ge(s_oc, b + 1)
                pe.matmul(banks[4][HP * n:HP * (n + 1), :], va[p][:, n, :], pT[:, n, :], start=True, stop=True).then_inc(s_av, 1)

            def tail_scores(b, p):
                for n in range(NH):
                    mm = pe.matmul(banks[7][HP * n:HP * n + NE * TAIL, 0:S], qt[p][:], kz[p][:, n, :],
                                   start=True, stop=True)
                mm.then_inc(s_st, 1)

            def tail_turn(b):
                pe.wait_ge(s_ptd, b + 1)
                pe.transpose(banks[7][:, S:S + P], pt_row[:, 0:MAIN], ident)
                pe.transpose(banks[7][0:TAIL, S + P:S + 2 * P], pt_row[:, MAIN:S], ident).then_inc(s_tt, 1)

            def tail_weigh(b, p):
                pe.wait_ge(s_ttc, b + 1)
                for n in range(NH):
                    dst = banks[7][HP * n:HP * (n + 1), S + 2 * P:S + 2 * P + NE * TAIL]
                    cols = slice(HP * n, HP * n + NE * TAIL)
                    pe.matmul(dst, va[p][:, n, :], ptT[:, cols], start=True, stop=False)
                    mm = pe.matmul(dst, va_t[p][:, n, :], ptT4[:, cols], start=False, stop=True)
                mm.then_inc(s_ut, 1)

            def turn_max(b):
                pe.wait_ge(s_p1_free, (b + 1) * NH + 2)
                pe.transpose(banks[7][0:NH * NE, 0:P], mx[:], ident).then_inc(s_mT, 1)

            def turn_out(b, src):
                for e in range(NE):
                    mm = pe.transpose(banks[4][:, e * P:(e + 1) * P], src[:, e], ident)
                mm.then_inc(s_tT, 1)

            def step_b(b, u, it):
                p, q, r = u % BUFS, (u - 1) % BUFS, (u + 1) % BUFS
                count = it + 1
                pass1(b, p, 0)
                pe.wait_ge(s_mTc, b)
                pe.wait_ge(s_utc, b)
                tail_scores(b, p)
                pass1(b, p, 1)
                pass2(b - 1, q, 0, count)
                pass2(b - 1, q, 1, count)
                pass1(b, p, 2)
                weigh_b(b - 1, q, 0)
                pe.wait_ge(s_stD, b + 1)
                tail_turn(b - 1)
                pass2(b - 1, q, 2, count)
                weigh_b(b - 1, q, 1)
                pass1(b, p, 3)
                tail_weigh(b - 1, q)
                pass2(b - 1, q, 3, count)
                weigh_b(b - 1, q, 2)
                pe.wait_ge(s_utc, b + 1)
                turn_max(b)
                weigh_b(b - 1, q, 3)
                if b is not B - 1:
                    project(b + 1, r, it + 1 if u % BUFS == 1 else it + 2)
                pe.wait_ge(s_uc, b)
                turn_out(b - 1, u_sb)

            project(0, 0, 1)
            for n in range(NH):
                pass1(0, 0, n)
            tail_scores(0, 0)
            pe.wait_ge(s_stD, 1)
            turn_max(0)
            project(1, 1, 1)
            steps_b(pe, step_b)
            q = (B - 1) % BUFS
            count = (B - 1) // BUFS + 1
            pass2(B - 1, q, 0, count)
            pass2(B - 1, q, 1, count)
            weigh_b(B - 1, q, 0)
            pe.wait_ge(s_mTc, B)
            tail_turn(B - 1)
            pass2(B - 1, q, 2, count)
            weigh_b(B - 1, q, 1)
            tail_weigh(B - 1, q)
            pass2(B - 1, q, 3, count)
            weigh_b(B - 1, q, 2)
            weigh_b(B - 1, q, 3)
            pe.wait_ge(s_uc, B)
            turn_out(B - 1, u_sb)
            pe.wait_ge(s_oc, B + 1)
            pe.wait_ge(s_utc, B + 1)
            turn_out(B, u_tail)
            pe.wait_ge(s_sxr, 1)
            pe.matmul(banks[6][:, 0:D], sx_rep[:, NH], c("wvs")[:, D:2 * D], start=True, stop=True)
            for n in range(NH):
                mm = pe.matmul(banks[6][:, D:2 * D], sx_rep[:, n], c("sel")[:, n * D:(n + 1) * D],
                               start=(n == 0), stop=(n == NH - 1))
            mm.then_inc(s_rs_mm, 1)

            def turn3(src):
                for q in range(3):
                    for t in range(4 * q, min(4 * q + 4, GT)):
                        mm = pe.transpose(banks[4 + q][0:D, (t % 4) * P:(t % 4 + 1) * P], src[:, t, :], ident)
                    mm.then_inc(s_pe_c, 1)

            for g in range(CGROUPS):
                dve_at, act_at = g * C_DVE, g * C_ACT
                pe.wait_ge(s_dve_c, dve_at + C_OM)
                for q in range((GT + 1) // 2):
                    if q >= 3:
                        pe.wait_ge(s_act_c, act_at + q - 2)
                    for t in range(2 * q, min(2 * q + 2, GT)):
                        for h in range(2):
                            mm = pe.transpose(banks[q % 3][:, ((t % 2) * 2 + h) * P:((t % 2) * 2 + h + 1) * P],
                                              om[:, t, h * P:(h + 1) * P], ident)
                    mm.then_inc(s_pe_c, 1)
                for t in range(GT):
                    if t % 2 == 0:
                        pe.wait_ge(s_act_c, act_at + t // 2 + 1)
                    for h in range(2):
                        mm = pe.matmul(banks[3][:, t * NE * NH:(t + 1) * NE * NH], omT[:, t, h, :],
                                       c("gw")[:, h * NE * NH:(h + 1) * NE * NH], start=(h == 0), stop=(h == 1))
                mm.then_inc(s_pe_c, 1)
                pe.wait_ge(s_dve_c, dve_at + C_FX)
                turn3(fx)
                pe.wait_ge(s_act_c, act_at + C_AFX)
                for q in range(3):
                    n = min(4, GT - 4 * q)
                    pe.matmul(banks[4 + q][0:D, 0:n * P], w("fc1"), fxT[:, q * 4 * P:(q * 4 + n) * P],
                              start=True, stop=True).then_inc(s_pe_c, 1)
                pe.wait_ge(s_dve_c, dve_at + C_HT)
                pe.wait_ge(s_init, 2 + BUFS + 3)
                for t in range(GT):
                    mm = pe.matmul(banks[t // 8][:, (t % 8) * D:(t % 8 + 1) * D], hT[:, t * P:(t + 1) * P], fc2_sb[:],
                                   start=True, stop=True)
                mm.then_inc(s_pe_c, 1)
                pe.wait_ge(s_dve_c, dve_at + C_FO)
                turn3(fx)
                pe.wait_ge(s_act_c, act_at + C_AFO)
                for t in range(GT):
                    mm = pe.matmul(banks[7][:, t * NH:(t + 1) * NH], fxT[:, t * P:(t + 1) * P], w("fg"), start=True, stop=True)
                mm.then_inc(s_pe_c, 1)


C_OM = 2
C_LGS = C_OM + 3
C_YC1 = C_LGS + 3 + 3 + 2
C_VAR1 = C_YC1 + 1
C_FX = C_VAR1 + 3
C_HT = C_FX + 3
C_YC2 = C_HT + 3 + 2
C_VAR2 = C_YC2 + 1
C_FO = C_VAR2 + 3
C_HGS = C_FO + 3
C_DVE = C_HGS + 3 + 2
C_AEXP = (GT + 1) // 2 + 1
C_ASQ1 = C_AEXP + 1
C_AFX = C_ASQ1 + 3
C_AH = C_AFX + 3
C_ASQ2 = C_AH + 1
C_AFO = C_ASQ2 + 3
C_AHG = C_AFO + 1
C_ACT = C_AHG
C_PLG = (GT + 1) // 2 + 1
C_PFX = C_PLG + 1
C_PFC1 = C_PFX + 3
C_PFC2 = C_PFC1 + 3
C_PFO = C_PFC2 + 1
C_PHG = C_PFO + 3
C_PE = C_PHG


_INS = ("x", "txt", "tokw", "c128", "c64", "fc2", "masks")


def laid_out(i):
    f = np.float32
    h = {n: np.asarray(v) for n, v in i.items()}
    c128 = np.zeros((P, N128), f)
    c64 = np.zeros((D, N64), f)

    def at(name, table=C128, dst=c128):
        a, b = table[name]
        return dst[:, a:b]
    at("ident")[:] = np.eye(P, dtype=f)
    kz = at("kz").reshape(P, NH, S)
    tmask = at("tmask")
    hl = at("hl", C64, c64)
    wq = at("wq").reshape(P, NE, P)
    wk, wvs = at("wk"), at("wvs")
    sel = at("sel").reshape(P, NH, D)
    gw = at("gw").reshape(P, 2, NE, NH)
    fc1 = at("fc1", C64, c64)
    fc2 = np.zeros((D + 1, D), f)
    for n in range(NH):
        r, k = slice(HP * n, HP * n + HD), slice(HD * n, HD * (n + 1))
        kz[HP * n + HD, n, :] = -1.0
        at("hl_b")[r, 0] = h["L0_ffn_hl_b"][n]
        hl[:, r] = h["L0_ffn_hl_w"][n].T
        for e in range(NE):
            wq[r, e, r] = h["L0_ffn_wq"][n, e].T
            for t in range(TAIL):
                tmask[HP * n + e * TAIL + t, MAIN + t + 1:] = BIG
            for e2 in range(NE):
                row = (e % 2) * D + n * HD
                gw[row:row + HD, e // 2, e2, n] = h["L0_ffn_gate_w"][n, e2, e * HD:(e + 1) * HD]
        wk[r, r] = h["L0_ffn_wk"][n].T
        wvs[r, k] = h["L0_ffn_wv"][n].T
        wvs[r, D + HD * n:D + HD * (n + 1)] = np.eye(HD, dtype=f)
        sel[r, n, k] = np.eye(HD, dtype=f)
        fc1[k, k] = h["L0_ffn_fc1_w"].T
        fc2[k, k] = h["L0_ffn_fc2_w"].T
        fc2[D, k] = h["L0_ffn_fc2_b"]
        at("fc1_b", C64, c64)[k, 0] = h["L0_ffn_fc1_b"]
        for name, src in (("ln_g", "ln_g"), ("ln_b", "ln_b"), ("fn_g", "fnorm_g"), ("fn_b", "fnorm_b")):
            at(name)[:, k] = h["L0_ffn_" + src]
    at("gate_b")[:] = h["L0_ffn_gate_b"].T.reshape(1, NE * NH)
    at("tok_b", C64, c64)[:, 0] = h["L0_tok_bias"]
    at("wv", C64, c64)[:] = h["L0_attn_Wv"].T
    at("aq", C64, c64)[:] = h["L0_attn_Wq"]
    at("ak", C64, c64)[:] = h["L0_attn_Wk"]
    at("fg", C64, c64)[:] = h["L0_ffn_fgate_w"].T
    masks = np.zeros((P, P + 2 * NE * P), f)
    masks[:, 0:P] = np.eye(P)
    for k in range(P):
        for e in range(NE):
            masks[k, P + e * P + k + 1:P + (e + 1) * P] = BIG
            masks[k, P + NE * P + e * P:P + NE * P + e * P + k] = BIG
    return {"x": h["x"], "txt": h["txt"], "tokw": h["L0_tok_weight"].reshape(PH, PW, D), "c128": c128, "c64": c64,
            "fc2": fc2, "masks": masks}


def kernel(**inputs):
    import concourse.bacc as bacc
    from concourse.bass_utils import run_bass_kernel_spmd as run

    nc = bacc.Bacc("TRN2", target_bir_lowering=False, num_devices=1)
    arrays, args = {}, []
    for name, a in laid_out(inputs).items():
        arrays[f"in_{name}"] = np.ascontiguousarray(a)
        args.append(nc.dram_tensor(f"in_{name}", a.shape, mybir.dt.from_np(a.dtype), kind="ExternalInput").ap())
    args.append(nc.dram_tensor("out_0", (B, S, D), F32, kind="ExternalOutput").ap())
    fusion_kernel(nc, *args)
    r = run(nc, [arrays], core_ids=[0])
    return r.results[0]["out_0"]
```

```python
import numpy as np
from contextlib import ExitStack

import concourse.bass as bass
from concourse import mybir

F32 = mybir.dt.float32
BF16 = mybir.dt.bfloat16
ALU = mybir.AluOpType
ACT = mybir.ActivationFunctionType
AX = mybir.AxisListType.X

B = 32
NTOK = 4
NTXT = 128
S = NTOK + NTXT
HS = S // 2
D = 64
NH, NE, HD = 4, 4, 16
HP = 32
PH, PW, STEP = 64, 25, 12
P = 128
MAIN = 128
TAIL = S - MAIN
TILES = B + 1
ARENA = 14080
BUFS = 3
BIG = -3e38

C128 = {}
C64 = {}


def _columns(table, *parts):
    at = 0
    for name, n in parts:
        table[name] = (at, at + n)
        at += n
    return at


N128 = _columns(C128, ("ident", P), ("kz", NH * S), ("tmask", S), ("hl_b", 1), ("wq", NE * P), ("wk", P),
                ("wvs", 2 * D), ("sel", NH * D), ("gw", 2 * NH * NE), ("gate_b", NH * NE), ("ln_g", D),
                ("ln_b", D), ("fn_g", D), ("fn_b", D))
N64 = _columns(C64, ("wv", D), ("aq", D), ("ak", D), ("hl", P), ("fc1", P), ("fg", NH), ("fc1_b", 1), ("tok_b", 1))

GB = 4
GROUPS = B // GB
GH = 2 * GB
GT = 3
GT_END = 6
CGROUPS = (TILES - GT_END) // GT

V_ORDER = ("nz om lg gmax gsub gsum ginv gs mix sum y s1 yc1 var1 yn1 nzf nzT hT z y2 s2 yc2 var2 yn2 "
           "hg hmax hsub hsum hinv hgs r1 res").split()
A_ORDER = "omT gexp sq1 fxT h sq2 foT hexp".split()
T_ORDER = "omT lg fxT h fc2 foT hg".split()
G_ORDER = "eps1 rs1 gain1 fx eps2 rs2 gain2 fo".split()


class Marks:

    def __init__(self, order):
        self.order = order

    def at(self, g, name):
        return g * len(self.order) + (self.order.index(name) + 1)


V, A, T, G = Marks(V_ORDER), Marks(A_ORDER), Marks(T_ORDER), Marks(G_ORDER)

DVE_A = 4
DVE_A_END = 3


class Chain:

    def __init__(self, eng, sem, base=0):
        self.eng, self.sem, self.base, self.n = eng, sem, base, 0

    def mark(self, ins):
        ins.then_inc(self.sem, 1)
        self.n += 1
        return self.n

    def need(self, n):
        self.eng.wait_ge(self.sem, self.base + n)


def fusion_kernel(nc, x, txt, tokw, c128, c64, fc2, masks, out, dbg=None):
    ctx = ExitStack()
    with ctx:
        def sb(name, shape, dt=F32):
            return ctx.enter_context(nc.sbuf_tensor(name, shape, dt))

        def sem(name):
            return ctx.enter_context(nc.semaphore(name))

        arena = sb("arena", [P, ARENA])

        class Carve:

            def __init__(self):
                self.at = 0

            def take(self, rows, *shape):
                n = int(np.prod(shape))
                a = arena[0:rows, self.at:self.at + n]
                self.at += n
                assert self.at <= ARENA
                names = "abc"[:len(shape)]
                if len(shape) == 1:
                    return a
                return a.rearrange("p (%s) -> p %s" % (" ".join(names), " ".join(names)), **dict(zip(names[1:], shape[1:])))

        k128 = sb("k128", [P, N128])
        k64 = sb("k64", [D, N64])
        fc2_sb = sb("fc2_sb", [D + 1, D])
        masks_sb = sb("masks_sb", [P, P + 2 * NE * P], BF16)

        def c(name, rows=P):
            a, b = C128[name]
            return k128[0:rows, a:b]

        def w(name):
            a, b = C64[name]
            return k64[:, a:b]

        ident = c("ident")
        ident_bf = masks_sb[:, 0:P]
        mask_rows = masks_sb[:, P:P + NE * P]
        mask_cols = masks_sb[:, P + NE * P:P + 2 * NE * P]
        gmat = sb("gmat", [D, P])
        half_neg = sb("half_neg", [P, GT_END * NH])
        eps_ln = sb("eps_ln", [HS, GH])
        eps_hd = sb("eps_hd", [P, GT_END * NH])

        early = Carve()
        xs = early.take(PH, B, D)
        tokw_sb = early.take(PH, PW, D)
        tokT = sb("tokT", [D, P])
        tok = sb("tok", [P, D])
        h0 = early.take(HS, B, 2, D)

        masks_f = early.take(P, P + 2 * NE * P)

        nsum = sb("nsum", [HS, 2, GH])
        xc = early.take(HS, 2, GH, D)
        sq = early.take(HS, 2, GH, D)
        var = sb("var", [HS, 2, GH])
        vare = sb("vare", [HS, 2, GH])
        rstd = sb("rstd", [HS, 2, GH])
        xn = early.take(HS, 2, GH, D)
        xnT = [early.take(D, GB * S) for i in range(2)]
        zT = [early.take(D, GB * S) for i in range(2)]
        vs = [sb(f"vs{i}", [HS, GH, D]) for i in range(2)]
        nmax = sb("nmax", [HS, GH])
        rsum = sb("rsum", [HS, GH])
        rinv = sb("rinv", [HS, GH])
        probs = [sb(f"probs{i}", [HS, 2, S]) for i in range(2)]
        probsT = [sb(f"probsT{i}", [HS, 2, S]) for i in range(2)]
        attn = sb("attn", [HS, GH, D])
        h1 = [sb(f"h1_{i}", [HS, GH, D]) for i in range(2)]
        xn2T = sb("xn2T", [D, GB * S])[:]
        sxT = sb("sxT", [P, B * S])
        h1_dram = nc.dram_tensor("h1_dram", (B, S, D), F32, kind="Internal").ap()

        sxb = [sb(f"sxb{i}", [P, S]) for i in range(BUFS)]
        qs = [sb(f"qs{i}", [P, NE, MAIN]) for i in range(BUFS)]
        qt = [sb(f"qt{i}", [P, NE * TAIL]) for i in range(BUFS)]
        kz = [sb(f"kz{i}", [P, NH, S]) for i in range(BUFS)]
        va = [sb(f"va{i}", [P, NH, HP]) for i in range(BUFS)]
        va_t = [sb(f"va_t{i}", [TAIL, NH, HP]) for i in range(BUFS)]
        mx = sb("mx", [P, NH * NE])
        mxT = sb("mxT", [NH * NE, P])
        st_m = sb("st_m", [P, S])
        nmt = sb("nmt", [P, 1])
        pt_row = sb("pt_row", [P, S])
        ptT = sb("ptT", [P, P])
        ptT4 = sb("ptT4", [TAIL, P])
        pT = sb("pT", [P, NH, NE * P])
        u_sb = sb("u_sb", [P, NE, P])
        u_tail = sb("u_tail", [P, NE, B, TAIL])
        rden = sb("rden", [P, NE * NH])
        sx_rep = sb("sx_rep", [P, NH + 1, B, TAIL])
        o_all = sb("o_all", [P, TILES, NE * D])
        sx_tok = sb("sx_tok", [P, TILES, D])
        resid = sb("resid", [P, TILES, D])

        late = Carve()
        h1c = sb("h1c", [P, TILES, D])
        nz = late.take(P, GT_END, D)
        om = late.take(P, GT_END, NE * D)
        omT = late.take(P, GT_END, 2, P)
        lg = sb("lg", [P, GT_END, NE * NH])
        lgm = sb("lgm", [P, GT_END, NH])
        y = late.take(P, GT_END, D)
        ysq = late.take(P, GT_END, D)
        yn = late.take(P, GT_END, D)
        fx = late.take(P, GT_END, D)
        nzf = late.take(P, GT_END, D)
        st1 = sb("st1", [P, GT_END * NH])
        st2 = sb("st2", [P, GT_END * NH])
        st3 = sb("st3", [P, GT_END * NH])
        fxT = late.take(D, GT_END * P)
        nzT = late.take(D, GT_END * P)
        hT = late.take(D + 1, GT_END * P)
        hg = sb("hg", [P, GT_END, NH])
        res = late.take(P, GT_END, D)

        banks = [ctx.enter_context(nc.psum_tensor(f"bank{i}", [P, 512], F32)) for i in range(8)]

        s_cst = sem("s_cst")
        s_x_in = sem("s_x_in")
        s_w_in = sem("s_w_in")
        s_h0_in = sem("s_h0_in")
        s_init = sem("s_init")
        s_gm = sem("s_gm")
        s_gmc = sem("s_gmc")
        s_tokp = sem("s_tokp")
        s_tokg = sem("s_tokg")
        s_tok_out = sem("s_tok_out")
        s_a_nm = sem("s_a_nm")
        s_a_sq = sem("s_a_sq")
        s_a_var = sem("s_a_var")
        s_a_rs = sem("s_a_rs")
        s_a_xn = sem("s_a_xn")
        s_a_tp = sem("s_a_tp")
        s_a_tc = sem("s_a_tc")
        s_a_zv = sem("s_a_zv")
        s_a_zc = sem("s_a_zc")
        s_a_vc = sem("s_a_vc")
        s_a_s = sem("s_a_s")
        s_a_mx = sem("s_a_mx")
        s_a_e = sem("s_a_e")
        s_a_pt = sem("s_a_pt")
        s_a_ptc = sem("s_a_ptc")
        s_a_av = sem("s_a_av")
        s_a_h1 = sem("s_a_h1")
        s_b_nm = sem("s_b_nm")
        s_b_sq = sem("s_b_sq")
        s_b_var = sem("s_b_var")
        s_b_rs = sem("s_b_rs")
        s_b_xn = sem("s_b_xn")
        s_b_tp = sem("s_b_tp")
        s_b_tc = sem("s_b_tc")
        s_b_sx = sem("s_b_sx")
        s_b_sxc = sem("s_b_sxc")
        s_dve_a_end = sem("s_dve_a_end")
        s_dve_a = sem("s_dve_a")
        s_pool_a = sem("s_pool_a")
        s_p1 = sem("s_p1")
        s_p1_free = sem("s_p1_free")
        s_p2 = sem("s_p2")
        s_ex = sem("s_ex")
        s_proj = sem("s_proj")
        s_pevA = sem("s_pevA")
        s_pevD = sem("s_pevD")
        s_mT = sem("s_mT")
        s_mTc = sem("s_mTc")
        s_st = sem("s_st")
        s_stD = sem("s_stD")
        s_nmtd = sem("s_nmtd")
        s_ptd = sem("s_ptd")
        s_tt = sem("s_tt")
        s_ttc = sem("s_ttc")
        s_ut = sem("s_ut")
        s_utc = sem("s_utc")
        s_av = sem("s_av")
        s_uc = sem("s_uc")
        s_tT = sem("s_tT")
        s_rd = sem("s_rd")
        s_oc = sem("s_oc")
        s_sxr = sem("s_sxr")
        s_rs_mm = sem("s_rs_mm")
        s_resd = sem("s_resd")
        s_h1_in = sem("s_h1_in")
        s_dve_c = sem("s_dve_c")
        s_act_c = sem("s_act_c")
        s_pe_c = sem("s_pe_c")
        s_pool_c = sem("s_pool_c")
        s_c_out = sem("s_c_out")
        m_in = [sem(f"s_m_in{i}") for i in range(BUFS)]
        sx_in = [sem(f"s_sx_in{i}") for i in range(BUFS)]
        a_out = [sem(f"s_a_out{i}") for i in range(2)]

        block = ctx.enter_context(nc.Block())
        N_CST = 4
        NB_TXT = 4
        PB = B // NB_TXT

        def steps_a(eng, step, last_too=True):
            step(0, 0, first=True)
            with eng.Fori(0, (GROUPS - 2) // 2) as it:
                for u in range(2):
                    step(it * 2 + (u + 1), (u + 1) % 2, it=it, u=u)
            step(GROUPS - 1, (GROUPS - 1) % 2, last=True)

        def steps_b(eng, step):
            for u in range(BUFS):
                step(u + 1, u + 1, 0, None)
            with eng.Fori(1, (B - 2) // BUFS) as it:
                for u in range(BUFS):
                    step(it * BUFS + (u + 1), u + 1, it, it - 1)
            step(B - 1, (B - 1) % BUFS + BUFS, (B - 2) // BUFS, None)

        class Group:

            def __init__(self, g, first, n, ends=False):
                self.g, self.first, self.n = g, first, n
                self.om_banks = [banks[5], banks[6], banks[0]]
                self.lg_bank = banks[3] if ends else banks[5]
                self.turn_banks = [banks[5], banks[1]]
                self.h_banks = [banks[6], banks[2]]

            def rows(self, a):
                return a[:, bass.ds(self.first, self.n), :]

        last_group = Group(CGROUPS, CGROUPS * GT, GT_END, ends=True)

        @block.sync
        def _(sp):
            sp.dma_start(xs[:], x.rearrange("b c r w -> r (b c) w")).then_inc(s_x_in, 16)
            sp.dma_start(k64[:], c64).then_inc(s_cst, 16)
            sp.dma_start(k128[:], c128).then_inc(s_cst, 16)
            for q in range(NB_TXT):
                rows = slice(q * PB, (q + 1) * PB)
                sp.dma_start(h0[NTOK:HS, rows, 0, :], txt[rows, 0:HS - NTOK, :].rearrange("b t d -> t b d")).then_inc(s_h0_in, 16)
                sp.dma_start(h0[:, rows, 1, :], txt[rows, HS - NTOK:NTXT, :].rearrange("b t d -> t b d")).then_inc(s_h0_in, 16)
            sp.wait_ge(s_tokg, 2)
            for n in range(NTOK):
                sp.dma_start(h0[n:n + 1, :, 0, :], tok[n:P:NTOK, :]).then_inc(s_tok_out, 16)

            def step(g, p, first=False, last=False, it=None, u=0):
                sp.wait_ge(s_a_h1, g + 1)
                dst = h1_dram[bass.ds(g * GB, GB), :, :].rearrange("b (h t) d -> t b h d", t=HS)
                src = h1[p][:].rearrange("t (b h) d -> t b h d", h=2)
                sp.dma_start(dst, src).then_inc(a_out[p], 16)
            steps_a(sp, step)

            def load_sx(b, p, first=False):
                if not first:
                    sp.wait_ge(s_mT, b - 1)
                sp.dma_start(sxb[p][:], sxT[:, bass.ds(b * S, S)]).then_inc(sx_in[p], 16)

            def send_m(b, p):
                sp.wait_ge(s_mTc, b + 1)
                for n in range(NH):
                    sp.dma_start(qs[p][HP * n + HD:HP * n + HD + 1, :, :],
                                 mxT[NE * n:NE * n + NE, :]).then_inc(m_in[p], 16)
            sp.wait_ge(s_b_sxc, 2 * GROUPS)
            load_sx(0, 0, True)
            load_sx(1, 1, True)
            send_m(0, 0)

            for q in range(2):
                sp.wait_ge(a_out[q], 16 * (GROUPS // 2 + 1))
            sp.dma_start(h1c[:, 0:B, :], h1_dram[:, 0:MAIN, :].rearrange("b t d -> t b d")).then_inc(s_h1_in, 16)
            sp.dma_start(h1c[:, B, :], h1_dram[:, MAIN:S, :]).then_inc(s_h1_in, 16)

            def step_b(b, u, it, g):
                if b is not B - 1:
                    load_sx(b + 1, (u + 1) % BUFS)
                send_m(b, u % BUFS)
                if g is not None and u == BUFS:
                    sp.wait_ge(s_dve_c, V.at(g, "res"))
                    sp.dma_start(out[bass.ds(g * GT, GT), 0:MAIN, :].rearrange("b t d -> t b d"), res[:, 0:GT, :]).then_inc(s_c_out, 16)
            steps_b(sp, step_b)
            n = GT_END - 1
            sp.wait_ge(s_dve_c, V.at(CGROUPS, "res"))
            sp.dma_start(out[B - n:B, 0:MAIN, :].rearrange("b t d -> t b d"), res[:, 0:n, :]).then_inc(s_c_out, 16)
            sp.dma_start(out[:, MAIN:S, :], res[:, n, :]).then_inc(s_c_out, 16)
            sp.wait_ge(s_c_out, 16 * (CGROUPS + 3))

        @block.gpsimd
        def _(pool):
            pool.dma_start(tokw_sb[:], tokw).then_inc(s_w_in, 16)
            pool.memset(eps_ln[:], 1e-5)
            pool.memset(eps_hd[:], 1e-8)
            pool.memset(half_neg[:], -0.5).then_inc(s_init, 1)
            pool.wait_ge(s_init, 1)

            def rs(which, n_sem, base):
                pool.tensor_tensor(vare[:, which, :], var[:, which, :], eps_ln[:], ALU.add).then_inc(s_pool_a, 1)
                pool.wait_ge(s_pool_a, base)
                pool.tensor_tensor(rstd[:, which, :], vare[:, which, :], half_neg[0:HS, 0:GH], ALU.pow).then_inc(n_sem, 1)

            def step(g, p, first=False, last=False, it=None, u=0):
                if not first:
                    pool.wait_ge(s_b_var, g)
                    rs(1, s_b_rs, 2 * g + 1)
                if not last:
                    pool.wait_ge(s_a_var, g + 2)
                    rs(0, s_a_rs, 2 * g + 2)
            pool.wait_ge(s_a_var, 1)
            rs(0, s_a_rs, 1)
            steps_a(pool, step)
            pool.wait_ge(s_b_var, GROUPS)
            rs(1, s_b_rs, 2 * GROUPS)

            def finish_norm(c_, k, dst, gain, shift):
                g, n = c_.g, c_.n
                pool.wait_ge(s_dve_c, V.at(g, f"var{k}"))
                pool.tensor_tensor(st2[:, 0:n * NH], st2[:, 0:n * NH], eps_hd[:, 0:n * NH], ALU.add).then_inc(s_pool_c, 1)
                pool.wait_ge(s_pool_c, G.at(g, f"eps{k}"))
                pool.tensor_tensor(st3[:, 0:n * NH], st2[:, 0:n * NH], half_neg[:, 0:n * NH], ALU.pow).then_inc(s_pool_c, 1)
                pool.wait_ge(s_dve_c, V.at(g, f"yn{k}"))
                pool.tensor_tensor(yn[:, 0:n, :], yn[:, 0:n, :], c(gain).unsqueeze(1).broadcast_to([P, n, D]), ALU.mult).then_inc(s_pool_c, 1)
                pool.wait_ge(s_pool_c, G.at(g, f"gain{k}"))
                pool.tensor_tensor(dst[:, 0:n, :], yn[:, 0:n, :], c(shift).unsqueeze(1).broadcast_to([P, n, D]), ALU.add).then_inc(s_pool_c, 1)

            def both(c_):
                finish_norm(c_, 1, fx, "ln_g", "ln_b")
                finish_norm(c_, 2, fx, "fn_g", "fn_b")

            with pool.Fori(0, CGROUPS) as g:
                both(Group(g, None, GT))
            both(last_group)

        @block.scalar
        def _(act):
            act.dma_start(fc2_sb[:], fc2).then_inc(s_cst, 16)
            act.dma_start(masks_f, masks).then_inc(s_cst, 16)
            act.wait_ge(s_cst, 16 * N_CST)
            act.wait_ge(s_tokp, 1)
            act.activation(tokT[:], banks[6][0:D, 0:P], ACT.Gelu, bias=w("tok_b")).then_inc(s_tokg, 1)
            act.wait_ge(s_tokp, 2)
            act.activation(tok[:], banks[6][:, P:P + D], ACT.Copy).then_inc(s_tokg, 1)

            def square(which, need, count, done):
                act.wait_ge(need, count)
                act.activation(sq[:, which], xc[:, which], ACT.Square, scale=float(D) ** -0.5).then_inc(done, 1)

            def evac2(dst, need, count, done):
                act.wait_ge(need, count)
                for h in range(2):
                    act.activation(dst[:, h * 2 * S:(h + 1) * 2 * S], banks[h][0:D, 0:2 * S], ACT.Copy).then_inc(done, 1)

            def evac_turned(dst, need, count, done):
                act.wait_ge(need, count)
                for h in range(2):
                    act.activation(dst.rearrange("d (b h t) -> d b h t", h=2, t=HS)[:, :, h, :],
                                   banks[0][h * D:(h + 1) * D, 0:GB * HS].rearrange("d (b t) -> d b t", t=HS),
                                   ACT.Copy).then_inc(done, 1)

            def entry_a(g, p, first):
                square(0, s_a_nm, g + 1, s_a_sq)
                evac_turned(xnT[p], s_a_tp, g + 1, s_a_tc)
                evac2(zT[p], s_a_zv, g + 1, s_a_zc)
                act.activation(vs[p][:], banks[2][0:HS, 0:GH * D].rearrange("t (j d) -> t j d", d=D), ACT.Copy).then_inc(s_a_vc, 1)

            def exps(g, b):
                act.wait_ge(s_a_mx, g * GB + b + 1)
                if b >= 2:
                    act.wait_ge(s_a_pt, g * GB + b - 1)
                for h in range(2):
                    act.activation(probs[b % 2][:, h, :], banks[4 + b % 2][0:HS, h * S:(h + 1) * S], ACT.Exp,
                                   bias=nmax[:, 2 * b + h:2 * b + h + 1],
                                   accum_out=rsum[:, 2 * b + h:2 * b + h + 1]).then_inc(s_a_e, 1)

            def exit_a(g):
                square(1, s_b_nm, g + 1, s_b_sq)
                evac_turned(xn2T, s_b_tp, g + 1, s_b_tc)
                act.wait_ge(s_b_sx, g + 1)
                for h in range(2):
                    act.activation(sxT[:, bass.ds(g * (GB * S) + h * 2 * S, 2 * S)], banks[h][:, 0:2 * S], ACT.Identity,
                                   bias=c("hl_b")).then_inc(s_b_sxc, 1)

            def step(g, p, first=False, last=False, it=None, u=0):
                if not first:
                    act.wait_ge(s_a_h1, g)
                for b in range(GB):
                    exps(g, b)
                    if b == 1 and not first:
                        exit_a(g - 1)
                if not last:
                    entry_a(g + 1, 1 - p, False)
            entry_a(0, 0, True)
            steps_a(act, step)
            exit_a(GROUPS - 1)

            def evac_proj(b, p):
                act.wait_ge(s_proj, b + 1)
                q = banks[5][:, 0:3 * S].rearrange("p (e t) -> p e t", e=3)
                act.activation(qs[p][:, 0:3, :], q[:, :, 0:MAIN], ACT.Copy)
                act.activation(qt[p][:, 0:3 * TAIL].rearrange("p (e t) -> p e t", e=3), q[:, :, MAIN:S], ACT.Copy).then_inc(s_pevA, 1)

            def exp_tail(b):
                act.wait_ge(s_nmtd, b + 1)
                act.activation(pt_row[:], st_m[:], ACT.Exp, bias=nmt[:]).then_inc(s_ptd, 1)

            def copy_m(b):
                act.wait_ge(s_mT, b + 1)
                act.activation(mxT[:], banks[7][0:NH * NE, 0:P], ACT.Copy).then_inc(s_mTc, 1)

            def exp_main(b, n):
                act.wait_ge(s_p2, b * NH + n + 1)
                act.activation(pT[:, n, :], banks[2 + n % 2][:, :], ACT.Exp).then_inc(s_ex, 1)

            def evac_tail_probs(b):
                act.wait_ge(s_tt, b + 1)
                act.activation(ptT[:], banks[7][:, S:S + P], ACT.Copy)
                act.activation(ptT4[:], banks[7][0:TAIL, S + P:S + 2 * P], ACT.Copy).then_inc(s_ttc, 1)

            def evac_tail_out(b):
                act.wait_ge(s_ut, b + 1)
                act.activation(u_tail[:, :, bass.ds(b, 1), :],
                               banks[7][:, S + 2 * P:S + 2 * P + NE * TAIL].rearrange("p (e o t) -> p e o t", e=NE, o=1),
                               ACT.Copy).then_inc(s_utc, 1)

            def evac_out(b):
                act.wait_ge(s_av, (b + 1) * NH)
                act.activation(u_sb[:], banks[4][:, :].rearrange("p (e t) -> p e t", e=NE), ACT.Copy).then_inc(s_uc, 1)

            def c_om(c_):
                act.wait_ge(s_pe_c, T.at(c_.g, "omT"))
                for q in range((c_.n + 1) // 2):
                    m = min(2, c_.n - 2 * q)
                    a = act.activation(omT[:, 2 * q:2 * q + m, :, :],
                                       c_.om_banks[q][:, 0:m * 2 * P].rearrange("p (t h s) -> p t h s", t=m, h=2), ACT.Copy)
                a.then_inc(s_act_c, 1)

            def c_exp(c_, buf, need):
                act.wait_ge(s_dve_c, V.at(c_.g, need))
                act.activation(buf[:, 0:c_.n, :], buf[:, 0:c_.n, :], ACT.Exp).then_inc(s_act_c, 1)

            def c_square(c_, need):
                act.wait_ge(s_dve_c, V.at(c_.g, need))
                act.activation(ysq[:, 0:c_.n, :], y[:, 0:c_.n, :], ACT.Square, scale=float(HD) ** -0.5).then_inc(s_act_c, 1)

            def c_evac(c_, dst, from_banks, name, relu=False):
                act.wait_ge(s_pe_c, T.at(c_.g, name))
                for q in range((c_.n + 3) // 4):
                    cols = min(4, c_.n - 4 * q) * P
                    src, to = from_banks[q][0:D, 0:cols], dst[0:D, q * 4 * P:q * 4 * P + cols]
                    if relu:
                        a = act.activation(to, src, ACT.Relu, bias=w("fc1_b"))
                    else:
                        a = act.activation(to, src, ACT.Copy)
                a.then_inc(s_act_c, 1)

            def step_b(b, u, it, g):
                c_ = None if g is None else Group(g, g * GT, GT)
                if c_ and u == 1:
                    c_om(c_)
                exp_main(b - 1, 0)
                if c_ and u == 2:
                    c_square(c_, "yc1")
                if c_ and u == 3:
                    c_square(c_, "yc2")
                exp_main(b - 1, 1)
                evac_tail_probs(b - 1)
                if c_ and u == 2:
                    c_evac(c_, fxT, c_.turn_banks, "fxT")
                if c_ and u == 3:
                    c_evac(c_, fxT, c_.turn_banks, "foT")
                exp_main(b - 1, 2)
                if c_ and u == 1:
                    c_exp(c_, lg, "gsub")
                if c_ and u == 2:
                    c_evac(c_, hT, c_.h_banks, "h", relu=True)
                evac_tail_out(b - 1)
                exp_main(b - 1, 3)
                copy_m(b)
                evac_out(b - 1)
                if b is not B - 1:
                    evac_proj(b + 1, (u + 1) % BUFS)
                exp_tail(b)
                if c_ and u == 3:
                    c_exp(c_, hg, "hsub")

            evac_proj(0, 0)
            evac_proj(1, 1)
            copy_m(0)
            exp_tail(0)
            steps_b(act, step_b)
            exp_main(B - 1, 0)
            exp_main(B - 1, 1)
            evac_tail_probs(B - 1)
            exp_main(B - 1, 2)
            evac_tail_out(B - 1)
            exp_main(B - 1, 3)
            evac_out(B - 1)

            c_om(last_group)
            c_exp(last_group, lg, "gsub")
            c_square(last_group, "yc1")
            c_evac(last_group, fxT, last_group.turn_banks, "fxT")
            c_evac(last_group, hT, last_group.h_banks, "h", relu=True)
            c_square(last_group, "yc2")
            c_evac(last_group, fxT, last_group.turn_banks, "foT")
            c_exp(last_group, hg, "hsub")

        @block.vector
        def _(dve):
            dve.memset(h1[0][:], 0.0).then_inc(a_out[0], 16)
            dve.memset(h1[1][:], 0.0).then_inc(a_out[1], 16)
            dve.memset(mx[:], 0.0).then_inc(s_p1_free, 2)
            dve.memset(st_m[:], 0.0).then_inc(s_ex, 2)
            dve.memset(ptT4[:], 0.0).then_inc(s_utc, 1)
            dve.memset(rden[:], 0.0).then_inc(s_oc, 1)
            for p in range(BUFS):
                dve.memset(va[p][:], 1.0)
                dve.memset(va_t[p][:], 1.0)
            dve.memset(banks[7][:], 0.0).then_inc(s_init, 1)
            dve.wait_ge(s_init, 2)
            dve.wait_ge(s_cst, 16 * N_CST)
            for p in range(BUFS):
                dve.tensor_copy(kz[p][:], c("kz").rearrange("p (n t) -> p n t", n=NH)).then_inc(s_init, 1)
            dve.tensor_copy(masks_sb[:], masks_f).then_inc(s_init, 1)
            dve.tensor_scalar(c("wq"), c("wq"), float(HD) ** 0.5, None, ALU.mult).then_inc(s_init, 1)
            dve.memset(gmat[:, D:P], 0.0)
            dve.wait_ge(s_gm, 1)
            dve.tensor_copy(gmat[:, 0:D], banks[7][0:D, 0:D]).then_inc(s_gmc, 1)

            def center(which, src, ch, done):
                a = ch.mark(dve.tensor_reduce(nsum[:, which, :], src, axis=AX, op=ALU.add, negate=True))
                ch.need(a)
                dve.scalar_tensor_tensor(xc[:, which], nsum[:, which, :].unsqueeze(2).broadcast_to([HS, GH, D]),
                                         1.0 / D, src, ALU.mult, ALU.add).then_inc(done, 1)

            def variance(which, need, count, done):
                dve.wait_ge(need, count)
                dve.tensor_reduce(var[:, which, :], sq[:, which], axis=AX, op=ALU.add).then_inc(done, 1)

            def scale(which, need, count, done):
                dve.wait_ge(need, count)
                dve.tensor_tensor(xn[:, which], xc[:, which], rstd[:, which, :].unsqueeze(2).broadcast_to([HS, GH, D]),
                                  ALU.mult).then_inc(done, 1)

            def h0_of(g):
                return h0[:, bass.ds(g * GB, GB), :, :].rearrange("t b h d -> t (b h) d")

            def maxima(g, b):
                dve.wait_ge(s_a_s, g * GB + b + 1)
                dve.tensor_reduce(nmax[:, 2 * b:2 * b + 2], banks[4 + b % 2][0:HS, 0:2 * S].rearrange("t (h u) -> t h u", h=2),
                                  axis=AX, op=ALU.max, negate=True).then_inc(s_a_mx, 1)

            def evac_pt(g, b, first):
                dve.wait_ge(s_a_pt, g * GB + b + 1)
                if not (first and b < 2):
                    dve.wait_ge(s_a_av, g * GB + b - 1)
                dve.tensor_copy(probsT[b % 2][:], banks[6 + b % 2][0:HS, 0:2 * S].rearrange("t (h u) -> t h u", h=2)).then_inc(s_a_ptc, 1)

            def step(g, p, first=False, last=False, it=None, u=0):
                if first:
                    ch = Chain(dve, s_dve_a_end, 1)
                elif last:
                    ch = Chain(dve, s_dve_a_end, 1 + DVE_A_END)
                else:
                    ch = Chain(dve, s_dve_a, (it * 2 + u) * DVE_A)
                if not first:
                    dve.wait_ge(s_a_h1, g)
                    center(1, h1[1 - p][:], ch, s_b_nm)
                maxima(g, 0)
                maxima(g, 1)
                if not first:
                    variance(1, s_b_sq, g, s_b_var)
                if not last:
                    center(0, h0_of(g + 1), ch, s_a_nm)
                evac_pt(g, 0, first)
                maxima(g, 2)
                if not first:
                    scale(1, s_b_rs, g, s_b_xn)
                evac_pt(g, 1, first)
                maxima(g, 3)
                evac_pt(g, 2, first)
                evac_pt(g, 3, first)
                if not last:
                    variance(0, s_a_sq, g + 2, s_a_var)
                dve.wait_ge(s_a_e, (g + 1) * GH)
                inverted = ch.mark(dve.reciprocal(rinv[:], rsum[:]))
                if not last:
                    scale(0, s_a_rs, g + 2, s_a_xn)
                ch.need(inverted)
                dve.wait_ge(s_a_av, (g + 1) * GB)
                scaled = ch.mark(dve.scalar_tensor_tensor(
                    attn[:], banks[3][0:HS, 0:GH * D].rearrange("t (j d) -> t j d", d=D), float(D) ** -0.5,
                    rinv[:].unsqueeze(2).broadcast_to([HS, GH, D]), ALU.mult, ALU.mult))
                ch.need(scaled)
                if last:
                    dve.wait_ge(a_out[p], 16 * ((GROUPS - 1) // 2 + 1))
                elif not first:
                    dve.wait_ge(a_out[p], (it + (u + 1)) * 16)
                dve.tensor_tensor(h1[p][:], attn[:], h0_of(g), ALU.add).then_inc(s_a_h1, 1)
                assert ch.n == (DVE_A_END if first or last else DVE_A)

            dve.wait_ge(s_h0_in, 16 * 2 * NB_TXT)
            dve.wait_ge(s_tok_out, 16 * NTOK)
            center(0, h0_of(0), Chain(dve, s_dve_a_end), s_a_nm)
            variance(0, s_a_sq, 1, s_a_var)
            scale(0, s_a_rs, 1, s_a_xn)
            steps_a(dve, step)
            dve.wait_ge(s_a_h1, GROUPS)
            center(1, h1[(GROUPS - 1) % 2][:], Chain(dve, s_dve_a_end, 1 + 2 * DVE_A_END), s_b_nm)
            variance(1, s_b_sq, GROUPS, s_b_var)
            scale(1, s_b_rs, GROUPS, s_b_xn)


            def evac_proj(b, p):
                dve.wait_ge(s_proj, b + 1)
                dve.tensor_copy(qs[p][:, 3, :], banks[6][:, 0:MAIN])
                dve.tensor_copy(qt[p][:, 3 * TAIL:], banks[6][:, MAIN:S])
                for n in range(NH):
                    rows = slice(HP * n, HP * n + HD)
                    dve.tensor_copy(kz[p][rows, n, :], banks[6][rows, S:2 * S])
                dve.tensor_copy(va[p][:, :, 0:HD], banks[6][:, 2 * S:2 * S + D].rearrange("t (n d) -> t n d", n=NH))
                dve.tensor_copy(va_t[p][:, :, 0:HD], banks[6][0:TAIL, 2 * S + 2 * D:2 * S + 3 * D].rearrange("t (n d) -> t n d", n=NH))
                dve.tensor_copy(sx_tok[:, bass.ds(b, 1), :], banks[6][:, 2 * S + D:2 * S + 2 * D].unsqueeze(1)).then_inc(s_pevD, 1)

            def row_max(b, n):
                dve.wait_ge(s_p1, b * NH + n + 1)
                dve.tensor_reduce(mx[:, n * NE:(n + 1) * NE], banks[n % 2][:, :].rearrange("p (e t) -> p e t", e=NE),
                                  axis=AX, op=ALU.max).then_inc(s_p1_free, 1)

            def tail_max(b):
                dve.wait_ge(s_st, b + 1)
                dve.wait_ge(s_ptd, b)
                dve.tensor_tensor(st_m[:], banks[7][:, 0:S], c("tmask"), ALU.add).then_inc(s_stD, 1)
                dve.wait_ge(s_stD, b + 1)
                dve.tensor_reduce(nmt[:], st_m[:], axis=AX, op=ALU.max, negate=True).then_inc(s_nmtd, 1)

            def norm(b):
                t = banks[4][:, :].rearrange("p (a h) -> p a h", h=HP)
                dve.wait_ge(s_tT, b + 1)
                dve.reciprocal(rden[:].unsqueeze(2), t[:, :, HD:HD + 1]).then_inc(s_rd, 1)
                dve.wait_ge(s_rd, b + 1)
                dve.tensor_tensor(o_all[:, bass.ds(b, 1), :].rearrange("p o (a d) -> p (o a) d", d=HD), t[:, :, 0:HD],
                                  rden[:].unsqueeze(2).broadcast_to([P, NE * NH, HD]), ALU.mult).then_inc(s_oc, 1)

            heads = "p t (n d) -> p (t n) d"

            def need(g, name):
                dve.wait_ge(s_dve_c, V.at(g, name))

            def softmax_sub(c_, buf, view, tiny, spread, names):
                dve.tensor_reduce(tiny, view, axis=AX, op=ALU.max).then_inc(s_dve_c, 1)
                need(c_.g, names[0])
                dve.tensor_tensor(buf, buf, spread(tiny), ALU.subtract).then_inc(s_dve_c, 1)

            def softmax_div(c_, buf, view, tiny, inv, spread, names, exp_name):
                dve.wait_ge(s_act_c, A.at(c_.g, exp_name))
                dve.tensor_reduce(tiny, view, axis=AX, op=ALU.add).then_inc(s_dve_c, 1)
                need(c_.g, names[0])
                dve.reciprocal(inv, tiny).then_inc(s_dve_c, 1)
                need(c_.g, names[1])
                dve.tensor_tensor(buf, buf, spread(inv), ALU.mult).then_inc(s_dve_c, 1)

            def gates(c_):
                n = c_.n
                return (lg[:, 0:n, :].rearrange("p t (e n) -> p t e n", e=NE), lg[:, 0:n, :].rearrange("p t (e n) -> p t n e", e=NE),
                        lambda v: v.unsqueeze(2).broadcast_to([P, n, NE, NH]))

            def c_mask(c_):
                n, g = c_.n, c_.g
                dve.tensor_scalar(nz[:, 0:n, :], c_.rows(sx_tok), 0.0, None, ALU.not_equal).then_inc(s_dve_c, 1)
                need(g, "nz")
                dve.tensor_tensor(om[:, 0:n, :].rearrange("p t (e d) -> p t e d", e=NE),
                                  c_.rows(o_all).rearrange("p t (e d) -> p t e d", e=NE),
                                  nz[:, 0:n, :].unsqueeze(2).broadcast_to([P, n, NE, D]), ALU.mult).then_inc(s_dve_c, 1)

            def c_gates1(c_):
                n, g = c_.n, c_.g
                buf, view, spread = gates(c_)
                dve.wait_ge(s_pe_c, T.at(g, "lg"))
                dve.tensor_tensor(lg[:, 0:n, :], c_.lg_bank[:, 0:n * NE * NH].rearrange("p (t a) -> p t a", t=n),
                                  c("gate_b").unsqueeze(1).broadcast_to([P, n, NE * NH]), ALU.add).then_inc(s_dve_c, 1)
                need(g, "lg")
                softmax_sub(c_, buf, view, lgm[:, 0:n, :], spread, ("gmax",))

            def c_gates2(c_):
                n = c_.n
                buf, view, spread = gates(c_)
                softmax_div(c_, buf, view, lgm[:, 0:n, :], st1[:, 0:n * NH].rearrange("p (t n) -> p t n", n=NH), spread,
                            ("gsum", "ginv"), "gexp")

            def c_mix(c_):
                n, g = c_.n, c_.g
                o = om[:, 0:n, :].rearrange("p t (a d) -> p (t a) d", d=HD)
                need(g, "gs")
                dve.tensor_tensor(o, o, lg[:, 0:n, :].rearrange("p t a -> p (t a)").unsqueeze(2).broadcast_to([P, n * NE * NH, HD]),
                                  ALU.mult).then_inc(s_dve_c, 1)
                need(g, "mix")
                dve.tensor_reduce(y[:, 0:n, :], om[:, 0:n, :].rearrange("p t (e d) -> p t d e", e=NE), axis=AX, op=ALU.add).then_inc(s_dve_c, 1)
                need(g, "sum")
                dve.tensor_tensor(y[:, 0:n, :], y[:, 0:n, :], c_.rows(resid), ALU.add).then_inc(s_dve_c, 1)

            def c_center(c_, k, before):
                n, g = c_.n, c_.g
                yh = y[:, 0:n, :].rearrange(heads, n=NH)
                need(g, before)
                dve.tensor_reduce(st1[:, 0:n * NH], yh, axis=AX, op=ALU.add, negate=True).then_inc(s_dve_c, 1)
                need(g, f"s{k}")
                dve.scalar_tensor_tensor(yh, st1[:, 0:n * NH].unsqueeze(2).broadcast_to([P, n * NH, HD]), 1.0 / HD, yh,
                                         ALU.mult, ALU.add).then_inc(s_dve_c, 1)

            def c_var(c_, k):
                n, g = c_.n, c_.g
                dve.wait_ge(s_act_c, A.at(g, f"sq{k}"))
                dve.tensor_reduce(st2[:, 0:n * NH], ysq[:, 0:n, :].rearrange(heads, n=NH), axis=AX, op=ALU.add).then_inc(s_dve_c, 1)

            def c_norm(c_, k):
                n, g = c_.n, c_.g
                dve.wait_ge(s_pool_c, G.at(g, f"rs{k}"))
                dve.tensor_tensor(yn[:, 0:n, :].rearrange(heads, n=NH), y[:, 0:n, :].rearrange(heads, n=NH),
                                  st3[:, 0:n * NH].unsqueeze(2).broadcast_to([P, n * NH, HD]), ALU.mult).then_inc(s_dve_c, 1)

            def c_nzf(c_):
                dve.wait_ge(s_pool_c, G.at(c_.g, "fx"))
                dve.tensor_scalar(nzf[:, 0:c_.n, :], fx[:, 0:c_.n, :], 0.0, None, ALU.not_equal).then_inc(s_dve_c, 1)

            def c_nzT(c_):
                dve.wait_ge(s_act_c, A.at(c_.g, "fxT"))
                dve.tensor_scalar(nzT[:, 0:c_.n * P], fxT[:, 0:c_.n * P], 0.0, None, ALU.not_equal).then_inc(s_dve_c, 1)

            def c_hidden(c_):
                cols = slice(0, c_.n * P)
                need(c_.g, "nzT")
                dve.wait_ge(s_act_c, A.at(c_.g, "h"))
                dve.tensor_tensor(hT[0:D, cols], hT[0:D, cols], nzT[:, cols], ALU.mult).then_inc(s_dve_c, 1)

            def c_second(c_):
                n, g = c_.n, c_.g
                dve.wait_ge(s_pe_c, T.at(g, "fc2"))
                dve.tensor_tensor(y[:, 0:n, :], banks[5][:, 0:n * D].rearrange("p (t d) -> p t d", d=D), nzf[:, 0:n, :], ALU.mult).then_inc(s_dve_c, 1)

            def c_second_in(c_):
                n, g = c_.n, c_.g
                need(g, "z")
                dve.tensor_tensor(y[:, 0:n, :], y[:, 0:n, :], fx[:, 0:n, :], ALU.add).then_inc(s_dve_c, 1)

            def c_head_gates(c_):
                n, g = c_.n, c_.g
                dve.wait_ge(s_pe_c, T.at(g, "hg"))
                dve.tensor_copy(hg[:, 0:n, :], banks[6][:, 0:n * NH].rearrange("p (t n) -> p t n", n=NH)).then_inc(s_dve_c, 1)

            def c_result(c_):
                n, g = c_.n, c_.g
                spread = lambda v: v.unsqueeze(2).broadcast_to([P, n, NH])
                need(g, "hg")
                softmax_sub(c_, hg[:, 0:n, :], hg[:, 0:n, :], st1[:, 0:n], spread, ("hmax",))
                softmax_div(c_, hg[:, 0:n, :], hg[:, 0:n, :], st1[:, 0:n], st2[:, 0:n], spread, ("hsum", "hinv"), "hexp")
                need(g, "hgs")
                dve.wait_ge(s_c_out, 16 * (g + 1))
                dve.tensor_tensor(res[:, 0:n, :].rearrange(heads, n=NH), fx[:, 0:n, :].rearrange(heads, n=NH),
                                  hg[:, 0:n, :].rearrange("p t n -> p (t n)").unsqueeze(2).broadcast_to([P, n * NH, HD]), ALU.mult).then_inc(s_dve_c, 1)
                need(g, "r1")
                dve.tensor_tensor(res[:, 0:n, :], res[:, 0:n, :], c_.rows(h1c), ALU.add).then_inc(s_dve_c, 1)

            def step_b(b, u, it, g):
                c_ = None if g is None else Group(g, g * GT, GT)
                row_max(b, 0)
                if c_ and u == 1:
                    c_mask(c_)
                if c_ and u == 2:
                    c_center(c_, 1, "y")
                if c_ and u == 3:
                    c_second_in(c_)
                    c_center(c_, 2, "y2")
                row_max(b, 1)
                if c_ and u > 1:
                    c_var(c_, u - 1)
                tail_max(b)
                row_max(b, 2)
                if c_ and u == 1:
                    c_gates1(c_)
                if c_ and u > 1:
                    c_norm(c_, u - 1)
                row_max(b, 3)
                if c_ and u == 1:
                    c_gates2(c_)
                if c_ and u == 2:
                    c_nzf(c_)
                    c_nzT(c_)
                    c_hidden(c_)
                    c_second(c_)
                if c_ and u == 3:
                    c_head_gates(c_)
                if b is not B - 1:
                    evac_proj(b + 1, (u + 1) % BUFS)
                norm(b - 1)
                if g is None and u == 3:
                    dve.wait_ge(s_pevD, NH)
                    residual(slice(0, B), B)
                    dve.wait_ge(s_resd, NH)
                if c_ and u == 1:
                    c_mix(c_)
                if c_ and u == 3:
                    c_result(c_)

            def residual(tiles, n_tiles):
                for n in range(NH):
                    dve.tensor_copy(resid[:, tiles, n * HD:(n + 1) * HD],
                                    sx_tok[:, n:n + 1, n * HD:(n + 1) * HD].broadcast_to([P, n_tiles, HD])).then_inc(s_resd, 1)

            evac_proj(0, 0)
            for n in range(NH):
                row_max(0, n)
            tail_max(0)
            evac_proj(1, 1)
            dve.memset(hT[D:D + 1, :], 1.0).then_inc(s_init, 1)
            dve.memset(res, 0.0).then_inc(s_c_out, 16)
            dve.wait_ge(s_h1_in, 32)
            steps_b(dve, step_b)
            norm(B - 1)
            tails = sxT[:].rearrange("p (b t) -> p b t", b=B)[:, :, MAIN:S]
            dve.tensor_copy(sx_rep[:, 0:NH], tails[:, 0:NH, :].unsqueeze(2).broadcast_to([P, NH, B, TAIL]))
            dve.tensor_copy(sx_rep[:, NH], tails).then_inc(s_sxr, 1)
            norm(B)
            dve.wait_ge(s_rs_mm, 1)
            dve.tensor_copy(sx_tok[:, B, :], banks[6][:, 0:D]).then_inc(s_resd, 1)
            dve.tensor_copy(resid[:, B, :], banks[6][:, D:2 * D]).then_inc(s_resd, 1)
            dve.wait_ge(s_resd, 2 + NH)
            dve.wait_ge(s_oc, TILES + 1)
            c_ = last_group
            c_mask(c_)
            c_gates1(c_)
            c_gates2(c_)
            c_mix(c_)
            c_center(c_, 1, "y")
            c_var(c_, 1)
            c_norm(c_, 1)
            c_nzf(c_)
            c_nzT(c_)
            c_hidden(c_)
            c_second(c_)
            c_second_in(c_)
            c_center(c_, 2, "y2")
            c_var(c_, 2)
            c_norm(c_, 2)
            c_head_gates(c_)
            c_result(c_)

        @block.tensor
        def _(pe):
            pe.wait_ge(s_cst, 16 * N_CST)
            pe.wait_ge(s_init, 2 + BUFS + 2)
            pe.matmul(banks[7][0:D, 0:D], w("aq"), w("ak"), start=True, stop=True).then_inc(s_gm, 1)
            pe.wait_ge(s_x_in, 16)
            pe.wait_ge(s_w_in, 16)
            for i in range(PW):
                mm = pe.matmul(banks[6][0:D, 0:P], tokw_sb[:, i, :], xs[:, :, i:i + STEP * (NTOK - 1) + 1:STEP],
                               start=(i == 0), stop=(i == PW - 1))
            mm.then_inc(s_tokp, 1)
            pe.wait_ge(s_tokg, 1)
            pe.transpose(banks[6][:, P:P + D], tokT[:], c("ident", D)[:, 0:D]).then_inc(s_tokp, 1)

            def turn_tokens(which, need, count, done):
                pe.wait_ge(need, count)
                for b in range(GB):
                    mm = pe.transpose(banks[0][:, b * HS:(b + 1) * HS],
                                      xn[:, which, 2 * b:2 * b + 2, :].rearrange("t h d -> t (h d)"),
                                      c("ident", HS)[:, 0:HS])
                mm.then_inc(done, 1)

            def entry_a(g, p, first):
                if not first:
                    turn_tokens(0, s_a_xn, g + 1, s_a_tp)
                else:
                    turn_tokens(0, s_a_xn, 1, s_a_tp)
                pe.wait_ge(s_a_tc, 2 * (g + 1))
                pe.wait_ge(s_gmc, 1)
                for h in range(2):
                    pe.matmul(banks[h][:, 0:2 * S], gmat[:], xnT[p][:, h * 2 * S:(h + 1) * 2 * S], start=True, stop=True)
                for j in range(GH):
                    mm = pe.matmul(banks[2][0:HS, j * D:(j + 1) * D], xnT[p][:, j * HS:(j + 1) * HS], w("wv"),
                                   start=True, stop=True)
                mm.then_inc(s_a_zv, 1)

            def exit_a(g):
                turn_tokens(1, s_b_xn, g + 1, s_b_tp)
                pe.wait_ge(s_b_tc, 2 * (g + 1))
                for h in range(2):
                    mm = pe.matmul(banks[h][:, 0:2 * S], w("hl"), xn2T[:, h * 2 * S:(h + 1) * 2 * S], start=True, stop=True)
                mm.then_inc(s_b_sx, 1)

            def scores(g, p, b, first):
                if b == 0:
                    pe.wait_ge(s_a_zc, 2 * (g + 1))
                    pe.wait_ge(s_a_vc, g + 1)
                if not (first and b < 2):
                    pe.wait_ge(s_a_e, 2 * (g * GB + b - 1))
                for h in range(2):
                    mm = pe.matmul(banks[4 + b % 2][0:HS, h * S:(h + 1) * S], zT[p][:, b * S + h * HS:b * S + (h + 1) * HS],
                                   xnT[p][:, b * S:(b + 1) * S], start=True, stop=True)
                mm.then_inc(s_a_s, 1)

            def turn(g, p, b, first):
                pe.wait_ge(s_a_e, 2 * (g * GB + b + 1))
                if not (first and b < 2):
                    pe.wait_ge(s_a_ptc, g * GB + b - 1)
                for h in range(2):
                    for u in range(2):
                        mm = pe.transpose(banks[6 + b % 2][0:HS, u * S + h * HS:u * S + (h + 1) * HS],
                                          probs[b % 2][:, h, u * HS:(u + 1) * HS], c("ident", HS)[:, 0:HS])
                mm.then_inc(s_a_pt, 1)

            def weigh(g, p, b, first):
                pe.wait_ge(s_a_ptc, g * GB + b + 1)
                if b == 0 and not first:
                    pe.wait_ge(s_a_h1, g)
                for h in range(2):
                    for u in range(2):
                        mm = pe.matmul(banks[3][0:HS, (2 * b + h) * D:(2 * b + h + 1) * D],
                                       probsT[b % 2][:, u, h * HS:(h + 1) * HS], vs[p][:, 2 * b + u, :],
                                       start=(u == 0), stop=(u == 1))
                mm.then_inc(s_a_av, 1)

            def step(g, p, first=False, last=False, it=None, u=0):
                scores(g, p, 0, first)
                scores(g, p, 1, first)
                turn(g, p, 0, first)
                scores(g, p, 2, first)
                turn(g, p, 1, first)
                weigh(g, p, 0, first)
                if not first:
                    exit_a(g - 1)
                scores(g, p, 3, first)
                turn(g, p, 2, first)
                weigh(g, p, 1, first)
                turn(g, p, 3, first)
                weigh(g, p, 2, first)
                weigh(g, p, 3, first)
                if not last:
                    if not first:
                        pe.wait_ge(s_b_sxc, 2 * g)
                    entry_a(g + 1, 1 - p, False)
            entry_a(0, 0, True)
            steps_a(pe, step)
            pe.wait_ge(s_b_sxc, 2 * (GROUPS - 1))
            exit_a(GROUPS - 1)

            def project(b, p, count):
                pe.wait_ge(sx_in[p], 16 * count)
                for e in range(NE):
                    dst = banks[5][:, e * S:(e + 1) * S] if e < 3 else banks[6][:, 0:S]
                    pe.matmul(dst, c("wq")[:, e * P:(e + 1) * P], sxb[p][:], start=True, stop=True)
                pe.matmul(banks[6][:, S:2 * S], c("wk"), sxb[p][:], start=True, stop=True)
                pe.matmul(banks[6][:, 2 * S:2 * S + 2 * D], sxb[p][:, 0:MAIN], c("wvs"), start=True, stop=True)
                pe.matmul(banks[6][0:TAIL, 2 * S + 2 * D:2 * S + 3 * D], sxb[p][:, MAIN:S], c("wvs")[:, 0:D],
                          start=True, stop=True).then_inc(s_proj, 1)

            def pass1(b, p, n):
                if n == 0:
                    pe.wait_ge(s_pevA, b + 1)
                    pe.wait_ge(s_pevD, b + 1)
                pe.wait_ge(s_p1_free, b * NH + n + 1)
                bank = banks[n % 2]
                pe.matmul(bank[:, :], ident_bf, mask_rows, start=True, stop=False)
                for e in range(NE):
                    mm = pe.matmul(bank[:, e * P:(e + 1) * P], qs[p][:, e, :], kz[p][:, n, 0:MAIN],
                                   start=False, stop=(e == NE - 1))
                mm.then_inc(s_p1, 1)

            def pass2(b, p, n, count):
                if n == 0:
                    pe.wait_ge(m_in[p], 16 * NH * count)
                pe.wait_ge(s_ex, b * NH + n + 1)
                bank = banks[2 + n % 2]
                pe.matmul(bank[:, :], ident_bf, mask_cols, start=True, stop=False)
                pe.matmul(bank[:, :], kz[p][:, n, 0:MAIN], qs[p][:, :, :], start=False, stop=True).then_inc(s_p2, 1)

            def weigh_b(b, p, n):
                pe.wait_ge(s_ex, b * NH + n + 3)
                if n == 0:
                    pe.wait_ge(s_oc, b + 1)
                pe.matmul(banks[4][HP * n:HP * (n + 1), :], va[p][:, n, :], pT[:, n, :], start=True, stop=True).then_inc(s_av, 1)

            def tail_scores(b, p):
                for n in range(NH):
                    mm = pe.matmul(banks[7][HP * n:HP * n + NE * TAIL, 0:S], qt[p][:], kz[p][:, n, :],
                                   start=True, stop=True)
                mm.then_inc(s_st, 1)

            def tail_turn(b):
                pe.wait_ge(s_ptd, b + 1)
                pe.transpose(banks[7][:, S:S + P], pt_row[:, 0:MAIN], ident)
                pe.transpose(banks[7][0:TAIL, S + P:S + 2 * P], pt_row[:, MAIN:S], ident).then_inc(s_tt, 1)

            def tail_weigh(b, p):
                pe.wait_ge(s_ttc, b + 1)
                for n in range(NH):
                    dst = banks[7][HP * n:HP * (n + 1), S + 2 * P:S + 2 * P + NE * TAIL]
                    cols = slice(HP * n, HP * n + NE * TAIL)
                    pe.matmul(dst, va[p][:, n, :], ptT[:, cols], start=True, stop=False)
                    mm = pe.matmul(dst, va_t[p][:, n, :], ptT4[:, cols], start=False, stop=True)
                mm.then_inc(s_ut, 1)

            def turn_max(b):
                pe.wait_ge(s_p1_free, (b + 1) * NH + 2)
                pe.transpose(banks[7][0:NH * NE, 0:P], mx[:], ident).then_inc(s_mT, 1)

            def turn_out(b, src):
                for e in range(NE):
                    mm = pe.transpose(banks[4][:, e * P:(e + 1) * P], src[:, e], ident)
                mm.then_inc(s_tT, 1)

            def c_om(c_):
                pe.wait_ge(s_dve_c, V.at(c_.g, "om"))
                for t in range(c_.n):
                    for h in range(2):
                        k = (t % 2) * 2 + h
                        mm = pe.transpose(c_.om_banks[t // 2][:, k * P:(k + 1) * P], om[:, t, h * P:(h + 1) * P], ident)
                mm.then_inc(s_pe_c, 1)

            def c_gates(c_):
                pe.wait_ge(s_act_c, A.at(c_.g, "omT"))
                for t in range(c_.n):
                    for h in range(2):
                        mm = pe.matmul(c_.lg_bank[:, t * NE * NH:(t + 1) * NE * NH], omT[:, t, h, :],
                                       c("gw")[:, h * NE * NH:(h + 1) * NE * NH], start=(h == 0), stop=(h == 1))
                mm.then_inc(s_pe_c, 1)

            def c_turn(c_):
                for t in range(c_.n):
                    mm = pe.transpose(c_.turn_banks[t // 4][0:D, (t % 4) * P:(t % 4 + 1) * P], fx[:, t, :], ident)
                mm.then_inc(s_pe_c, 1)

            def c_first(c_):
                pe.wait_ge(s_act_c, A.at(c_.g, "fxT"))
                for q in range((c_.n + 3) // 4):
                    cols = min(4, c_.n - 4 * q) * P
                    mm = pe.matmul(c_.h_banks[q][:, 0:cols], w("fc1"), fxT[:, q * 4 * P:q * 4 * P + cols], start=True, stop=True)
                mm.then_inc(s_pe_c, 1)

            def c_second(c_):
                pe.wait_ge(s_dve_c, V.at(c_.g, "hT"))
                for t in range(c_.n):
                    mm = pe.matmul(banks[5][:, t * D:(t + 1) * D], hT[:, t * P:(t + 1) * P], fc2_sb[:], start=True, stop=True)
                mm.then_inc(s_pe_c, 1)

            def c_head_gates(c_):
                pe.wait_ge(s_act_c, A.at(c_.g, "foT"))
                for t in range(c_.n):
                    mm = pe.matmul(banks[6][:, t * NH:(t + 1) * NH], fxT[:, t * P:(t + 1) * P], w("fg"), start=True, stop=True)
                mm.then_inc(s_pe_c, 1)

            def step_b(b, u, it, g):
                c_ = None if g is None else Group(g, g * GT, GT)
                p, q, r = u % BUFS, (u - 1) % BUFS, (u + 1) % BUFS
                count = it + 1
                pass1(b, p, 0)
                pe.wait_ge(s_mTc, b)
                pe.wait_ge(s_utc, b)
                tail_scores(b, p)
                if c_ and u == 1:
                    c_om(c_)
                pass1(b, p, 1)
                pass2(b - 1, q, 0, count)
                pass2(b - 1, q, 1, count)
                pass1(b, p, 2)
                weigh_b(b - 1, q, 0)
                pe.wait_ge(s_stD, b + 1)
                if c_ and u > 1:
                    pe.wait_ge(s_pool_c, G.at(g, ("fx", "fo")[u - 2]))
                tail_turn(b - 1)
                if c_ and u == 1:
                    c_gates(c_)
                if c_ and u > 1:
                    c_turn(c_)
                pass2(b - 1, q, 2, count)
                weigh_b(b - 1, q, 1)
                pass1(b, p, 3)
                if c_ and u == 2:
                    c_first(c_)
                tail_weigh(b - 1, q)
                pass2(b - 1, q, 3, count)
                weigh_b(b - 1, q, 2)
                pe.wait_ge(s_utc, b + 1)
                turn_max(b)
                if c_ and u == 2:
                    c_second(c_)
                if c_ and u == 3:
                    c_head_gates(c_)
                weigh_b(b - 1, q, 3)
                if c_:
                    pe.wait_ge(s_dve_c, V.at(g, ("lg", "z", "hg")[u - 1]))
                if b is not B - 1:
                    project(b + 1, r, it + 1 if u % BUFS == 1 else it + 2)
                pe.wait_ge(s_uc, b)
                turn_out(b - 1, u_sb)

            project(0, 0, 1)
            for n in range(NH):
                pass1(0, 0, n)
            tail_scores(0, 0)
            pe.wait_ge(s_stD, 1)
            turn_max(0)
            project(1, 1, 1)
            steps_b(pe, step_b)
            q = (B - 1) % BUFS
            count = (B - 1) // BUFS + 1
            pass2(B - 1, q, 0, count)
            pass2(B - 1, q, 1, count)
            weigh_b(B - 1, q, 0)
            pe.wait_ge(s_mTc, B)
            tail_turn(B - 1)
            pass2(B - 1, q, 2, count)
            weigh_b(B - 1, q, 1)
            tail_weigh(B - 1, q)
            pass2(B - 1, q, 3, count)
            weigh_b(B - 1, q, 2)
            weigh_b(B - 1, q, 3)
            pe.wait_ge(s_uc, B)
            turn_out(B - 1, u_sb)
            pe.wait_ge(s_oc, B + 1)
            pe.wait_ge(s_utc, B + 1)
            turn_out(B, u_tail)
            pe.wait_ge(s_sxr, 1)
            pe.matmul(banks[6][:, 0:D], sx_rep[:, NH], c("wvs")[:, D:2 * D], start=True, stop=True)
            for n in range(NH):
                mm = pe.matmul(banks[6][:, D:2 * D], sx_rep[:, n], c("sel")[:, n * D:(n + 1) * D],
                               start=(n == 0), stop=(n == NH - 1))
            mm.then_inc(s_rs_mm, 1)

            c_om(last_group)
            c_gates(last_group)
            pe.wait_ge(s_pool_c, G.at(CGROUPS, "fx"))
            c_turn(last_group)
            c_first(last_group)
            c_second(last_group)
            pe.wait_ge(s_pool_c, G.at(CGROUPS, "fo"))
            c_turn(last_group)
            c_head_gates(last_group)


def laid_out(i):
    f = np.float32
    h = {n: np.asarray(v) for n, v in i.items()}
    c128 = np.zeros((P, N128), f)
    c64 = np.zeros((D, N64), f)

    def at(name, table=C128, dst=c128):
        a, b = table[name]
        return dst[:, a:b]
    at("ident")[:] = np.eye(P, dtype=f)
    kz = at("kz").reshape(P, NH, S)
    tmask = at("tmask")
    hl = at("hl", C64, c64)
    wq = at("wq").reshape(P, NE, P)
    wk, wvs = at("wk"), at("wvs")
    sel = at("sel").reshape(P, NH, D)
    gw = at("gw").reshape(P, 2, NE, NH)
    fc1 = at("fc1", C64, c64)
    fc2 = np.zeros((D + 1, D), f)
    for n in range(NH):
        r, k = slice(HP * n, HP * n + HD), slice(HD * n, HD * (n + 1))
        kz[HP * n + HD, n, :] = -1.0
        at("hl_b")[r, 0] = h["L0_ffn_hl_b"][n]
        hl[:, r] = h["L0_ffn_hl_w"][n].T
        for e in range(NE):
            wq[r, e, r] = h["L0_ffn_wq"][n, e].T
            for t in range(TAIL):
                tmask[HP * n + e * TAIL + t, MAIN + t + 1:] = BIG
            for e2 in range(NE):
                row = (e % 2) * D + n * HD
                gw[row:row + HD, e // 2, e2, n] = h["L0_ffn_gate_w"][n, e2, e * HD:(e + 1) * HD]
        wk[r, r] = h["L0_ffn_wk"][n].T
        wvs[r, k] = h["L0_ffn_wv"][n].T
        wvs[r, D + HD * n:D + HD * (n + 1)] = np.eye(HD, dtype=f)
        sel[r, n, k] = np.eye(HD, dtype=f)
        fc1[k, k] = h["L0_ffn_fc1_w"].T
        fc2[k, k] = h["L0_ffn_fc2_w"].T
        fc2[D, k] = h["L0_ffn_fc2_b"]
        at("fc1_b", C64, c64)[k, 0] = h["L0_ffn_fc1_b"]
        for name, src in (("ln_g", "ln_g"), ("ln_b", "ln_b"), ("fn_g", "fnorm_g"), ("fn_b", "fnorm_b")):
            at(name)[:, k] = h["L0_ffn_" + src]
    at("gate_b")[:] = h["L0_ffn_gate_b"].T.reshape(1, NE * NH)
    at("tok_b", C64, c64)[:, 0] = h["L0_tok_bias"]
    at("wv", C64, c64)[:] = h["L0_attn_Wv"].T
    at("aq", C64, c64)[:] = h["L0_attn_Wq"]
    at("ak", C64, c64)[:] = h["L0_attn_Wk"]
    at("fg", C64, c64)[:] = h["L0_ffn_fgate_w"].T
    masks = np.zeros((P, P + 2 * NE * P), f)
    masks[:, 0:P] = np.eye(P)
    for k in range(P):
        for e in range(NE):
            masks[k, P + e * P + k + 1:P + (e + 1) * P] = BIG
            masks[k, P + NE * P + e * P:P + NE * P + e * P + k] = BIG
    return {"x": h["x"], "txt": h["txt"], "tokw": h["L0_tok_weight"].reshape(PH, PW, D), "c128": c128, "c64": c64,
            "fc2": fc2, "masks": masks}


def kernel(**inputs):
    import concourse.bacc as bacc
    from concourse.bass_utils import run_bass_kernel_spmd as run

    nc = bacc.Bacc("TRN2", target_bir_lowering=False, num_devices=1)
    arrays, args = {}, []
    for name, a in laid_out(inputs).items():
        arrays[f"in_{name}"] = np.ascontiguousarray(a)
        args.append(nc.dram_tensor(f"in_{name}", a.shape, mybir.dt.from_np(a.dtype), kind="ExternalInput").ap())
    args.append(nc.dram_tensor("out_0", (B, S, D), F32, kind="ExternalOutput").ap())
    fusion_kernel(nc, *args)
    r = run(nc, [arrays], core_ids=[0])
    return r.results[0]["out_0"]
```

```python
import numpy as np
from contextlib import ExitStack

import concourse.bass as bass
from concourse import mybir

F32 = mybir.dt.float32
BF16 = mybir.dt.bfloat16
ALU = mybir.AluOpType
ACT = mybir.ActivationFunctionType
AX = mybir.AxisListType.X

B = 32
NTOK = 4
NTXT = 128
S = NTOK + NTXT
HS = S // 2
D = 64
NH, NE, HD = 4, 4, 16
HP = 32
PH, PW, STEP = 64, 25, 12
P = 128
MAIN = 128
TAIL = S - MAIN
TILES = B + 1
ARENA = 14080
BUFS = 3
PARTS = 3
PAIRS = 6
Q_PART = (0, 1, 2, 0, 1, 0)
K_PART = (0, 1, 0, 2, 0, 1)
ROWS = PAIRS * HD
QCOLS = NE * MAIN
HALF = QCOLS // 2
PCOLS = HALF + S
SENDS = 2 * PAIRS
BIG = -3e38

C128 = {}
C64 = {}


def _columns(table, *parts):
    at = 0
    for name, n in parts:
        table[name] = (at, at + n)
        at += n
    return at


N128 = _columns(C128, ("ident", P), ("tmask", S), ("hl_b", 1), ("wq", NE // 2 * P), ("wk", P),
                ("wvs", 2 * D), ("sel", NH * D), ("gw", 2 * NH * NE), ("gate_b", NH * NE), ("ln_g", D),
                ("ln_b", D), ("fn_g", D), ("fn_b", D))
N64 = _columns(C64, ("wv", D), ("aq", D), ("ak", D), ("hl", P), ("fc1", P), ("fg", NH), ("fc1_b", 1), ("tok_b", 1))

GB = 4
GROUPS = B // GB
GH = 2 * GB
GT = 3
GT_END = 6
CGROUPS = (TILES - GT_END) // GT

V_ORDER = ("lg gmax gsub gsum ginv gs mix sum y s1 yc1 var1 yn1 nzf nzT hT z y2 s2 yc2 var2 yn2 "
           "hg hmax hsub hsum hinv hgs r1 res").split()
A_ORDER = "omT gexp sq1 fxT h sq2 foT hexp".split()
T_ORDER = "omT lg fxT h fc2 foT hg".split()
G_ORDER = "eps1 rs1 gain1 fx eps2 rs2 gain2 fo".split()


class Marks:

    def __init__(self, order):
        self.order = order

    def at(self, g, name):
        return g * len(self.order) + (self.order.index(name) + 1)


V, A, T, G = Marks(V_ORDER), Marks(A_ORDER), Marks(T_ORDER), Marks(G_ORDER)

DVE_A = 4
DVE_A_END = 3


class Chain:

    def __init__(self, eng, sem, base=0):
        self.eng, self.sem, self.base, self.n = eng, sem, base, 0

    def mark(self, ins):
        ins.then_inc(self.sem, 1)
        self.n += 1
        return self.n

    def need(self, n):
        self.eng.wait_ge(self.sem, self.base + n)


def fusion_kernel(nc, x, txt, tokw, c128, c64, fc2, masks, out, dbg=None):
    ctx = ExitStack()
    with ctx:
        def sb(name, shape, dt=F32):
            return ctx.enter_context(nc.sbuf_tensor(name, shape, dt))

        def sem(name):
            return ctx.enter_context(nc.semaphore(name))

        arena = sb("arena", [P, ARENA])

        class Carve:

            def __init__(self):
                self.at = 0

            def take(self, rows, *shape):
                n = int(np.prod(shape))
                a = arena[0:rows, self.at:self.at + n]
                self.at += n
                assert self.at <= ARENA
                names = "abc"[:len(shape)]
                if len(shape) == 1:
                    return a
                return a.rearrange("p (%s) -> p %s" % (" ".join(names), " ".join(names)), **dict(zip(names[1:], shape[1:])))

        k128 = sb("k128", [P, N128])
        k64 = sb("k64", [D, N64])
        fc2_sb = sb("fc2_sb", [D + 1, D])
        masks_sb = sb("masks_sb", [P, P + 2 * NE * P], BF16)

        def c(name, rows=P):
            a, b = C128[name]
            return k128[0:rows, a:b]

        def w(name):
            a, b = C64[name]
            return k64[:, a:b]

        ident = c("ident")
        ident_bf = masks_sb[:, 0:P]
        mask_rows = masks_sb[:, P:P + NE * P]
        mask_cols = masks_sb[:, P + NE * P:P + 2 * NE * P]
        gmat = sb("gmat", [D, P])
        half_neg = sb("half_neg", [P, GT_END * NH])
        eps_ln = sb("eps_ln", [HS, GH])
        eps_hd = sb("eps_hd", [P, GT_END * NH])

        early = Carve()
        xs = early.take(PH, B, D)
        tokw_sb = early.take(PH, PW, D)
        tokT = sb("tokT", [D, P])
        tok = sb("tok", [P, D])
        h0 = early.take(HS, B, 2, D)

        masks_f = early.take(P, P + 2 * NE * P)

        nsum = sb("nsum", [HS, 2, GH])
        xc = early.take(HS, 2, GH, D)
        sq = early.take(HS, 2, GH, D)
        var = sb("var", [HS, 2, GH])
        vare = sb("vare", [HS, 2, GH])
        rstd = sb("rstd", [HS, 2, GH])
        xn = early.take(HS, 2, GH, D)
        xnT = [early.take(D, GB * S) for i in range(2)]
        zT = [early.take(D, GB * S) for i in range(2)]
        vs = [sb(f"vs{i}", [HS, GH, D]) for i in range(2)]
        nmax = sb("nmax", [HS, GH])
        rsum = [sb(f"rsum{i}", [HS, GH]) for i in range(2)]
        rinv = sb("rinv", [HS, GH])
        probs = [sb(f"probs{i}", [HS, 2, S]) for i in range(2)]
        probsT = [sb(f"probsT{i}", [HS, 2, S]) for i in range(2)]
        attn = sb("attn", [HS, GH, D])
        h1 = [sb(f"h1_{i}", [HS, GH, D]) for i in range(2)]
        xn2T = sb("xn2T", [D, GB * S])[:]
        sxT = sb("sxT", [P, B * S])
        h1_dram = nc.dram_tensor("h1_dram", (B, S, D), F32, kind="Internal").ap()

        sxb = [sb(f"sxb{i}", [P, S]) for i in range(BUFS)]
        parts = sb("parts", [P, PARTS, PCOLS], BF16)
        rest = sb("rest", [P, PCOLS])
        tparts = sb("tparts", [P, PARTS, HALF], BF16)
        trest = sb("trest", [P, HALF])
        tstack = sb("tstack", [ROWS, NH, QCOLS], BF16)
        tq = sb("tq", [ROWS, NH * NE, TAIL], BF16)
        qstack = [sb(f"qstack{i}", [ROWS + PARTS, NH, QCOLS], BF16) for i in range(BUFS)]
        kstack = [sb(f"kstack{i}", [ROWS + PARTS, NH, S], BF16) for i in range(BUFS)]
        va = [sb(f"va{i}", [P, NH, HP]) for i in range(BUFS)]
        va_t = [sb(f"va_t{i}", [TAIL, NH, HP]) for i in range(BUFS)]
        mx = sb("mx", [P, NH * NE])
        mparts = sb("mparts", [NH * NE, PARTS, P], BF16)
        mrest = sb("mrest", [NH * NE, P])
        st_m = sb("st_m", [P, S])
        nmt = sb("nmt", [P, 1])
        pt_row = sb("pt_row", [P, S])
        ptT = sb("ptT", [P, P])
        ptT4 = sb("ptT4", [TAIL, P])
        pT = sb("pT", [P, NH, NE * P])
        u_sb = sb("u_sb", [P, NE, P])
        u_tail = sb("u_tail", [P, NE, B, TAIL])
        rden = sb("rden", [P, NE * NH])
        sx_rep = sb("sx_rep", [P, NH + 1, B, TAIL])
        o_all = sb("o_all", [P, TILES, NE * D])
        sx_tok = sb("sx_tok", [P, TILES, D])
        resid = sb("resid", [P, TILES, D])

        late = Carve()
        h1c = sb("h1c", [P, TILES, D])
        nz = late.take(P, GT_END, D)
        om = late.take(P, GT_END, NE * D)
        omT = late.take(P, GT_END, 2, P)
        lg = sb("lg", [P, GT_END, NE * NH])
        lgm = sb("lgm", [P, GT_END, NH])
        y = late.take(P, GT_END, D)
        ysq = late.take(P, GT_END, D)
        yn = late.take(P, GT_END, D)
        fx = late.take(P, GT_END, D)
        nzf = late.take(P, GT_END, D)
        st1 = sb("st1", [P, GT_END * NH])
        st2 = sb("st2", [P, GT_END * NH])
        st3 = sb("st3", [P, GT_END * NH])
        fxT = late.take(D, GT_END * P)
        nzT = late.take(D, GT_END * P)
        hT = late.take(D + 1, GT_END * P)
        hg = sb("hg", [P, GT_END, NH])
        res = late.take(P, GT_END, D)

        banks = [ctx.enter_context(nc.psum_tensor(f"bank{i}", [P, 512], F32)) for i in range(8)]

        s_cst = sem("s_cst")
        s_x_in = sem("s_x_in")
        s_w_in = sem("s_w_in")
        s_h0_in = sem("s_h0_in")
        s_init = sem("s_init")
        s_gm = sem("s_gm")
        s_gmc = sem("s_gmc")
        s_tokp = sem("s_tokp")
        s_tokg = sem("s_tokg")
        s_tok_out = sem("s_tok_out")
        s_a_nm = sem("s_a_nm")
        s_a_sq = sem("s_a_sq")
        s_a_var = sem("s_a_var")
        s_a_rs = sem("s_a_rs")
        s_a_xn = sem("s_a_xn")
        s_a_tp = sem("s_a_tp")
        s_a_tc = sem("s_a_tc")
        s_a_z = sem("s_a_z")
        s_a_v = sem("s_a_v")
        s_a_zc = sem("s_a_zc")
        s_a_vc = sem("s_a_vc")
        s_a_s = sem("s_a_s")
        s_a_mx = sem("s_a_mx")
        s_a_e = sem("s_a_e")
        s_a_pt = sem("s_a_pt")
        s_a_ptc = sem("s_a_ptc")
        s_a_av = sem("s_a_av")
        s_a_h1 = sem("s_a_h1")
        s_b_nm = sem("s_b_nm")
        s_b_sq = sem("s_b_sq")
        s_b_var = sem("s_b_var")
        s_b_rs = sem("s_b_rs")
        s_b_xn = sem("s_b_xn")
        s_b_tp = sem("s_b_tp")
        s_b_tc = sem("s_b_tc")
        s_b_sx = sem("s_b_sx")
        s_b_sxc = sem("s_b_sxc")
        s_dve_a_end = sem("s_dve_a_end")
        s_dve_a = sem("s_dve_a")
        s_pool_a = sem("s_pool_a")
        s_p1 = sem("s_p1")
        s_p1_free = sem("s_p1_free")
        s_p2 = sem("s_p2")
        s_ex = sem("s_ex")
        s_proj = sem("s_proj")
        s_val = sem("s_val")
        s_high = sem("s_high")
        s_rest = sem("s_rest")
        s_vals = sem("s_vals")
        s_mid = sem("s_mid")
        s_low = sem("s_low")
        s_tproj = sem("s_tproj")
        s_thigh = sem("s_thigh")
        s_trest = sem("s_trest")
        s_tmid = sem("s_tmid")
        s_tlow = sem("s_tlow")
        s_tstack_in = sem("s_tstack_in")
        s_tq = sem("s_tq")
        s_mT = sem("s_mT")
        s_mhigh = sem("s_mhigh")
        s_mrest = sem("s_mrest")
        s_mmid = sem("s_mmid")
        s_mlow = sem("s_mlow")
        s_st = sem("s_st")
        s_stD = sem("s_stD")
        s_nmtd = sem("s_nmtd")
        s_ptd = sem("s_ptd")
        s_tt = sem("s_tt")
        s_ttc = sem("s_ttc")
        s_ut = sem("s_ut")
        s_utc = sem("s_utc")
        s_av = sem("s_av")
        s_uc = sem("s_uc")
        s_tT = sem("s_tT")
        s_rd = sem("s_rd")
        s_oc = sem("s_oc")
        s_sxr = sem("s_sxr")
        s_rs_mm = sem("s_rs_mm")
        s_resd = sem("s_resd")
        s_h1_in = sem("s_h1_in")
        s_dve_c = sem("s_dve_c")
        s_act_c = sem("s_act_c")
        s_pe_c = sem("s_pe_c")
        s_pool_c = sem("s_pool_c")
        s_om = sem("s_om")
        s_c_out = sem("s_c_out")
        stack_in = [sem(f"s_stack_in{i}") for i in range(BUFS)]
        m_in = [sem(f"s_m_in{i}") for i in range(BUFS)]
        sx_in = [sem(f"s_sx_in{i}") for i in range(BUFS)]
        a_out = [sem(f"s_a_out{i}") for i in range(2)]

        block = ctx.enter_context(nc.Block())
        N_CST = 4
        NB_TXT = 4
        PB = B // NB_TXT

        def steps_a(eng, step, last_too=True):
            step(0, 0, first=True)
            with eng.Fori(0, (GROUPS - 2) // 2) as it:
                for u in range(2):
                    step(it * 2 + (u + 1), (u + 1) % 2, it=it, u=u)
            step(GROUPS - 1, (GROUPS - 1) % 2, last=True)

        def steps_b(eng, step):
            for u in range(BUFS):
                step(u + 1, u + 1, 0, None)
            turns = (B - 2) // BUFS
            with eng.Fori(1, turns - 1) as it:
                for u in range(BUFS):
                    step(it * BUFS + (u + 1), u + 1, it, it - 1)
            for u in range(BUFS):
                step((turns - 1) * BUFS + (u + 1), u + 1, turns - 1, turns - 2)
            step(B - 1, (B - 1) % BUFS + BUFS, turns, None)

        def ahead(b):
            return not isinstance(b, int) or b + 2 < B

        def turn_of(u, it):
            return it + (2 if u > 0 else 1)

        class Group:

            def __init__(self, g, first, n, ends=False):
                self.g, self.first, self.n = g, first, n
                self.om_banks = [banks[5], banks[6], banks[0]]
                self.lg_out = banks[3] if ends else banks[6]
                self.z_out = banks[5] if ends else banks[6]
                self.hg_out = banks[6]
                self.turn_banks = [banks[5], banks[1]] if ends else [banks[6]]
                self.h_banks = [banks[6], banks[2]]

            def rows(self, a):
                return a[:, bass.ds(self.first, self.n), :]

        last_group = Group(CGROUPS, CGROUPS * GT, GT_END, ends=True)

        def masked(eng, c_, count):
            n, g = c_.n, c_.g
            eng.wait_ge(s_om, 2 * g + 1)
            eng.wait_ge(s_oc, count)
            eng.tensor_tensor(om[:, 0:n, :].rearrange("p t (e d) -> p t e d", e=NE),
                               c_.rows(o_all).rearrange("p t (e d) -> p t e d", e=NE),
                               nz[:, 0:n, :].unsqueeze(2).broadcast_to([P, n, NE, D]), ALU.mult).then_inc(s_om, 1)

        def affine(eng, c_, k):
            g, n = c_.g, c_.n
            gain, shift = (("ln_g", "ln_b"), ("fn_g", "fn_b"))[k - 1]
            eng.wait_ge(s_dve_c, V.at(g, f"yn{k}"))
            eng.tensor_tensor(yn[:, 0:n, :], yn[:, 0:n, :], c(gain).unsqueeze(1).broadcast_to([P, n, D]), ALU.mult).then_inc(s_pool_c, 1)
            eng.wait_ge(s_pool_c, G.at(g, f"gain{k}"))
            eng.tensor_tensor(fx[:, 0:n, :], yn[:, 0:n, :], c(shift).unsqueeze(1).broadcast_to([P, n, D]), ALU.add).then_inc(s_pool_c, 1)

        @block.sync
        def _(sp):
            sp.dma_start(xs[:], x.rearrange("b c r w -> r (b c) w")).then_inc(s_x_in, 16)
            sp.dma_start(k64[:], c64).then_inc(s_cst, 16)
            sp.dma_start(k128[:], c128).then_inc(s_cst, 16)
            for q in range(NB_TXT):
                rows = slice(q * PB, (q + 1) * PB)
                sp.dma_start(h0[NTOK:HS, rows, 0, :], txt[rows, 0:HS - NTOK, :].rearrange("b t d -> t b d")).then_inc(s_h0_in, 16)
                sp.dma_start(h0[:, rows, 1, :], txt[rows, HS - NTOK:NTXT, :].rearrange("b t d -> t b d")).then_inc(s_h0_in, 16)
            sp.wait_ge(s_tokg, 2)
            for n in range(NTOK):
                sp.dma_start(h0[n:n + 1, :, 0, :], tok[n:P:NTOK, :]).then_inc(s_tok_out, 16)

            def load_sx(b, p):
                sp.dma_start(sxb[p][:], sxT[:, bass.ds(b * S, S)]).then_inc(sx_in[p], 16)

            def step(g, p, first=False, last=False, it=None, u=0):
                if last:
                    sp.wait_ge(s_b_sxc, 2)
                    for b in range(BUFS):
                        load_sx(b, b)
                sp.wait_ge(s_a_h1, g + 1)
                dst = h1_dram[bass.ds(g * GB, GB), :, :].rearrange("b (h t) d -> t b h d", t=HS)
                src = h1[p][:].rearrange("t (b h) d -> t b h d", h=2)
                sp.dma_start(dst, src).then_inc(a_out[p], 16)
            steps_a(sp, step)

            def send(pair, src, dst, done):
                sp.dma_start(dst[pair * HD:(pair + 1) * HD], src).then_inc(done, 16)

            def send_parts(b, p):
                for part, ready in enumerate((s_high, s_mid, s_low)):
                    sp.wait_ge(ready, b + 1)
                    for pair in range(PAIRS):
                        if Q_PART[pair] == part:
                            send(pair, parts[:, part, 0:HALF], qstack[p], stack_in[p])
                        if K_PART[pair] == part:
                            send(pair, parts[0:P:2, part, HALF:PCOLS], kstack[p], stack_in[p])

            def send_m(b, p):
                sp.wait_ge(s_mlow, b + 1)
                for k in range(PARTS):
                    sp.dma_start(qstack[p][ROWS + k:ROWS + k + 1, :, :],
                                 mparts[:, k, :]).then_inc(m_in[p], 16)
            send_parts(0, 0)
            send_parts(1, 1)
            sp.wait_ge(s_tlow, 1)
            for pair in range(PAIRS):
                send(pair, tparts[:, Q_PART[pair], :], tstack, s_tstack_in)
            send_m(0, 0)
            for q in range(2):
                sp.wait_ge(a_out[q], 16 * (GROUPS // 2 + 1))
            sp.dma_start(h1c[:, 0:B, :], h1_dram[:, 0:MAIN, :].rearrange("b t d -> t b d")).then_inc(s_h1_in, 16)
            sp.dma_start(h1c[:, B, :], h1_dram[:, MAIN:S, :]).then_inc(s_h1_in, 16)

            def step_b(b, u, it, g):
                if ahead(b):
                    sp.wait_ge(s_val, b)
                    load_sx(b + 2, (u + 2) % BUFS)
                if b is not B - 1:
                    send_parts(b + 1, (u + 1) % BUFS)
                send_m(b, u % BUFS)
                if g is not None and u == BUFS:
                    sp.wait_ge(s_dve_c, V.at(g, "res"))
                    sp.dma_start(out[bass.ds(g * GT, GT), 0:MAIN, :].rearrange("b t d -> t b d"), res[:, 0:GT, :]).then_inc(s_c_out, 16)
            steps_b(sp, step_b)
            n = GT_END - 1
            sp.wait_ge(s_dve_c, V.at(CGROUPS, "res"))
            sp.dma_start(out[B - n:B, 0:MAIN, :].rearrange("b t d -> t b d"), res[:, 0:n, :]).then_inc(s_c_out, 16)
            sp.dma_start(out[:, MAIN:S, :], res[:, n, :]).then_inc(s_c_out, 16)
            sp.wait_ge(s_c_out, 16 * (CGROUPS + 3))

        @block.gpsimd
        def _(pool):
            pool.dma_start(tokw_sb[:], tokw).then_inc(s_w_in, 16)
            pool.memset(eps_ln[:], 1e-5)
            pool.memset(eps_hd[:], 1e-8)
            pool.memset(half_neg[:], -0.5).then_inc(s_init, 1)
            pool.wait_ge(s_init, 1)

            def rs(which, n_sem, base):
                pool.tensor_tensor(vare[:, which, :], var[:, which, :], eps_ln[:], ALU.add).then_inc(s_pool_a, 1)
                pool.wait_ge(s_pool_a, base)
                pool.tensor_tensor(rstd[:, which, :], vare[:, which, :], half_neg[0:HS, 0:GH], ALU.pow).then_inc(n_sem, 1)

            def step(g, p, first=False, last=False, it=None, u=0):
                if not first:
                    pool.wait_ge(s_b_var, g)
                    rs(1, s_b_rs, 2 * g + 1)
                if not last:
                    pool.wait_ge(s_a_var, g + 2)
                    rs(0, s_a_rs, 2 * g + 2)
            pool.wait_ge(s_a_var, 1)
            rs(0, s_a_rs, 1)
            steps_a(pool, step)
            pool.wait_ge(s_b_var, GROUPS)
            rs(1, s_b_rs, 2 * GROUPS)


            def deviations(c_, k):
                g, n = c_.g, c_.n
                pool.wait_ge(s_dve_c, V.at(g, f"var{k}"))
                pool.tensor_tensor(st2[:, 0:n * NH], st2[:, 0:n * NH], eps_hd[:, 0:n * NH], ALU.add).then_inc(s_pool_c, 1)
                pool.wait_ge(s_pool_c, G.at(g, f"eps{k}"))
                pool.tensor_tensor(st3[:, 0:n * NH], st2[:, 0:n * NH], half_neg[:, 0:n * NH], ALU.pow).then_inc(s_pool_c, 1)

            def low(b):
                pool.wait_ge(s_mid, b + 1)
                pool.tensor_tensor(parts[:, 2, :], rest[:], parts[:, 1, :], ALU.subtract).then_inc(s_low, 1)

            def m_low(b):
                pool.wait_ge(s_mmid, b + 1)
                pool.tensor_tensor(mparts[:, 2, :], mrest[:], mparts[:, 1, :], ALU.subtract).then_inc(s_mlow, 1)

            def step_b(b, u, it, g):
                c_ = None if g is None else Group(g, g * GT, GT)
                if c_ and u > 1:
                    deviations(c_, u - 1)
                if b is not B - 1:
                    low(b + 1)
                if c_ and u > 1:
                    affine(pool, c_, u - 1)
                m_low(b)
                if u == 3 and b is not B - 2:
                    masked(pool, Group(it, it * GT, GT), b + 1)

            low(0)
            low(1)
            pool.wait_ge(s_tmid, 1)
            pool.tensor_tensor(tparts[:, 2, :], trest[:], tparts[:, 1, :], ALU.subtract).then_inc(s_tlow, 1)
            m_low(0)
            steps_b(pool, step_b)
            for k in (1, 2):
                deviations(last_group, k)

        @block.scalar
        def _(act):
            act.dma_start(fc2_sb[:], fc2).then_inc(s_cst, 16)
            act.dma_start(masks_f, masks).then_inc(s_cst, 16)
            act.wait_ge(s_cst, 16 * N_CST)
            act.wait_ge(s_tokp, 1)
            act.activation(tokT[:], banks[6][0:D, 0:P], ACT.Gelu, bias=w("tok_b")).then_inc(s_tokg, 1)
            act.wait_ge(s_tokp, 2)
            act.activation(tok[:], banks[6][:, P:P + D], ACT.Copy).then_inc(s_tokg, 1)

            def square(which, need, count, done):
                act.wait_ge(need, count)
                act.activation(sq[:, which], xc[:, which], ACT.Square, scale=float(D) ** -0.5).then_inc(done, 1)

            def evac2(dst, need, count, done):
                act.wait_ge(need, count)
                for h in range(2):
                    act.activation(dst[:, h * 2 * S:(h + 1) * 2 * S], banks[h][0:D, 0:2 * S], ACT.Copy).then_inc(done, 1)

            def evac_turned(dst, bank, need, count, done):
                act.wait_ge(need, count)
                for h in range(2):
                    act.activation(dst.rearrange("d (b h t) -> d b h t", h=2, t=HS)[:, :, h, :],
                                   bank[h * D:(h + 1) * D, 0:GB * HS].rearrange("d (b t) -> d b t", t=HS),
                                   ACT.Copy).then_inc(done, 1)

            def entry_a(g, p):
                evac_turned(xnT[p], banks[2], s_a_tp, g + 1, s_a_tc)
                evac2(zT[p], s_a_z, g + 1, s_a_zc)
                act.wait_ge(s_a_v, g + 1)
                act.activation(vs[p][:], banks[2][0:HS, 0:GH * D].rearrange("t (j d) -> t j d", d=D), ACT.Copy).then_inc(s_a_vc, 1)

            def exps(g, p, b, first):
                act.wait_ge(s_a_mx, g * GB + b + 1)
                if not (first and b < 2):
                    act.wait_ge(s_a_pt, g * GB + b - 1)
                for h in range(2):
                    act.activation(probs[b % 2][:, h, :], banks[4 + b % 2][0:HS, h * S:(h + 1) * S], ACT.Exp,
                                   bias=nmax[:, 2 * b + h:2 * b + h + 1],
                                   accum_out=rsum[p][:, 2 * b + h:2 * b + h + 1]).then_inc(s_a_e, 1)

            def exit_sx(g):
                act.wait_ge(s_b_sx, g + 1)
                for h in range(2):
                    act.activation(sxT[:, bass.ds(g * (GB * S) + h * 2 * S, 2 * S)], banks[h][:, 0:2 * S], ACT.Identity,
                                   bias=c("hl_b")).then_inc(s_b_sxc, 1)

            def step(g, p, first=False, last=False, it=None, u=0):
                exps(g, p, 0, first)
                exps(g, p, 1, first)
                if not first:
                    square(1, s_b_nm, g, s_b_sq)
                if not last:
                    square(0, s_a_nm, g + 2, s_a_sq)
                exps(g, p, 2, first)
                exps(g, p, 3, first)
                if not first:
                    evac_turned(xn2T, banks[0], s_b_tp, g, s_b_tc)
                    exit_sx(g - 1)
                if not last:
                    entry_a(g + 1, 1 - p)
            square(0, s_a_nm, 1, s_a_sq)
            entry_a(0, 0)
            steps_a(act, step)

            def high(b, before, count):
                act.wait_ge(s_proj, b + 1)
                if before is not None:
                    act.wait_ge(stack_in[before], 16 * SENDS * count)
                act.activation(parts[:, 0, :], banks[5][:, 0:PCOLS], ACT.Copy).then_inc(s_high, 1)

            def mid(b):
                act.wait_ge(s_rest, b + 1)
                act.activation(parts[:, 1, :], rest[:], ACT.Copy).then_inc(s_mid, 1)

            def exp_tail(b):
                act.wait_ge(s_nmtd, b + 1)
                act.activation(pt_row[:], st_m[:], ACT.Exp, bias=nmt[:]).then_inc(s_ptd, 1)

            def m_high(b, before, count):
                act.wait_ge(s_mT, b + 1)
                if before is not None:
                    act.wait_ge(m_in[before], 16 * PARTS * count)
                act.activation(mparts[:, 0, :], banks[1][0:NH * NE, 0:P], ACT.Copy).then_inc(s_mhigh, 1)

            def m_mid(b):
                act.wait_ge(s_mrest, b + 1)
                act.activation(mparts[:, 1, :], mrest[:], ACT.Copy).then_inc(s_mmid, 1)

            def exp_main(b, n):
                act.wait_ge(s_p2, b * NH + n + 1)
                act.activation(pT[:, n, :], banks[2 + n % 2][:, :], ACT.Exp).then_inc(s_ex, 1)

            def evac_tail_probs(b):
                act.wait_ge(s_tt, b + 1)
                act.activation(ptT[:], banks[7][:, S:S + P], ACT.Copy)
                act.activation(ptT4[:], banks[7][0:TAIL, S + P:S + 2 * P], ACT.Copy).then_inc(s_ttc, 1)

            def evac_tail_out(b):
                act.wait_ge(s_ut, b + 1)
                act.activation(u_tail[:, :, bass.ds(b, 1), :],
                               banks[7][:, S + 2 * P:S + 2 * P + NE * TAIL].rearrange("p (e o t) -> p e o t", e=NE, o=1),
                               ACT.Copy).then_inc(s_utc, 1)

            def evac_out(b):
                act.wait_ge(s_av, (b + 1) * NH)
                act.activation(u_sb[:], banks[4][:, :].rearrange("p (e t) -> p e t", e=NE), ACT.Copy).then_inc(s_uc, 1)

            def c_om(c_):
                act.wait_ge(s_pe_c, T.at(c_.g, "omT"))
                for q in range((c_.n + 1) // 2):
                    m = min(2, c_.n - 2 * q)
                    a = act.activation(omT[:, 2 * q:2 * q + m, :, :],
                                       c_.om_banks[q][:, 0:m * 2 * P].rearrange("p (t h s) -> p t h s", t=m, h=2), ACT.Copy)
                a.then_inc(s_act_c, 1)

            def c_exp(c_, buf, need):
                act.wait_ge(s_dve_c, V.at(c_.g, need))
                act.activation(buf[:, 0:c_.n, :], buf[:, 0:c_.n, :], ACT.Exp).then_inc(s_act_c, 1)

            def c_square(c_, need):
                act.wait_ge(s_dve_c, V.at(c_.g, need))
                act.activation(ysq[:, 0:c_.n, :], y[:, 0:c_.n, :], ACT.Square, scale=float(HD) ** -0.5).then_inc(s_act_c, 1)

            def c_evac(c_, dst, from_banks, name, relu=False):
                act.wait_ge(s_pe_c, T.at(c_.g, name))
                for q in range((c_.n + 3) // 4):
                    cols = min(4, c_.n - 4 * q) * P
                    src, to = from_banks[q][0:D, 0:cols], dst[0:D, q * 4 * P:q * 4 * P + cols]
                    if relu:
                        a = act.activation(to, src, ACT.Relu, bias=w("fc1_b"))
                    else:
                        a = act.activation(to, src, ACT.Copy)
                a.then_inc(s_act_c, 1)

            def step_b(b, u, it, g):
                c_ = None if g is None else Group(g, g * GT, GT)
                if b is not B - 1:
                    high(b + 1, u % BUFS, it + 2 if u == BUFS else it + 1)
                exp_main(b - 1, 0)
                evac_tail_probs(b - 1)
                exp_main(b - 1, 1)
                if c_ and u == 1:
                    c_om(c_)
                if b is not B - 1:
                    mid(b + 1)
                evac_tail_out(b - 1)
                exp_main(b - 1, 2)
                exp_main(b - 1, 3)
                m_high(b, (u - 1) % BUFS, it + 1)
                m_mid(b)
                if c_ and u == 1:
                    c_exp(c_, lg, "gsub")
                if c_ and u > 1:
                    c_evac(c_, fxT, c_.turn_banks, ("fxT", "foT")[u - 2])
                evac_out(b - 1)
                if c_ and u == 2:
                    c_evac(c_, hT, c_.h_banks, "h", relu=True)
                exp_tail(b)
                if c_ and u < 3:
                    c_square(c_, f"yc{u}")
                if c_ and u == 3:
                    c_exp(c_, hg, "hsub")

            high(0, None, None)
            square(1, s_b_nm, GROUPS, s_b_sq)
            mid(0)
            evac_turned(xn2T, banks[0], s_b_tp, GROUPS, s_b_tc)
            exit_sx(GROUPS - 1)
            high(1, 0, 1)
            mid(1)
            act.wait_ge(s_tproj, 1)
            act.activation(tparts[:, 0, :], banks[3][:, 0:HALF], ACT.Copy).then_inc(s_thigh, 1)
            act.wait_ge(s_trest, 1)
            act.activation(tparts[:, 1, :], trest[:], ACT.Copy).then_inc(s_tmid, 1)
            m_high(0, None, None)
            m_mid(0)
            exp_tail(0)
            steps_b(act, step_b)
            exp_main(B - 1, 0)
            evac_tail_probs(B - 1)
            exp_main(B - 1, 1)
            evac_tail_out(B - 1)
            exp_main(B - 1, 2)
            exp_main(B - 1, 3)
            evac_out(B - 1)

            c_om(last_group)
            c_exp(last_group, lg, "gsub")
            c_square(last_group, "yc1")
            c_evac(last_group, fxT, last_group.turn_banks, "fxT")
            c_evac(last_group, hT, last_group.h_banks, "h", relu=True)
            c_square(last_group, "yc2")
            c_evac(last_group, fxT, last_group.turn_banks, "foT")
            c_exp(last_group, hg, "hsub")

        @block.vector
        def _(dve):
            dve.memset(h1[0][:], 0.0).then_inc(a_out[0], 16)
            dve.memset(h1[1][:], 0.0).then_inc(a_out[1], 16)
            dve.memset(mx[:], 0.0).then_inc(s_p1_free, 2)
            dve.memset(st_m[:], 0.0).then_inc(s_ex, 2)
            dve.memset(ptT4[:], 0.0).then_inc(s_utc, 1)
            dve.memset(rden[:], 0.0).then_inc(s_oc, 1)
            for p in range(BUFS):
                dve.memset(va[p][:], 1.0)
                dve.memset(va_t[p][:], 1.0)
            dve.memset(banks[7][:], 0.0).then_inc(s_init, 1)
            dve.wait_ge(s_init, 2)
            dve.wait_ge(s_cst, 16 * N_CST)
            for p in range(BUFS):
                dve.memset(kstack[p][ROWS:ROWS + PARTS, :, :], -1.0).then_inc(s_init, 1)
            dve.tensor_copy(masks_sb[:], masks_f).then_inc(s_init, 1)
            dve.tensor_scalar(c("wq"), c("wq"), float(HD) ** 0.5, None, ALU.mult).then_inc(s_init, 1)
            dve.memset(gmat[:, D:P], 0.0)
            dve.wait_ge(s_gm, 1)
            dve.tensor_copy(gmat[:, 0:D], banks[7][0:D, 0:D]).then_inc(s_gmc, 1)

            def center(which, src, ch, done):
                a = ch.mark(dve.tensor_reduce(nsum[:, which, :], src, axis=AX, op=ALU.add, negate=True))
                ch.need(a)
                dve.scalar_tensor_tensor(xc[:, which], nsum[:, which, :].unsqueeze(2).broadcast_to([HS, GH, D]),
                                         1.0 / D, src, ALU.mult, ALU.add).then_inc(done, 1)

            def variance(which, need, count, done):
                dve.wait_ge(need, count)
                dve.tensor_reduce(var[:, which, :], sq[:, which], axis=AX, op=ALU.add).then_inc(done, 1)

            def scale(which, need, count, done):
                dve.wait_ge(need, count)
                dve.tensor_tensor(xn[:, which], xc[:, which], rstd[:, which, :].unsqueeze(2).broadcast_to([HS, GH, D]),
                                  ALU.mult).then_inc(done, 1)

            def h0_of(g):
                return h0[:, bass.ds(g * GB, GB), :, :].rearrange("t b h d -> t (b h) d")

            def maxima(g, b):
                dve.wait_ge(s_a_s, g * GB + b + 1)
                dve.tensor_reduce(nmax[:, 2 * b:2 * b + 2], banks[4 + b % 2][0:HS, 0:2 * S].rearrange("t (h u) -> t h u", h=2),
                                  axis=AX, op=ALU.max, negate=True).then_inc(s_a_mx, 1)

            def evac_pt(g, b, first):
                dve.wait_ge(s_a_pt, g * GB + b + 1)
                if not (first and b < 2):
                    dve.wait_ge(s_a_av, g * GB + b - 1)
                dve.tensor_copy(probsT[b % 2][:], banks[6 + b % 2][0:HS, 0:2 * S].rearrange("t (h u) -> t h u", h=2)).then_inc(s_a_ptc, 1)

            def step(g, p, first=False, last=False, it=None, u=0):
                if first:
                    ch = Chain(dve, s_dve_a_end, 1)
                elif last:
                    ch = Chain(dve, s_dve_a_end, 1 + DVE_A_END)
                else:
                    ch = Chain(dve, s_dve_a, (it * 2 + u) * DVE_A)
                maxima(g, 0)
                maxima(g, 1)
                if not first:
                    dve.wait_ge(s_a_h1, g)
                    center(1, h1[1 - p][:], ch, s_b_nm)
                evac_pt(g, 0, first)
                maxima(g, 2)
                if not last:
                    center(0, h0_of(g + 1), ch, s_a_nm)
                if not first:
                    variance(1, s_b_sq, g, s_b_var)
                evac_pt(g, 1, first)
                maxima(g, 3)
                if not last:
                    variance(0, s_a_sq, g + 2, s_a_var)
                evac_pt(g, 2, first)
                if not first:
                    scale(1, s_b_rs, g, s_b_xn)
                if not last:
                    scale(0, s_a_rs, g + 2, s_a_xn)
                evac_pt(g, 3, first)
                dve.wait_ge(s_a_e, (g + 1) * GH)
                inverted = ch.mark(dve.reciprocal(rinv[:], rsum[p][:]))
                ch.need(inverted)
                dve.wait_ge(s_a_av, (g + 1) * GB)
                scaled = ch.mark(dve.scalar_tensor_tensor(
                    attn[:], banks[3][0:HS, 0:GH * D].rearrange("t (j d) -> t j d", d=D), float(D) ** -0.5,
                    rinv[:].unsqueeze(2).broadcast_to([HS, GH, D]), ALU.mult, ALU.mult))
                ch.need(scaled)
                if last:
                    dve.wait_ge(a_out[p], 16 * ((GROUPS - 1) // 2 + 1))
                elif not first:
                    dve.wait_ge(a_out[p], (it + (u + 1)) * 16)
                dve.tensor_tensor(h1[p][:], attn[:], h0_of(g), ALU.add).then_inc(s_a_h1, 1)
                assert ch.n == (DVE_A_END if first or last else DVE_A)

            dve.wait_ge(s_h0_in, 16 * 2 * NB_TXT)
            dve.wait_ge(s_tok_out, 16 * NTOK)
            center(0, h0_of(0), Chain(dve, s_dve_a_end), s_a_nm)
            variance(0, s_a_sq, 1, s_a_var)
            scale(0, s_a_rs, 1, s_a_xn)
            steps_a(dve, step)
            dve.wait_ge(s_a_h1, GROUPS)
            center(1, h1[(GROUPS - 1) % 2][:], Chain(dve, s_dve_a_end, 1 + 2 * DVE_A_END), s_b_nm)


            def take_rest(b):
                dve.wait_ge(s_high, b + 1)
                dve.tensor_tensor(rest[:], banks[5][:, 0:PCOLS], parts[:, 0, :], ALU.subtract).then_inc(s_rest, 1)

            def tail_queries(b):
                dve.tensor_copy(tq[:], tstack[:].rearrange("r n (e t) -> r (n e) t", e=NE)[:, :, bass.ds(b * TAIL, TAIL)]).then_inc(s_tq, 1)

            def take_values(b, p):
                dve.wait_ge(s_val, b + 1)
                dve.tensor_copy(va[p][:, :, 0:HD], banks[6][:, 0:D].rearrange("t (n d) -> t n d", n=NH))
                dve.tensor_copy(va_t[p][:, :, 0:HD], banks[6][0:TAIL, 2 * D:3 * D].rearrange("t (n d) -> t n d", n=NH))
                dve.tensor_copy(sx_tok[:, bass.ds(b, 1), :], banks[6][:, D:2 * D].unsqueeze(1)).then_inc(s_vals, 1)

            def m_rest(b):
                dve.wait_ge(s_mhigh, b + 1)
                dve.tensor_tensor(mrest[:], banks[1][0:NH * NE, 0:P], mparts[:, 0, :], ALU.subtract).then_inc(s_mrest, 1)

            def row_max(b, n):
                dve.wait_ge(s_p1, b * NH + n + 1)
                dve.tensor_reduce(mx[:, n * NE:(n + 1) * NE], banks[n % 2][:, :].rearrange("p (e t) -> p e t", e=NE),
                                  axis=AX, op=ALU.max).then_inc(s_p1_free, 1)

            def tail_max(b):
                dve.wait_ge(s_st, b + 1)
                dve.wait_ge(s_ptd, b)
                dve.tensor_tensor(st_m[:], banks[7][:, 0:S], c("tmask"), ALU.add).then_inc(s_stD, 1)
                dve.wait_ge(s_stD, b + 1)
                dve.tensor_reduce(nmt[:], st_m[:], axis=AX, op=ALU.max, negate=True).then_inc(s_nmtd, 1)

            def norm(b):
                t = banks[4][:, :].rearrange("p (a h) -> p a h", h=HP)
                dve.wait_ge(s_tT, b + 1)
                dve.reciprocal(rden[:].unsqueeze(2), t[:, :, HD:HD + 1]).then_inc(s_rd, 1)
                dve.wait_ge(s_rd, b + 1)
                dve.tensor_tensor(o_all[:, bass.ds(b, 1), :].rearrange("p o (a d) -> p (o a) d", d=HD), t[:, :, 0:HD],
                                  rden[:].unsqueeze(2).broadcast_to([P, NE * NH, HD]), ALU.mult).then_inc(s_oc, 1)

            heads = "p t (n d) -> p (t n) d"

            def need(g, name):
                dve.wait_ge(s_dve_c, V.at(g, name))

            def softmax_sub(c_, buf, view, tiny, spread, names):
                dve.tensor_reduce(tiny, view, axis=AX, op=ALU.max).then_inc(s_dve_c, 1)
                need(c_.g, names[0])
                dve.tensor_tensor(buf, buf, spread(tiny), ALU.subtract).then_inc(s_dve_c, 1)

            def softmax_div(c_, buf, view, tiny, inv, spread, names, exp_name):
                dve.wait_ge(s_act_c, A.at(c_.g, exp_name))
                dve.tensor_reduce(tiny, view, axis=AX, op=ALU.add).then_inc(s_dve_c, 1)
                need(c_.g, names[0])
                dve.reciprocal(inv, tiny).then_inc(s_dve_c, 1)
                need(c_.g, names[1])
                dve.tensor_tensor(buf, buf, spread(inv), ALU.mult).then_inc(s_dve_c, 1)

            def gates(c_):
                n = c_.n
                return (lg[:, 0:n, :].rearrange("p t (e n) -> p t e n", e=NE), lg[:, 0:n, :].rearrange("p t (e n) -> p t n e", e=NE),
                        lambda v: v.unsqueeze(2).broadcast_to([P, n, NE, NH]))

            def c_mask(c_):
                n, g = c_.n, c_.g
                dve.tensor_scalar(nz[:, 0:n, :], c_.rows(sx_tok), 0.0, None, ALU.not_equal).then_inc(s_om, 1)

            def c_gates1(c_):
                n, g = c_.n, c_.g
                buf, view, spread = gates(c_)
                dve.wait_ge(s_pe_c, T.at(g, "lg"))
                dve.tensor_tensor(lg[:, 0:n, :], c_.lg_out[:, 0:n * NE * NH].rearrange("p (t a) -> p t a", t=n),
                                  c("gate_b").unsqueeze(1).broadcast_to([P, n, NE * NH]), ALU.add).then_inc(s_dve_c, 1)
                need(g, "lg")
                softmax_sub(c_, buf, view, lgm[:, 0:n, :], spread, ("gmax",))

            def c_gates2(c_):
                n = c_.n
                buf, view, spread = gates(c_)
                softmax_div(c_, buf, view, lgm[:, 0:n, :], st1[:, 0:n * NH].rearrange("p (t n) -> p t n", n=NH), spread,
                            ("gsum", "ginv"), "gexp")

            def c_mix(c_):
                n, g = c_.n, c_.g
                o = om[:, 0:n, :].rearrange("p t (a d) -> p (t a) d", d=HD)
                need(g, "gs")
                dve.wait_ge(s_om, 2 * g + 2)
                dve.tensor_tensor(o, o, lg[:, 0:n, :].rearrange("p t a -> p (t a)").unsqueeze(2).broadcast_to([P, n * NE * NH, HD]),
                                  ALU.mult).then_inc(s_dve_c, 1)
                need(g, "mix")
                dve.tensor_reduce(y[:, 0:n, :], om[:, 0:n, :].rearrange("p t (e d) -> p t d e", e=NE), axis=AX, op=ALU.add).then_inc(s_dve_c, 1)
                need(g, "sum")
                dve.tensor_tensor(y[:, 0:n, :], y[:, 0:n, :], c_.rows(resid), ALU.add).then_inc(s_dve_c, 1)

            def c_center(c_, k, before):
                n, g = c_.n, c_.g
                yh = y[:, 0:n, :].rearrange(heads, n=NH)
                need(g, before)
                dve.tensor_reduce(st1[:, 0:n * NH], yh, axis=AX, op=ALU.add, negate=True).then_inc(s_dve_c, 1)
                need(g, f"s{k}")
                dve.scalar_tensor_tensor(yh, st1[:, 0:n * NH].unsqueeze(2).broadcast_to([P, n * NH, HD]), 1.0 / HD, yh,
                                         ALU.mult, ALU.add).then_inc(s_dve_c, 1)

            def c_var(c_, k):
                n, g = c_.n, c_.g
                dve.wait_ge(s_act_c, A.at(g, f"sq{k}"))
                dve.tensor_reduce(st2[:, 0:n * NH], ysq[:, 0:n, :].rearrange(heads, n=NH), axis=AX, op=ALU.add).then_inc(s_dve_c, 1)

            def c_norm(c_, k):
                n, g = c_.n, c_.g
                dve.wait_ge(s_pool_c, G.at(g, f"rs{k}"))
                dve.tensor_tensor(yn[:, 0:n, :].rearrange(heads, n=NH), y[:, 0:n, :].rearrange(heads, n=NH),
                                  st3[:, 0:n * NH].unsqueeze(2).broadcast_to([P, n * NH, HD]), ALU.mult).then_inc(s_dve_c, 1)

            def c_nzf(c_):
                dve.wait_ge(s_pool_c, G.at(c_.g, "fx"))
                dve.tensor_scalar(nzf[:, 0:c_.n, :], fx[:, 0:c_.n, :], 0.0, None, ALU.not_equal).then_inc(s_dve_c, 1)

            def c_nzT(c_):
                dve.wait_ge(s_act_c, A.at(c_.g, "fxT"))
                dve.tensor_scalar(nzT[:, 0:c_.n * P], fxT[:, 0:c_.n * P], 0.0, None, ALU.not_equal).then_inc(s_dve_c, 1)

            def c_hidden(c_):
                cols = slice(0, c_.n * P)
                need(c_.g, "nzT")
                dve.wait_ge(s_act_c, A.at(c_.g, "h"))
                dve.tensor_tensor(hT[0:D, cols], hT[0:D, cols], nzT[:, cols], ALU.mult).then_inc(s_dve_c, 1)

            def c_second(c_):
                n, g = c_.n, c_.g
                dve.wait_ge(s_pe_c, T.at(g, "fc2"))
                dve.tensor_tensor(y[:, 0:n, :], c_.z_out[:, 0:n * D].rearrange("p (t d) -> p t d", d=D), nzf[:, 0:n, :], ALU.mult).then_inc(s_dve_c, 1)

            def c_second_in(c_):
                n, g = c_.n, c_.g
                need(g, "z")
                dve.tensor_tensor(y[:, 0:n, :], y[:, 0:n, :], fx[:, 0:n, :], ALU.add).then_inc(s_dve_c, 1)

            def c_head_gates(c_):
                n, g = c_.n, c_.g
                dve.wait_ge(s_pe_c, T.at(g, "hg"))
                dve.tensor_copy(hg[:, 0:n, :], c_.hg_out[:, 0:n * NH].rearrange("p (t n) -> p t n", n=NH)).then_inc(s_dve_c, 1)

            def c_result1(c_):
                n, g = c_.n, c_.g
                spread = lambda v: v.unsqueeze(2).broadcast_to([P, n, NH])
                need(g, "hg")
                softmax_sub(c_, hg[:, 0:n, :], hg[:, 0:n, :], st1[:, 0:n], spread, ("hmax",))

            def c_result2(c_):
                n, g = c_.n, c_.g
                spread = lambda v: v.unsqueeze(2).broadcast_to([P, n, NH])
                softmax_div(c_, hg[:, 0:n, :], hg[:, 0:n, :], st1[:, 0:n], st2[:, 0:n], spread, ("hsum", "hinv"), "hexp")
                need(g, "hgs")
                dve.wait_ge(s_c_out, 16 * (g + 1))
                dve.tensor_tensor(res[:, 0:n, :].rearrange(heads, n=NH), fx[:, 0:n, :].rearrange(heads, n=NH),
                                  hg[:, 0:n, :].rearrange("p t n -> p (t n)").unsqueeze(2).broadcast_to([P, n * NH, HD]), ALU.mult).then_inc(s_dve_c, 1)
                need(g, "r1")
                dve.tensor_tensor(res[:, 0:n, :], res[:, 0:n, :], c_.rows(h1c), ALU.add).then_inc(s_dve_c, 1)

            def step_b(b, u, it, g):
                c_ = None if g is None else Group(g, g * GT, GT)
                row_max(b, 0)
                if b is not B - 1:
                    take_rest(b + 1)
                row_max(b, 1)
                if b is not B - 1:
                    take_values(b + 1, (u + 1) % BUFS)
                row_max(b, 2)
                if c_ and u > 1:
                    c_norm(c_, u - 1)
                row_max(b, 3)
                m_rest(b)
                if c_ and u == 1:
                    c_gates1(c_)
                tail_max(b)
                if b is not B - 1:
                    tail_queries(b + 1)
                if c_ and u == 1:
                    c_gates2(c_)
                    c_mix(c_)
                    c_center(c_, 1, "y")
                if c_ and u == 2:
                    c_nzf(c_)
                    c_nzT(c_)
                    c_hidden(c_)
                    c_second(c_)
                    c_second_in(c_)
                    c_center(c_, 2, "y2")
                if c_ and u == 3:
                    c_head_gates(c_)
                    c_result1(c_)
                norm(b - 1)
                if c_ and u < 3:
                    c_var(c_, u)
                if g is None and u == 3:
                    dve.wait_ge(s_vals, NH)
                    residual(slice(0, B), B)
                    dve.wait_ge(s_h1_in, 32)
                    dve.wait_ge(s_resd, NH)
                if u == 3 and b is not B - 2:
                    c_mask(Group(it, it * GT, GT))
                if c_ and u == 3:
                    c_result2(c_)

            def residual(tiles, n_tiles):
                for n in range(NH):
                    dve.tensor_copy(resid[:, tiles, n * HD:(n + 1) * HD],
                                    sx_tok[:, n:n + 1, n * HD:(n + 1) * HD].broadcast_to([P, n_tiles, HD])).then_inc(s_resd, 1)

            take_rest(0)
            variance(1, s_b_sq, GROUPS, s_b_var)
            take_values(0, 0)
            scale(1, s_b_rs, GROUPS, s_b_xn)
            take_rest(1)
            take_values(1, 1)
            dve.wait_ge(s_thigh, 1)
            dve.tensor_tensor(trest[:], banks[3][:, 0:HALF], tparts[:, 0, :], ALU.subtract).then_inc(s_trest, 1)
            for n in range(NH):
                row_max(0, n)
            m_rest(0)
            dve.wait_ge(s_tstack_in, 16 * PAIRS)
            tail_queries(0)
            tail_max(0)
            tail_queries(1)
            dve.memset(hT[D:D + 1, :], 1.0).then_inc(s_init, 1)
            dve.memset(res, 0.0).then_inc(s_c_out, 16)
            steps_b(dve, step_b)
            norm(B - 1)
            tails = sxT[:].rearrange("p (b t) -> p b t", b=B)[:, :, MAIN:S]
            dve.tensor_copy(sx_rep[:, 0:NH], tails[:, 0:NH, :].unsqueeze(2).broadcast_to([P, NH, B, TAIL]))
            dve.tensor_copy(sx_rep[:, NH], tails).then_inc(s_sxr, 1)
            norm(B)
            dve.wait_ge(s_rs_mm, 1)
            dve.tensor_copy(sx_tok[:, B, :], banks[6][:, 0:D]).then_inc(s_resd, 1)
            dve.tensor_copy(resid[:, B, :], banks[6][:, D:2 * D]).then_inc(s_resd, 1)
            dve.wait_ge(s_resd, 2 + NH)
            dve.wait_ge(s_oc, TILES + 1)
            c_ = last_group
            c_mask(c_)
            masked(dve, c_, TILES + 1)
            c_gates1(c_)
            c_gates2(c_)
            c_mix(c_)
            c_center(c_, 1, "y")
            c_var(c_, 1)
            c_norm(c_, 1)
            affine(dve, c_, 1)
            c_nzf(c_)
            c_nzT(c_)
            c_hidden(c_)
            c_second(c_)
            c_second_in(c_)
            c_center(c_, 2, "y2")
            c_var(c_, 2)
            c_norm(c_, 2)
            affine(dve, c_, 2)
            c_head_gates(c_)
            c_result1(c_)
            c_result2(c_)

        @block.tensor
        def _(pe):
            pe.wait_ge(s_cst, 16 * N_CST)
            pe.wait_ge(s_init, 2 + BUFS + 2)
            pe.matmul(banks[7][0:D, 0:D], w("aq"), w("ak"), start=True, stop=True).then_inc(s_gm, 1)
            pe.wait_ge(s_x_in, 16)
            pe.wait_ge(s_w_in, 16)
            for i in range(PW):
                mm = pe.matmul(banks[6][0:D, 0:P], tokw_sb[:, i, :], xs[:, :, i:i + STEP * (NTOK - 1) + 1:STEP],
                               start=(i == 0), stop=(i == PW - 1))
            mm.then_inc(s_tokp, 1)
            pe.wait_ge(s_tokg, 1)
            pe.transpose(banks[6][:, P:P + D], tokT[:], c("ident", D)[:, 0:D]).then_inc(s_tokp, 1)

            def turn_tokens(which, bank, need, count, done):
                pe.wait_ge(need, count)
                for b in range(GB):
                    mm = pe.transpose(bank[:, b * HS:(b + 1) * HS],
                                      xn[:, which, 2 * b:2 * b + 2, :].rearrange("t h d -> t (h d)"),
                                      c("ident", HS)[:, 0:HS])
                mm.then_inc(done, 1)

            def entry_a(g, p):
                pe.wait_ge(s_a_tc, 2 * (g + 1))
                for h in range(2):
                    mm = pe.matmul(banks[h][:, 0:2 * S], gmat[:], xnT[p][:, h * 2 * S:(h + 1) * 2 * S], start=True, stop=True)
                mm.then_inc(s_a_z, 1)
                for j in range(GH):
                    mm = pe.matmul(banks[2][0:HS, j * D:(j + 1) * D], xnT[p][:, j * HS:(j + 1) * HS], w("wv"),
                                   start=True, stop=True)
                mm.then_inc(s_a_v, 1)

            def exit_a(g):
                pe.wait_ge(s_b_tc, 2 * (g + 1))
                for h in range(2):
                    mm = pe.matmul(banks[h][:, 0:2 * S], w("hl"), xn2T[:, h * 2 * S:(h + 1) * 2 * S], start=True, stop=True)
                mm.then_inc(s_b_sx, 1)

            def scores(g, p, b, first):
                if b == 0:
                    pe.wait_ge(s_a_zc, 2 * (g + 1))
                if not (first and b < 2):
                    pe.wait_ge(s_a_e, 2 * (g * GB + b - 1))
                for h in range(2):
                    mm = pe.matmul(banks[4 + b % 2][0:HS, h * S:(h + 1) * S], zT[p][:, b * S + h * HS:b * S + (h + 1) * HS],
                                   xnT[p][:, b * S:(b + 1) * S], start=True, stop=True)
                mm.then_inc(s_a_s, 1)

            def turn(g, p, b, first):
                pe.wait_ge(s_a_e, 2 * (g * GB + b + 1))
                if not (first and b < 2):
                    pe.wait_ge(s_a_ptc, g * GB + b - 1)
                for h in range(2):
                    for u in range(2):
                        mm = pe.transpose(banks[6 + b % 2][0:HS, u * S + h * HS:u * S + (h + 1) * HS],
                                          probs[b % 2][:, h, u * HS:(u + 1) * HS], c("ident", HS)[:, 0:HS])
                mm.then_inc(s_a_pt, 1)

            def weigh(g, p, b, first):
                pe.wait_ge(s_a_ptc, g * GB + b + 1)
                if b == 0:
                    pe.wait_ge(s_a_vc, g + 1)
                    if not first:
                        pe.wait_ge(s_a_h1, g)
                for h in range(2):
                    for u in range(2):
                        mm = pe.matmul(banks[3][0:HS, (2 * b + h) * D:(2 * b + h + 1) * D],
                                       probsT[b % 2][:, u, h * HS:(h + 1) * HS], vs[p][:, 2 * b + u, :],
                                       start=(u == 0), stop=(u == 1))
                mm.then_inc(s_a_av, 1)

            def step(g, p, first=False, last=False, it=None, u=0):
                scores(g, p, 0, first)
                scores(g, p, 1, first)
                turn(g, p, 0, first)
                scores(g, p, 2, first)
                turn(g, p, 1, first)
                weigh(g, p, 0, first)
                scores(g, p, 3, first)
                turn(g, p, 2, first)
                weigh(g, p, 1, first)
                turn(g, p, 3, first)
                if not first:
                    turn_tokens(1, banks[0], s_b_xn, g, s_b_tp)
                weigh(g, p, 2, first)
                if not first:
                    exit_a(g - 1)
                if not last:
                    turn_tokens(0, banks[2], s_a_xn, g + 2, s_a_tp)
                weigh(g, p, 3, first)
                if not last:
                    if not first:
                        pe.wait_ge(s_b_sxc, 2 * g)
                    entry_a(g + 1, 1 - p)
            turn_tokens(0, banks[2], s_a_xn, 1, s_a_tp)
            pe.wait_ge(s_gmc, 1)
            entry_a(0, 0)
            steps_a(pe, step)
            def project(b, p, count):
                pe.wait_ge(sx_in[p], 16 * count)
                for j in range(NE // 2):
                    pe.matmul(banks[5][:, j * MAIN:(j + 1) * MAIN], c("wq")[:, j * P:(j + 1) * P], sxb[p][:, 0:MAIN], start=True, stop=True)
                pe.matmul(banks[5][:, HALF:PCOLS], c("wk"), sxb[p][:], start=True, stop=True).then_inc(s_proj, 1)

            def project_values(b, p):
                pe.matmul(banks[6][:, 0:2 * D], sxb[p][:, 0:MAIN], c("wvs"), start=True, stop=True)
                pe.matmul(banks[6][0:TAIL, 2 * D:3 * D], sxb[p][:, MAIN:S], c("wvs")[:, 0:D],
                          start=True, stop=True).then_inc(s_val, 1)

            def project_tails():
                pe.wait_ge(s_b_sxc, 2 * GROUPS)
                for j in range(NE // 2):
                    mm = pe.matmul(banks[3][:, j * P:(j + 1) * P], c("wq")[:, j * P:(j + 1) * P],
                                   sxT[:].rearrange("p (b t) -> p b t", b=B)[:, :, MAIN:S], start=True, stop=True)
                mm.then_inc(s_tproj, 1)

            def pass1(b, p, n, count):
                if n == 0:
                    pe.wait_ge(stack_in[p], 16 * SENDS * count)
                if n == 1 and not (isinstance(b, int) and b == 0):
                    pe.wait_ge(s_mrest, b)
                pe.wait_ge(s_p1_free, b * NH + n + 1)
                bank = banks[n % 2]
                pe.matmul(bank[:, :], ident_bf, mask_rows, start=True, stop=False)
                for e in range(NE):
                    mm = pe.matmul(bank[:, e * P:(e + 1) * P], qstack[p][0:ROWS, n, e * MAIN:(e + 1) * MAIN],
                                   kstack[p][0:ROWS, n, 0:MAIN], start=False, stop=(e == NE - 1))
                mm.then_inc(s_p1, 1)

            def pass2(b, p, n, count):
                if n == 0:
                    pe.wait_ge(m_in[p], 16 * PARTS * count)
                pe.wait_ge(s_ex, b * NH + n + 1)
                bank = banks[2 + n % 2]
                pe.matmul(bank[:, :], ident_bf, mask_cols, start=True, stop=False)
                pe.matmul(bank[:, :], kstack[p][:, n, 0:MAIN], qstack[p][:, n, :], start=False, stop=True).then_inc(s_p2, 1)

            def weigh_b(b, p, n):
                pe.wait_ge(s_ex, b * NH + n + 3)
                if n == 0:
                    pe.wait_ge(s_oc, b + 1)
                pe.matmul(banks[4][HP * n:HP * (n + 1), :], va[p][:, n, :], pT[:, n, :], start=True, stop=True).then_inc(s_av, 1)

            def tail_scores(b, p):
                pe.wait_ge(s_tq, b + 1)
                for n in range(NH):
                    mm = pe.matmul(banks[7][HP * n:HP * n + NE * TAIL, 0:S], tq[:, n * NE:(n + 1) * NE, :].rearrange("r e t -> r (e t)"),
                                   kstack[p][0:ROWS, n, :], start=True, stop=True)
                mm.then_inc(s_st, 1)

            def tail_turn(b):
                pe.wait_ge(s_ptd, b + 1)
                pe.transpose(banks[7][:, S:S + P], pt_row[:, 0:MAIN], ident)
                pe.transpose(banks[7][0:TAIL, S + P:S + 2 * P], pt_row[:, MAIN:S], ident).then_inc(s_tt, 1)

            def tail_weigh(b, p):
                pe.wait_ge(s_ttc, b + 1)
                for n in range(NH):
                    dst = banks[7][HP * n:HP * (n + 1), S + 2 * P:S + 2 * P + NE * TAIL]
                    cols = slice(HP * n, HP * n + NE * TAIL)
                    pe.matmul(dst, va[p][:, n, :], ptT[:, cols], start=True, stop=False)
                    mm = pe.matmul(dst, va_t[p][:, n, :], ptT4[:, cols], start=False, stop=True)
                mm.then_inc(s_ut, 1)

            def turn_max(b):
                pe.wait_ge(s_p1_free, (b + 1) * NH + 2)
                pe.transpose(banks[1][0:NH * NE, 0:P], mx[:], ident).then_inc(s_mT, 1)

            def turn_out(b, src):
                for e in range(NE):
                    mm = pe.transpose(banks[4][:, e * P:(e + 1) * P], src[:, e], ident)
                mm.then_inc(s_tT, 1)

            def c_om(c_):
                pe.wait_ge(s_om, 2 * c_.g + 2)
                for t in range(c_.n):
                    for h in range(2):
                        k = (t % 2) * 2 + h
                        mm = pe.transpose(c_.om_banks[t // 2][:, k * P:(k + 1) * P], om[:, t, h * P:(h + 1) * P], ident)
                mm.then_inc(s_pe_c, 1)

            def c_gates(c_):
                pe.wait_ge(s_act_c, A.at(c_.g, "omT"))
                for t in range(c_.n):
                    for h in range(2):
                        mm = pe.matmul(c_.lg_out[:, t * NE * NH:(t + 1) * NE * NH], omT[:, t, h, :],
                                       c("gw")[:, h * NE * NH:(h + 1) * NE * NH], start=(h == 0), stop=(h == 1))
                mm.then_inc(s_pe_c, 1)

            def c_turn(c_):
                for t in range(c_.n):
                    mm = pe.transpose(c_.turn_banks[t // 4][0:D, (t % 4) * P:(t % 4 + 1) * P], fx[:, t, :], ident)
                mm.then_inc(s_pe_c, 1)

            def c_first(c_):
                pe.wait_ge(s_act_c, A.at(c_.g, "fxT"))
                for q in range((c_.n + 3) // 4):
                    cols = min(4, c_.n - 4 * q) * P
                    mm = pe.matmul(c_.h_banks[q][:, 0:cols], w("fc1"), fxT[:, q * 4 * P:q * 4 * P + cols], start=True, stop=True)
                mm.then_inc(s_pe_c, 1)

            def c_second(c_):
                pe.wait_ge(s_dve_c, V.at(c_.g, "hT"))
                for t in range(c_.n):
                    mm = pe.matmul(c_.z_out[:, t * D:(t + 1) * D], hT[:, t * P:(t + 1) * P], fc2_sb[:], start=True, stop=True)
                mm.then_inc(s_pe_c, 1)

            def c_head_gates(c_):
                pe.wait_ge(s_act_c, A.at(c_.g, "foT"))
                for t in range(c_.n):
                    mm = pe.matmul(c_.hg_out[:, t * NH:(t + 1) * NH], fxT[:, t * P:(t + 1) * P], w("fg"), start=True, stop=True)
                mm.then_inc(s_pe_c, 1)

            def step_b(b, u, it, g):
                c_ = None if g is None else Group(g, g * GT, GT)
                p, q = u % BUFS, (u - 1) % BUFS
                count = it + 1
                count_b = it + 2 if u == BUFS else it + 1
                pass1(b, p, 0, count_b)
                tail_turn(b - 1)
                pass1(b, p, 1, count_b)
                pass2(b - 1, q, 0, count)
                pass2(b - 1, q, 1, count)
                pass1(b, p, 2, count_b)
                if c_ and u == 1:
                    pe.wait_ge(s_vals, b + 2)
                    c_om(c_)
                tail_weigh(b - 1, q)
                weigh_b(b - 1, q, 0)
                pass1(b, p, 3, count_b)
                pass2(b - 1, q, 2, count)
                if c_ and u == 1:
                    c_gates(c_)
                weigh_b(b - 1, q, 1)
                pass2(b - 1, q, 3, count)
                turn_max(b)
                pe.wait_ge(s_utc, b + 1)
                tail_scores(b, p)
                if c_ and u > 1:
                    pe.wait_ge(s_vals, b + 2)
                    pe.wait_ge(s_pool_c, G.at(g, ("fx", "fo")[u - 2]))
                weigh_b(b - 1, q, 2)
                if c_ and u > 1:
                    c_turn(c_)
                weigh_b(b - 1, q, 3)
                if ahead(b):
                    pe.wait_ge(s_rest, b + 2)
                    project(b + 2, (u + 2) % BUFS, turn_of(u, it))
                if c_ and u == 2:
                    c_first(c_)
                if c_ and u == 3:
                    c_head_gates(c_)
                if c_ is None or u == 1:
                    next_values(b, u, c_)
                pe.wait_ge(s_uc, b)
                turn_out(b - 1, u_sb)
                if c_ and u == 2:
                    c_second(c_)
                if c_ and u > 1:
                    next_values(b, u, c_)

            def next_values(b, u, c_):
                if ahead(b):
                    pe.wait_ge(s_vals, b + 2)
                    if c_:
                        pe.wait_ge(s_dve_c, V.at(c_.g, ("lg", "z", "hg")[u - 1]))
                    project_values(b + 2, (u + 2) % BUFS)

            project(0, 0, 1)
            project_values(0, 0)
            pe.wait_ge(s_b_sxc, 2 * (GROUPS - 1))
            turn_tokens(1, banks[0], s_b_xn, GROUPS, s_b_tp)
            exit_a(GROUPS - 1)
            pe.wait_ge(s_vals, 1)
            project(1, 1, 1)
            project_values(1, 1)
            project_tails()
            for n in range(NH):
                pass1(0, 0, n, 1)
            turn_max(0)
            pe.wait_ge(s_vals, 2)
            project(2, 2, 1)
            project_values(2, 2)
            tail_scores(0, 0)
            steps_b(pe, step_b)
            q = (B - 1) % BUFS
            count = (B - 1) // BUFS + 1
            tail_turn(B - 1)
            pass2(B - 1, q, 0, count)
            pass2(B - 1, q, 1, count)
            tail_weigh(B - 1, q)
            weigh_b(B - 1, q, 0)
            pass2(B - 1, q, 2, count)
            weigh_b(B - 1, q, 1)
            pass2(B - 1, q, 3, count)
            weigh_b(B - 1, q, 2)
            weigh_b(B - 1, q, 3)
            pe.wait_ge(s_uc, B)
            turn_out(B - 1, u_sb)
            pe.wait_ge(s_oc, B + 1)
            pe.wait_ge(s_utc, B + 1)
            turn_out(B, u_tail)
            pe.wait_ge(s_sxr, 1)
            pe.matmul(banks[6][:, 0:D], sx_rep[:, NH], c("wvs")[:, D:2 * D], start=True, stop=True)
            for n in range(NH):
                mm = pe.matmul(banks[6][:, D:2 * D], sx_rep[:, n], c("sel")[:, n * D:(n + 1) * D],
                               start=(n == 0), stop=(n == NH - 1))
            mm.then_inc(s_rs_mm, 1)

            c_om(last_group)
            c_gates(last_group)
            pe.wait_ge(s_pool_c, G.at(CGROUPS, "fx"))
            c_turn(last_group)
            c_first(last_group)
            c_second(last_group)
            pe.wait_ge(s_pool_c, G.at(CGROUPS, "fo"))
            c_turn(last_group)
            c_head_gates(last_group)


def laid_out(i):
    f = np.float32
    h = {n: np.asarray(v) for n, v in i.items()}
    c128 = np.zeros((P, N128), f)
    c64 = np.zeros((D, N64), f)

    def at(name, table=C128, dst=c128):
        a, b = table[name]
        return dst[:, a:b]
    at("ident")[:] = np.eye(P, dtype=f)
    tmask = at("tmask")
    hl = at("hl", C64, c64)
    wq = at("wq").reshape(P, NE // 2, P)
    wk, wvs = at("wk"), at("wvs")
    sel = at("sel").reshape(P, NH, D)
    gw = at("gw").reshape(P, 2, NE, NH)
    fc1 = at("fc1", C64, c64)
    fc2 = np.zeros((D + 1, D), f)
    for n in range(NH):
        r, k = slice(HP * n, HP * n + HD), slice(HD * n, HD * (n + 1))
        at("hl_b")[r, 0] = h["L0_ffn_hl_b"][n]
        hl[:, r] = h["L0_ffn_hl_w"][n].T
        for e in range(NE):
            half, j = divmod(e, NE // 2)
            wq[r, j, 2 * n + half::2 * NH] = h["L0_ffn_wq"][n, e].T
            for t in range(TAIL):
                tmask[HP * n + e * TAIL + t, MAIN + t + 1:] = BIG
            for e2 in range(NE):
                row = (e % 2) * D + n * HD
                gw[row:row + HD, e // 2, e2, n] = h["L0_ffn_gate_w"][n, e2, e * HD:(e + 1) * HD]
        wk[r, 2 * n::2 * NH] = h["L0_ffn_wk"][n].T
        wvs[r, k] = h["L0_ffn_wv"][n].T
        wvs[r, D + HD * n:D + HD * (n + 1)] = np.eye(HD, dtype=f)
        sel[r, n, k] = np.eye(HD, dtype=f)
        fc1[k, k] = h["L0_ffn_fc1_w"].T
        fc2[k, k] = h["L0_ffn_fc2_w"].T
        fc2[D, k] = h["L0_ffn_fc2_b"]
        at("fc1_b", C64, c64)[k, 0] = h["L0_ffn_fc1_b"]
        for name, src in (("ln_g", "ln_g"), ("ln_b", "ln_b"), ("fn_g", "fnorm_g"), ("fn_b", "fnorm_b")):
            at(name)[:, k] = h["L0_ffn_" + src]
    at("gate_b")[:] = h["L0_ffn_gate_b"].T.reshape(1, NE * NH)
    at("tok_b", C64, c64)[:, 0] = h["L0_tok_bias"]
    at("wv", C64, c64)[:] = h["L0_attn_Wv"].T
    at("aq", C64, c64)[:] = h["L0_attn_Wq"]
    at("ak", C64, c64)[:] = h["L0_attn_Wk"]
    at("fg", C64, c64)[:] = h["L0_ffn_fgate_w"].T
    masks = np.zeros((P, P + 2 * NE * P), f)
    masks[:, 0:P] = np.eye(P)
    for k in range(P):
        for e in range(NE):
            masks[k, P + e * P + k + 1:P + (e + 1) * P] = BIG
            masks[k, P + NE * P + e * P:P + NE * P + e * P + k] = BIG
    return {"x": h["x"], "txt": h["txt"], "tokw": h["L0_tok_weight"].reshape(PH, PW, D), "c128": c128, "c64": c64,
            "fc2": fc2, "masks": masks}


def kernel(**inputs):
    import concourse.bacc as bacc
    from concourse.bass_utils import run_bass_kernel_spmd as run

    nc = bacc.Bacc("TRN2", target_bir_lowering=False, num_devices=1)
    arrays, args = {}, []
    for name, a in laid_out(inputs).items():
        arrays[f"in_{name}"] = np.ascontiguousarray(a)
        args.append(nc.dram_tensor(f"in_{name}", a.shape, mybir.dt.from_np(a.dtype), kind="ExternalInput").ap())
    args.append(nc.dram_tensor("out_0", (B, S, D), F32, kind="ExternalOutput").ap())
    fusion_kernel(nc, *args)
    r = run(nc, [arrays], core_ids=[0])
    return r.results[0]["out_0"]
```
